# Optimizing a Trainium2 kernel written in Bass

```python
import numpy as np
import jax
import jax.numpy as jnp

def _softmax(x, axis=-1):
    return jax.nn.softmax(x, axis=axis)

def _gelu(x):
    return jax.nn.gelu(x, approximate=True)

def _silu(x):
    return jax.nn.silu(x)

def _sigmoid(x):
    return jax.nn.sigmoid(x)

def _layernorm(x, axis=-1, eps=1e-05):
    m = jnp.mean(x, axis=axis, keepdims=True)
    v = jnp.var(x, axis=axis, keepdims=True)
    return (x - m) / jnp.sqrt(v + eps)

def _scatter_add(tgt, idx, src, axis=0):
    return tgt.at[idx].add(src)

def _segment_sum(src, seg, n):
    return jax.ops.segment_sum(src, seg, n)
kernel_name = 'mk_decoder_preln_d2_seqx_r8_bbaa3a'

def setup_inputs(seed: int=0):
    np.random.seed(seed)
    _w = jnp.asarray

    def _rec_inputs():
        import jax
        import jax.numpy as jnp
        _rk = jax.random.key(seed)
        x = -0.0002928 + 1 * jax.random.normal(jax.random.fold_in(_rk, 1), (16, 128, 256), jnp.float32)
        _lenS = 128 - jax.random.randint(jax.random.fold_in(_rk, 7), (16,), 0, max(1, 128 // 4) + 1, jnp.int32)
        _lenS2 = 128 - jax.random.randint(jax.random.fold_in(_rk, 8), (16,), 0, max(1, 128 // 4) + 1, jnp.int32)
        fside_S2_0 = -0.00337071 + 1.01897 * jax.random.normal(jax.random.fold_in(_rk, 11), (128,), jnp.float32)
        _ctx_2048P = jax.random.normal(jax.random.fold_in(_rk, 12), (16, 16, 256), jnp.float32)
        _ctx_2048c = jax.random.dirichlet(jax.random.fold_in(_rk, 512), 0.3 * jnp.ones((16,), jnp.float32), (16, 128))
        _ctx_2048t = jnp.einsum('bsk,bkd->bsd', _ctx_2048c, _ctx_2048P)
        _ctx_2048t = _ctx_2048t * jax.lax.rsqrt(jnp.mean(jnp.square(_ctx_2048t)) + 1e-12) * 0.953939
        ctx_2048 = 0.000675642 + 1.00031 * (_ctx_2048t + 0.3 * jax.random.normal(jax.random.fold_in(_rk, 612), (16, 128, 256), jnp.float32))
        return (x, fside_S2_0, ctx_2048)
    x, fside_S2_0, ctx_2048 = _rec_inputs()

    def _L0_attn_setup():
        import math
        import jax, jax.numpy as jnp
        import numpy as np
        N_HEADS = 16
        N_KV_HEADS = 4
        HEAD_DIM = 128
        D_MODEL = 256
        THETA = 10000.0
        SCALE_BASE = 64

        def _rope_cos_sin(seq_len, head_dim, theta):
            half = head_dim // 2
            inv_freq = 1.0 / theta ** (jnp.arange(half, dtype=jnp.float32) / half)
            pos = jnp.arange(seq_len, dtype=jnp.float32)
            freqs = jnp.outer(pos, inv_freq)
            freqs = jnp.concatenate([freqs, freqs], axis=-1)
            return (jnp.cos(freqs), jnp.sin(freqs))

        def _rotate_half(x):
            half = x.shape[-1] // 2
            return jnp.concatenate([-x[..., half:], x[..., :half]], axis=-1)

        def _xpos_scale(seq_len, head_dim, scale_base):
            pos = jnp.arange(seq_len, dtype=jnp.float32)
            scale = (pos + scale_base / 2.0) / scale_base
            half = head_dim // 2
            s = jnp.broadcast_to(scale[:, None], (seq_len, half))
            return jnp.stack([s, 1.0 / s], axis=-1).reshape(seq_len, head_dim)
        key = jax.random.key(seed)
        ks = jax.random.split(key, 5)
        std = 1.0 / math.sqrt(D_MODEL)
        x = jax.random.normal(ks[0], (2, 256, D_MODEL), dtype=jnp.float32)
        Wq = jax.random.normal(ks[1], (D_MODEL, N_HEADS * HEAD_DIM), dtype=jnp.float32) * std
        Wk = jax.random.normal(ks[2], (D_MODEL, N_KV_HEADS * HEAD_DIM), dtype=jnp.float32) * std
        Wv = jax.random.normal(ks[3], (D_MODEL, N_KV_HEADS * HEAD_DIM), dtype=jnp.float32) * std
        Wo = jax.random.normal(ks[4], (N_HEADS * HEAD_DIM, D_MODEL), dtype=jnp.float32) * std
        return {'x': x, 'Wq': Wq, 'Wk': Wk, 'Wv': Wv, 'Wo': Wo}
    _L0_attn_all = _L0_attn_setup()
    _L0_attn_in = {k: v for k, v in _L0_attn_all.items() if k in ('Wq', 'Wk', 'Wv', 'Wo')}
    del _L0_attn_all

    def _L0_xattn_setup():
        import jax, jax.numpy as jnp
        import numpy as np
        key = jax.random.key(seed)
        ks = jax.random.split(key, 5)
        B, D, L, NH = (2, 128, 256, 8)
        H = D // NH
        return {'v': jax.random.normal(ks[0], (B, D, L), jnp.float32), 'k': jax.random.normal(ks[1], (H, L), jnp.float32) * 0.1, 'bias': jax.random.normal(ks[2], (D,), jnp.float32), 'x1': jax.random.normal(ks[3], (B, D, L), jnp.float32), 'x2': jax.random.normal(ks[4], (B, D, L), jnp.float32), 'num_heads': NH}
    _L0_xattn_all = _L0_xattn_setup()
    _L0_xattn_in = {k: v for k, v in _L0_xattn_all.items() if k in ('k',)}
    del _L0_xattn_all

    def _L0_ffn_setup():
        import jax, jax.numpy as jnp
        import numpy as np
        E = 16
        D = 256
        H = 176
        HS = 2 * 176
        TOP_K = 6
        ROUTE_SCALE = 1.0
        key = jax.random.key(seed)
        ks = jax.random.split(key, 16)
        s = 0.02
        return {'x': jax.random.normal(ks[0], (4, 128, D), dtype=jnp.float32), 'gate_w': jax.random.normal(ks[1], (E, D), dtype=jnp.float32) * s, 'gate_b': jax.random.normal(ks[2], (E,), dtype=jnp.float32) * s, 'w1': jax.random.normal(ks[3], (E, H, D), dtype=jnp.float32) * s, 'b1': jax.random.normal(ks[4], (E, H), dtype=jnp.float32) * s, 'w2': jax.random.normal(ks[5], (E, D, H), dtype=jnp.float32) * s, 'b2': jax.random.normal(ks[6], (E, D), dtype=jnp.float32) * s, 'w3': jax.random.normal(ks[7], (E, H, D), dtype=jnp.float32) * s, 'b3': jax.random.normal(ks[8], (E, H), dtype=jnp.float32) * s, 'ws1': jax.random.normal(ks[9], (HS, D), dtype=jnp.float32) * s, 'bs1': jax.random.normal(ks[10], (HS,), dtype=jnp.float32) * s, 'ws2': jax.random.normal(ks[11], (D, HS), dtype=jnp.float32) * s, 'bs2': jax.random.normal(ks[12], (D,), dtype=jnp.float32) * s, 'ws3': jax.random.normal(ks[13], (HS, D), dtype=jnp.float32) * s, 'bs3': jax.random.normal(ks[14], (HS,), dtype=jnp.float32) * s}
    _L0_ffn_all = _L0_ffn_setup()
    _L0_ffn_in = {k: v for k, v in _L0_ffn_all.items() if k in ('gate_w', 'gate_b', 'w1', 'b1', 'w2', 'b2', 'w3', 'b3', 'ws1', 'bs1', 'ws2', 'bs2', 'ws3', 'bs3')}
    del _L0_ffn_all

    def _L1_attn_setup():
        import jax, jax.numpy as jnp
        import numpy as np
        NUM_HEADS = 16

        def _l2_normalize_complex(z):
            n = jnp.sqrt(jnp.sum(jnp.abs(z) ** 2, axis=-1, keepdims=True))
            return z / n
        key = jax.random.key(seed)
        k1, k2, k3, k4 = jax.random.split(key, 4)
        B, S, D = (4, 512, 256)
        scale = 1.0 / np.sqrt(D)
        return {'x': jax.random.normal(k1, (B, S, D), dtype=jnp.float32), 'W_q': jax.random.normal(k2, (D, D), dtype=jnp.float32) * scale, 'W_kv': jax.random.normal(k3, (D, D), dtype=jnp.float32) * scale, 'W_o': jax.random.normal(k4, (D, D), dtype=jnp.float32) * scale}
    _L1_attn_all = _L1_attn_setup()
    _L1_attn_in = {k: v for k, v in _L1_attn_all.items() if k in ('W_q', 'W_kv', 'W_o')}
    del _L1_attn_all

    def _L1_xattn_setup():
        import jax, jax.numpy as jnp
        import numpy as np
        key = jax.random.key(seed)
        k1, k2, k3, k4, k5 = jax.random.split(key, 5)
        B, D_MODEL, L = (2, 128, 256)
        HEAD_DIM = 8
        H = D_MODEL // HEAD_DIM
        return {'k': jax.random.normal(k1, (B, D_MODEL, L), dtype=jnp.float32), 'v': jax.random.normal(k2, (B, D_MODEL, L), dtype=jnp.float32), 'q': jax.random.normal(k3, (B, D_MODEL, L), dtype=jnp.float32), 'ssm_kernel': jax.random.normal(k4, (H, L), dtype=jnp.float32), 'D': jax.random.normal(k5, (H,), dtype=jnp.float32), 'head_dim': HEAD_DIM}
    _L1_xattn_all = _L1_xattn_setup()
    _L1_xattn_in = {k: v for k, v in _L1_xattn_all.items() if k in ('ssm_kernel', 'D')}
    del _L1_xattn_all

    def _L1_ffn_setup():
        import jax, jax.numpy as jnp
        import numpy as np
        NUM_EXPERTS = 8
        TOP_K = 2
        HIDDEN = 256
        INTER = 256
        SWIGLU_LIMIT = 7.0
        BATCH, SEQ = (4, 256)
        key = jax.random.key(seed)
        k0, k1, k2, k3, k4 = jax.random.split(key, 5)
        x = jax.random.normal(k0, (BATCH, SEQ, HIDDEN), jnp.float32)
        Wr = jax.random.normal(k1, (HIDDEN, NUM_EXPERTS), jnp.float32) * 0.02
        Wg = jax.random.normal(k2, (NUM_EXPERTS, HIDDEN, INTER), jnp.float32) * 0.02
        Wu = jax.random.normal(k3, (NUM_EXPERTS, HIDDEN, INTER), jnp.float32) * 0.02
        Wd = jax.random.normal(k4, (NUM_EXPERTS, INTER, HIDDEN), jnp.float32) * 0.02
        return {'hidden_states': x, 'Wr': Wr, 'Wg': Wg, 'Wu': Wu, 'Wd': Wd}
    _L1_ffn_all = _L1_ffn_setup()
    _L1_ffn_in = {k: v for k, v in _L1_ffn_all.items() if k in ('Wr', 'Wg', 'Wu', 'Wd')}
    del _L1_ffn_all
    return {'x': x, 'fside_S2_0': fside_S2_0, 'ctx_2048': ctx_2048, 'L0_attn_Wq': _L0_attn_in['Wq'], 'L0_attn_Wk': _L0_attn_in['Wk'], 'L0_attn_Wv': _L0_attn_in['Wv'], 'L0_attn_Wo': _L0_attn_in['Wo'], 'L0_xattn_k': _L0_xattn_in['k'], 'L0_ffn_gate_w': _L0_ffn_in['gate_w'], 'L0_ffn_gate_b': _L0_ffn_in['gate_b'], 'L0_ffn_w1': _L0_ffn_in['w1'], 'L0_ffn_b1': _L0_ffn_in['b1'], 'L0_ffn_w2': _L0_ffn_in['w2'], 'L0_ffn_b2': _L0_ffn_in['b2'], 'L0_ffn_w3': _L0_ffn_in['w3'], 'L0_ffn_b3': _L0_ffn_in['b3'], 'L0_ffn_ws1': _L0_ffn_in['ws1'], 'L0_ffn_bs1': _L0_ffn_in['bs1'], 'L0_ffn_ws2': _L0_ffn_in['ws2'], 'L0_ffn_bs2': _L0_ffn_in['bs2'], 'L0_ffn_ws3': _L0_ffn_in['ws3'], 'L0_ffn_bs3': _L0_ffn_in['bs3'], 'L1_attn_W_q': _L1_attn_in['W_q'], 'L1_attn_W_kv': _L1_attn_in['W_kv'], 'L1_attn_W_o': _L1_attn_in['W_o'], 'L1_xattn_ssm_kernel': _L1_xattn_in['ssm_kernel'], 'L1_xattn_D': _L1_xattn_in['D'], 'L1_ffn_Wr': _L1_ffn_in['Wr'], 'L1_ffn_Wg': _L1_ffn_in['Wg'], 'L1_ffn_Wu': _L1_ffn_in['Wu'], 'L1_ffn_Wd': _L1_ffn_in['Wd']}

def reference(x, fside_S2_0, ctx_2048, L0_attn_Wq, L0_attn_Wk, L0_attn_Wv, L0_attn_Wo, L0_xattn_k, L0_ffn_gate_w, L0_ffn_gate_b, L0_ffn_w1, L0_ffn_b1, L0_ffn_w2, L0_ffn_b2, L0_ffn_w3, L0_ffn_b3, L0_ffn_ws1, L0_ffn_bs1, L0_ffn_ws2, L0_ffn_bs2, L0_ffn_ws3, L0_ffn_bs3, L1_attn_W_q, L1_attn_W_kv, L1_attn_W_o, L1_xattn_ssm_kernel, L1_xattn_D, L1_ffn_Wr, L1_ffn_Wg, L1_ffn_Wu, L1_ffn_Wd):
    import jax
    import jax.numpy as jnp

    def _L0_attn_ref(x, Wq, Wk, Wv, Wo):
        import math
        import jax, jax.numpy as jnp
        import numpy as np
        N_HEADS = 16
        N_KV_HEADS = 4
        HEAD_DIM = 128
        D_MODEL = 256
        THETA = 10000.0
        SCALE_BASE = 64

        def _rope_cos_sin(seq_len, head_dim, theta):
            half = head_dim // 2
            inv_freq = 1.0 / theta ** (jnp.arange(half, dtype=jnp.float32) / half)
            pos = jnp.arange(seq_len, dtype=jnp.float32)
            freqs = jnp.outer(pos, inv_freq)
            freqs = jnp.concatenate([freqs, freqs], axis=-1)
            return (jnp.cos(freqs), jnp.sin(freqs))

        def _rotate_half(x):
            half = x.shape[-1] // 2
            return jnp.concatenate([-x[..., half:], x[..., :half]], axis=-1)

        def _xpos_scale(seq_len, head_dim, scale_base):
            pos = jnp.arange(seq_len, dtype=jnp.float32)
            scale = (pos + scale_base / 2.0) / scale_base
            half = head_dim // 2
            s = jnp.broadcast_to(scale[:, None], (seq_len, half))
            return jnp.stack([s, 1.0 / s], axis=-1).reshape(seq_len, head_dim)
        B, S, _ = x.shape
        kv_groups = N_HEADS // N_KV_HEADS
        q = (x @ Wq).reshape(B, S, N_HEADS, HEAD_DIM).transpose(0, 2, 1, 3)
        k = (x @ Wk).reshape(B, S, N_KV_HEADS, HEAD_DIM).transpose(0, 2, 1, 3)
        v = (x @ Wv).reshape(B, S, N_KV_HEADS, HEAD_DIM).transpose(0, 2, 1, 3)
        cos, sin = _rope_cos_sin(S, HEAD_DIM, THETA)
        cos = cos[None, None]
        sin = sin[None, None]
        q = q * cos + _rotate_half(q) * sin
        k = k * cos + _rotate_half(k) * sin
        xscale = _xpos_scale(S, HEAD_DIM, SCALE_BASE)[None, None]
        q = q * xscale
        k = k * (1.0 / xscale)
        k = jnp.repeat(k, kv_groups, axis=1)
        v = jnp.repeat(v, kv_groups, axis=1)
        scale = math.sqrt(HEAD_DIM)
        scores = jnp.einsum('bhqd,bhkd->bhqk', q, k) / scale
        causal = jnp.tril(jnp.ones((S, S), dtype=bool))
        scores = jnp.where(causal[None, None], scores, -jnp.inf)
        attn = jax.nn.softmax(scores, axis=-1)
        out = jnp.einsum('bhqk,bhkd->bhqd', attn, v)
        out = out.transpose(0, 2, 1, 3).reshape(B, S, N_HEADS * HEAD_DIM)
        return out @ Wo

    def _L0_xattn_ref(v, k, bias, x1, x2, num_heads):
        import jax, jax.numpy as jnp
        import numpy as np
        B, D, L = v.shape
        H = D // num_heads
        fft_size = 2 * L
        vr = v.reshape(B, H, num_heads, L)
        x1r = x1.reshape(B, H, num_heads, L)
        x2r = x2.reshape(B, H, num_heads, L)
        kv = vr[:, :, :, None, :] * x2r[:, :, None, :, :]
        k_f = jnp.fft.rfft(k.astype(jnp.float32), n=fft_size)
        y = jnp.fft.irfft(jnp.fft.rfft(kv, n=fft_size) * k_f[None, :, None, None, :], n=fft_size)[..., :L]
        skip = bias.astype(jnp.float32).reshape(H, num_heads)[None, :, :, None, None]
        y = y + kv * skip
        out = jnp.einsum('bhijl,bhil->bhjl', y, x1r)
        return out.reshape(B, D, L)

    def _L0_ffn_ref(x, gate_w, gate_b, w1, b1, w2, b2, w3, b3, ws1, bs1, ws2, bs2, ws3, bs3):
        import jax, jax.numpy as jnp
        import numpy as np
        E = 16
        D = 256
        H = 176
        HS = 2 * 176
        TOP_K = 6
        ROUTE_SCALE = 1.0
        shape = x.shape
        xf = x.reshape(-1, shape[-1])
        scores = xf @ gate_w.T
        probs = jax.nn.softmax(scores.astype(jnp.float32), axis=-1)
        biased = probs + gate_b
        _, idx = jax.lax.top_k(biased, TOP_K)
        weights = jnp.take_along_axis(probs, idx, axis=1) * ROUTE_SCALE
        weights = weights.astype(x.dtype)
        onehot = jax.nn.one_hot(idx, E, dtype=weights.dtype)
        cw = jnp.einsum('tk,tke->te', weights, onehot)

        def expert_step(y, params):
            W1, B1, W2, B2, W3, B3, c = params
            h = jax.nn.silu(xf @ W1.T + B1) * (xf @ W3.T + B3)
            out = h @ W2.T + B2
            return (y + c[:, None] * out, None)
        y0 = jnp.zeros_like(xf)
        y, _ = jax.lax.scan(expert_step, y0, (w1, b1, w2, b2, w3, b3, cw.T))
        z = jax.nn.silu(xf @ ws1.T + bs1) * (xf @ ws3.T + bs3) @ ws2.T + bs2
        return (y + z).reshape(shape)

    def _L1_attn_ref(x, W_q, W_kv, W_o):
        import jax, jax.numpy as jnp
        import numpy as np
        NUM_HEADS = 16

        def _l2_normalize_complex(z):
            n = jnp.sqrt(jnp.sum(jnp.abs(z) ** 2, axis=-1, keepdims=True))
            return z / n
        B, S, D = x.shape
        H = NUM_HEADS
        hd = D // H
        q = (x @ W_q.T).reshape(B, S, H, hd)
        kv = (x @ W_kv.T).reshape(B, S, H, hd)
        qf = jnp.fft.fft(q, axis=-1)
        kvf = jnp.fft.fft(kv, axis=-1)
        qf = _l2_normalize_complex(qf)
        kvf = _l2_normalize_complex(kvf)
        kvf = jnp.cumsum(kvf, axis=1)
        qv = qf * kvf
        values_hat = jnp.fft.ifft(qv, axis=-1).real.astype(x.dtype)
        values_hat = values_hat.reshape(B, S, D)
        return values_hat @ W_o.T

    def _L1_xattn_ref(k, v, q, ssm_kernel, D, head_dim):
        import jax, jax.numpy as jnp
        import numpy as np
        B, HD, L = k.shape
        H = HD // head_dim
        fft_size = 2 * L
        k_ = k.reshape(B, H, head_dim, L)
        v_ = v.reshape(B, H, head_dim, L)
        q_ = q.reshape(B, H, head_dim, L)
        kv = jnp.einsum('bhil,bhjl->bijhl', k_, v_)
        kv_f = jnp.fft.rfft(kv, n=fft_size)
        kernel_f = jnp.fft.rfft(ssm_kernel, n=fft_size)
        y = jnp.fft.irfft(kv_f * kernel_f, n=fft_size)[..., :L]
        out = y + kv * D[None, None, None, :, None]
        out = jnp.einsum('bijhl,bhil->bjhl', out, q_)
        out = jnp.transpose(out, (0, 2, 1, 3)).reshape(B, H * head_dim, L)
        return out.astype(k.dtype)

    def _L1_ffn_ref(hidden_states, Wr, Wg, Wu, Wd):
        import jax, jax.numpy as jnp
        import numpy as np
        NUM_EXPERTS = 8
        TOP_K = 2
        HIDDEN = 256
        INTER = 256
        SWIGLU_LIMIT = 7.0
        BATCH, SEQ = (4, 256)
        router_logits = jnp.einsum('bsh,he->bse', hidden_states, Wr)
        topk_logits, selected = jax.lax.top_k(router_logits, TOP_K)
        router_probs = jax.nn.softmax(topk_logits, axis=-1)
        out = jnp.zeros_like(hidden_states)
        for e in range(NUM_EXPERTS):
            w_e = jnp.where(selected == e, router_probs, 0.0).sum(axis=-1, keepdims=True)
            g = jnp.einsum('bsh,hi->bsi', hidden_states, Wg[e])
            g = jnp.clip(jax.nn.silu(g), -SWIGLU_LIMIT, SWIGLU_LIMIT)
            u = jnp.einsum('bsh,hi->bsi', hidden_states, Wu[e])
            h = jnp.einsum('bsi,ih->bsh', g * u, Wd[e])
            out = out + h * w_e
        return out
    x = x + _L0_attn_ref(_layernorm(x, axis=-1), L0_attn_Wq, L0_attn_Wk, L0_attn_Wv, L0_attn_Wo)
    x = x + _L0_xattn_ref(_layernorm(x, axis=-1), L0_xattn_k, fside_S2_0, ctx_2048, ctx_2048, 8)
    x = x + _L0_ffn_ref(_layernorm(x, axis=-1), L0_ffn_gate_w, L0_ffn_gate_b, L0_ffn_w1, L0_ffn_b1, L0_ffn_w2, L0_ffn_b2, L0_ffn_w3, L0_ffn_b3, L0_ffn_ws1, L0_ffn_bs1, L0_ffn_ws2, L0_ffn_bs2, L0_ffn_ws3, L0_ffn_bs3)
    x = x + _L1_attn_ref(_layernorm(x, axis=-1), L1_attn_W_q, L1_attn_W_kv, L1_attn_W_o)
    x = x + _L1_xattn_ref(ctx_2048, ctx_2048, _layernorm(x, axis=-1), L1_xattn_ssm_kernel, L1_xattn_D, 8)
    x = x + _L1_ffn_ref(_layernorm(x, axis=-1), L1_ffn_Wr, L1_ffn_Wg, L1_ffn_Wu, L1_ffn_Wd)
    return x

_drawn_inputs = setup_inputs


def setup_inputs(seed=0):
    import zlib

    import numpy as np

    out = dict(_drawn_inputs(seed))
    spreads = {}
    factors = {'L0_ffn_gate_w': 8.0,
     'L0_ffn_gate_b': 8.0,
     'L0_ffn_w1': 8.0,
     'L0_ffn_b1': 8.0,
     'L0_ffn_w2': 8.0,
     'L0_ffn_b2': 46.458,
     'L0_ffn_w3': 8.0,
     'L0_ffn_b3': 8.0,
     'L0_ffn_ws1': 8.0,
     'L0_ffn_bs1': 8.0,
     'L0_ffn_ws2': 8.0,
     'L0_ffn_bs2': 25.9,
     'L0_ffn_ws3': 8.0,
     'L0_ffn_bs3': 8.0,
     'L1_ffn_Wr': 8.0,
     'L1_ffn_Wg': 8.0,
     'L1_ffn_Wu': 8.0,
     'L1_ffn_Wd': 8.0,
     'L1_attn_W_q': 3.842,
     'L1_attn_W_kv': 3.91,
     'L1_attn_W_o': 3.705}
    for name, (base, spread) in spreads.items():
        noise = np.random.default_rng([zlib.crc32(name.encode()), seed]).standard_normal(out[name].shape)
        drawn = base * np.exp(spread * noise) if base else spread * noise
        out[name] = jnp.asarray(drawn.astype(out[name].dtype))
    for name, factor in factors.items():
        out[name] = (out[name] * factor).astype(out[name].dtype)
    return out
```

```python
from contextlib import ExitStack

import numpy as np
import concourse.bass as bass
from concourse import mybir

F32 = mybir.dt.float32
F32R = mybir.dt.float32r
BF16 = mybir.dt.bfloat16
ALU = mybir.AluOpType
ACT = mybir.ActivationFunctionType
AX = mybir.AxisListType

P = 128
B = 16
S = 128
D = 256
DC = D // P
EPS = 1e-5

HEADS, KV, HD = 16, 4, 128
REP = HEADS // KV
GQ = REP * HD
GC = GQ + 2 * HD
MASKED = -1e30


def three_pass(pe, out, lhs, rhs, start, stop):
    (lh, ll), (rh, rl) = lhs, rhs
    pe.matmul(out, lh, rh, start=start, stop=False)
    pe.matmul(out, lh, rl, start=False, stop=False)
    return pe.matmul(out, ll, rh, start=False, stop=stop)


def wait_from(eng, semaphore, count):
    if not isinstance(count, int) or count > 0:
        eng.wait_ge(semaphore, count)


def copy_hi(act, dst, src):
    return act.activation(dst, src, ACT.Copy)


def sub_lo(eng, dst, src, hi):
    return eng.tensor_tensor(dst, src, hi.bitcast(F32), ALU.subtract)


class Core:

    def __init__(self, nc, stack, dram):
        self.nc, self.stack, self.dram = nc, stack, dram
        self.x = self.sbuf(stack, "x", [P, B, D])
        self.ctxT = self.sbuf(stack, "ctxT_sb", [P, DC, B * S])
        self.ident = self.sbuf(stack, "ident_sb", [P, P])
        self.mark = self.sbuf(stack, "mark", [P, 1])
        self.kinds, self.used_again = {}, []
        self.minus_half = self.sbuf(stack, "minus_half", [P, 1])
        (self.x0_loaded, self.x_loaded, self.const_loaded, self.ctx_loaded, self.half_set,
         self.stored) = self.sems("", "x0_loaded x_loaded const_loaded ctx_loaded half_set stored")

    def sems(self, tag, names):
        return [self.stack.enter_context(self.nc.semaphore(tag + n)) for n in names.split()]

    def layer_sems(self, kind, names):
        if (kind, names) in self.kinds:
            self.used_again += self.kinds[kind, names]
        else:
            self.kinds[kind, names] = self.sems(kind, names)
        return self.kinds[kind, names]

    def start(self, gate):
        again, self.used_again = self.used_again, []
        if not again:
            return lambda eng: eng.wait_ge(*gate), lambda pool: None
        cleared, entered = self.sems(f"{len(again)}_", "cleared entered")

        def clear(pool):
            pool.wait_ge(*gate)
            for s in again:
                pool.sem_clear(s)
            pool.memset(self.mark[:, :], 0.0).then_inc(cleared, 1)

        def enter(eng):
            eng.wait_ge(cleared, 1)
            eng.sem_inc(entered, 1)

        return enter, clear

    def sbuf(self, ctx, name, shape, dt=F32):
        return ctx.enter_context(self.nc.sbuf_tensor(name, shape, dt))

    def psum(self, ctx, name, shape, dt=F32):
        return ctx.enter_context(self.nc.psum_tensor(name, shape, dt))

    def tile(self, b):
        return self.x[:, bass.ds(b, 1), :].rearrange("p a d -> p (a d)")


def constants():
    half = HD // 2
    inv = (1.0 / 10000.0 ** (np.arange(half, dtype=np.float64) / half))
    ang = np.outer(np.arange(S), inv)
    cos = np.concatenate([np.cos(ang)] * 2, -1)
    sin = np.concatenate([-np.sin(ang), np.sin(ang)], -1)
    s = (np.arange(S) + 32.0) / 64.0
    xs = np.where(np.arange(HD) % 2 == 0, s[:, None], 1.0 / s[:, None])
    q = xs / np.sqrt(HD)
    rope = np.concatenate([cos * q, sin * q, cos / xs, sin / xs], -1)
    mask = np.where(np.arange(S)[None, :] > np.arange(S)[:, None], MASKED, 0.0)
    forward, inverse = transforms()
    return {
        "forward": forward,
        "inverse": inverse,
        "before": np.triu(np.ones((S, S), np.float32)),
        "pick0": pick(Layer0),
        "pick1": pick(Layer1),
        "same_head": np.kron(np.eye(S // 8), np.ones((8, 8))).astype(np.float32),
        "ident": np.eye(P, dtype=np.float32),
        "rope": rope.astype(np.float32),
        "mask": mask.astype(np.float32),
    }


def attention0(core, ctx):
    dram, x, ident, minus_half = core.dram, core.x, core.ident, core.minus_half
    x0_loaded, x_loaded, const_loaded, half_set = core.x0_loaded, core.x_loaded, core.const_loaded, core.half_set
    w_h = core.sbuf(ctx, "a0_w_h", [P, DC, KV, GC], F32R)
    w_l = core.sbuf(ctx, "a0_w_l", [P, DC, KV, GC], F32R)
    wo_h = core.sbuf(ctx, "a0_wo_h", [P, HEADS, D], F32R)
    wo_l = core.sbuf(ctx, "a0_wo_l", [P, HEADS, D], F32R)
    w_raw = core.sbuf(ctx, "a0_w_raw", [P, 2, DC, GC])
    wo_raw = core.sbuf(ctx, "a0_wo_raw", [P, 2, REP, D])
    rope = core.sbuf(ctx, "a0_rope", [P, 4, HD])
    mask_f = core.sbuf(ctx, "a0_mask_f", [P, S])
    mask = core.sbuf(ctx, "a0_mask", [P, S], BF16)
    ident_b = core.sbuf(ctx, "a0_ident_b", [P, P], BF16)
    stats = core.sbuf(ctx, "a0_stats", [P, 6])
    mv = core.sbuf(ctx, "a0_mv", [P, 2])
    vare = core.sbuf(ctx, "a0_vare", [P, 1])
    rstd = core.sbuf(ctx, "a0_rstd", [P, 1])
    xn = core.sbuf(ctx, "a0_xn", [P, D])
    xT_h = core.sbuf(ctx, "a0_xT_h", [P, DC, P], F32R)
    xT_l = core.sbuf(ctx, "a0_xT_l", [P, DC, P], F32R)
    rc = core.sbuf(ctx, "a0_rc", [P, GQ + HD])
    rs = core.sbuf(ctx, "a0_rs", [P, GQ + HD])
    qk = core.sbuf(ctx, "a0_qk", [P, GQ + HD])
    v_h = core.sbuf(ctx, "a0_v_h", [P, KV, HD], F32R)
    v_l = core.sbuf(ctx, "a0_v_l", [P, KV, HD], F32R)
    qkT_h = core.sbuf(ctx, "a0_qkT_h", [P, 2, GQ + HD], F32R)
    qkT_l = core.sbuf(ctx, "a0_qkT_l", [P, 2, GQ + HD], F32R)
    nmax = core.sbuf(ctx, "a0_nmax", [P, 2, REP])
    rsum = core.sbuf(ctx, "a0_rsum", [P, 2, REP])
    rinv = core.sbuf(ctx, "a0_rinv", [P, 2, REP])
    pr = core.sbuf(ctx, "a0_pr", [P, 2, REP, S])
    pT_h = core.sbuf(ctx, "a0_pT_h", [P, REP * S], F32R)
    pT_l = core.sbuf(ctx, "a0_pT_l", [P, REP * S], F32R)
    oT_h = core.sbuf(ctx, "a0_oT_h", [P, REP, S], F32R)
    oT_l = core.sbuf(ctx, "a0_oT_l", [P, REP, S], F32R)

    ps_q = core.psum(ctx, "a0_ps_q", [P, 512])
    ps_kvx = core.psum(ctx, "a0_ps_kvx", [P, 512])
    ps_t = core.psum(ctx, "a0_ps_t", [P, 1024])
    ps_s = core.psum(ctx, "a0_ps_s", [P, 512])
    ps_pT = core.psum(ctx, "a0_ps_pT", [P, 512])
    ps_oT = core.psum(ctx, "a0_ps_oT", [P, 512])
    ps_y = core.psum(ctx, "a0_ps_y", [P, 512])
    ps_kv, ps_xT = ps_kvx[:, 0:2 * HD], ps_kvx[:, 2 * HD:512]

    w_loaded = core.sems("a0_", "w_loaded_even w_loaded_odd")
    wo_loaded = core.sems("a0_", "wo_loaded_even wo_loaded_odd")
    (w_hi, w_lo, wo_hi, wo_lo, stat_done, var_done, rstd_done, xn_done,
     xt_done, xt_hi, xt_lo, proj_done, rope_mul, roped, v_hi, v_lo, tq_done, qkt_hi, qkt_lo,
     scores_done, max_done, exp_done, recip_done, norm_done, pt_done, pt_hi, pt_lo, pv_done,
     ot_hi, ot_lo, wo_done, y_added, cast_done) = core.sems("a0_", (
         "w_hi w_lo wo_hi wo_lo stat_done var_done rstd_done xn_done "
         "xt_done xt_hi xt_lo proj_done rope_mul roped v_hi v_lo tq_done qkt_hi qkt_lo "
         "scores_done max_done exp_done recip_done norm_done pt_done pt_hi pt_lo pv_done "
         "ot_hi ot_lo wo_done y_added cast_done"))

    w_q = dram["L0_attn_Wq"].rearrange("(c p) n -> p c n", p=P)
    w_k = dram["L0_attn_Wk"].rearrange("(c p) n -> p c n", p=P)
    w_v = dram["L0_attn_Wv"].rearrange("(c p) n -> p c n", p=P)
    w_o = dram["L0_attn_Wo"].rearrange("(h p) n -> p h n", p=P)


    def attn0_sync(sp):
        xs = dram["x"].rearrange("b s d -> s b d")
        sp.dma_start(x[:, 0:1, :], xs[:, 0:1, :]).then_inc(x0_loaded, 16)
        sp.dma_start(ident[:, :], dram["ident"]).then_inc(const_loaded, 16)
        sp.dma_start(rope[:, :, :], dram["rope"].rearrange("s (a d) -> s a d", a=4)).then_inc(const_loaded, 16)
        sp.dma_start(mask_f[:, :], dram["mask"]).then_inc(const_loaded, 16)
        def load_out(g):
            if g >= 2:
                sp.wait_ge(wo_lo, g - 1)
            sp.dma_start(wo_raw[:, g % 2, :, :], w_o[:, g * REP:(g + 1) * REP, :]).then_inc(wo_loaded[g % 2], 16)

        for g in range(KV):
            if g >= 2:
                sp.wait_ge(w_lo, g - 1)
            sp.dma_start(w_raw[:, g % 2, :, 0:GQ], w_q[:, :, g * GQ:(g + 1) * GQ]).then_inc(w_loaded[g % 2], 16)
            sp.dma_start(w_raw[:, g % 2, :, GQ:GQ + HD], w_k[:, :, g * HD:(g + 1) * HD]).then_inc(w_loaded[g % 2], 16)
            sp.dma_start(w_raw[:, g % 2, :, GQ + HD:GC], w_v[:, :, g * HD:(g + 1) * HD]).then_inc(w_loaded[g % 2], 16)
            if g == 1:
                sp.dma_start(x[:, 1:B, :], xs[:, 1:B, :]).then_inc(x_loaded, 16)
            if g >= 1:
                load_out(g - 1)
        load_out(KV - 1)
        sp.dma_start(core.ctxT[:, :, :], dram["ctxT"].rearrange("(c p) t -> p c t", p=P)).then_inc(core.ctx_loaded, 16)

    def attn0_tensor(pe):
        def transpose_x(b, n):
            pe.wait_ge(xn_done, b + 1)
            if n is not None:
                pe.wait_ge(v_lo, n)
            for c in range(DC):
                last = pe.transpose(ps_xT[:, c * P:(c + 1) * P], xn[:, c * P:(c + 1) * P], ident[:, :])
            last.then_inc(xt_done, 1)

        def project(b, g, n):
            if isinstance(n, int) and n < KV:
                pe.wait_ge(w_hi, g + 1)
                pe.wait_ge(w_lo, g + 1)
            if g == 0:
                pe.wait_ge(xt_hi, b + 1)
                pe.wait_ge(xt_lo, b + 1)
            for lo, hi, dst, read in ((0, GQ, ps_q[:, :], rope_mul), (GQ, GC, ps_kv, v_lo)):
                wait_from(pe, read, n)
                for c in range(DC):
                    last = three_pass(pe, dst, (xT_h[:, c, :], xT_l[:, c, :]),
                                      (w_h[:, c, g, lo:hi], w_l[:, c, g, lo:hi]), c == 0, c == DC - 1)
            last.then_inc(proj_done, 1)

        def transpose_qk(g, n):
            pe.wait_ge(roped, n + 1)
            wait_from(pe, qkt_lo, n)
            for h in range(REP + 1):
                last = pe.transpose(ps_t[:, h * P:(h + 1) * P], qk[:, h * HD:(h + 1) * HD], ident[:, :])
            last.then_inc(tq_done, 1)

        def scores(g, m):
            pe.wait_ge(qkt_hi, m + 1)
            pe.wait_ge(qkt_lo, m + 1)
            wait_from(pe, exp_done, m)
            pe.matmul(ps_s[:, :], ident_b[:, :], mask[:, :].unsqueeze(1).to_broadcast([P, REP, S]),
                      start=True, stop=False, skip_group_check=True)
            k = slice(GQ, GQ + HD)
            for h in range(REP):
                q = slice(h * HD, (h + 1) * HD)
                o = ps_s[:, h * S:(h + 1) * S]
                for a, w in ((qkT_h, qkT_h), (qkT_h, qkT_l), (qkT_l, qkT_h)):
                    last = pe.matmul(o, a[:, g % 2, q], w[:, g % 2, k], start=False,
                                     stop=a is qkT_l and h == REP - 1, skip_group_check=True)
            last.then_inc(scores_done, 1)

        def transpose_p(g, m):
            pe.wait_ge(norm_done, m + 1)
            wait_from(pe, pt_lo, m)
            for h in range(REP):
                last = pe.transpose(ps_pT[:, h * P:(h + 1) * P], pr[:, g % 2, h, :], ident[:, :])
            last.then_inc(pt_done, 1)

        def weigh_values(g, m):
            pe.wait_ge(pt_hi, m + 1)
            pe.wait_ge(pt_lo, m + 1)
            pe.wait_ge(v_hi, m + 1)
            pe.wait_ge(v_lo, m + 1)
            wait_from(pe, ot_lo, m)
            three_pass(pe, ps_oT[:, :], (v_h[:, g, :], v_l[:, g, :]),
                       (pT_h[:, :], pT_l[:, :]), True, True).then_inc(pv_done, 1)

        def project_out(b, g, m):
            if isinstance(m, int) and m < KV:
                pe.wait_ge(wo_hi, g + 1)
                pe.wait_ge(wo_lo, g + 1)
            pe.wait_ge(ot_hi, m + 1)
            pe.wait_ge(ot_lo, m + 1)
            if g == 0:
                wait_from(pe, y_added, b)
            for h in range(REP):
                last = three_pass(pe, ps_y[:, 0:D], (oT_h[:, h, :], oT_l[:, h, :]),
                                  (wo_h[:, g * REP + h, :], wo_l[:, g * REP + h, :]),
                                  g == 0 and h == 0, g == KV - 1 and h == REP - 1)
            last.then_inc(wo_done, 1)

        def sequence(b, head, tail):
            for g in range(KV):
                m = KV * b + g
                before, back = (b, g - 1) if g else (b - 1, KV - 1), not (head and g == 0)
                scores(g, m)
                if g == KV - 2 and not tail:
                    transpose_x(b + 1, m + 2)
                if back:
                    weigh_values(before[1], m - 1)
                if not (tail and g == KV - 1):
                    transpose_qk((g + 1) % KV, m + 1)
                if not (tail and g >= KV - 2):
                    project(b + (g + 2) // KV, (g + 2) % KV, m + 2)
                if back:
                    project_out(*before, m - 1)
                transpose_p(g, m)

        pe.wait_ge(const_loaded, 48)
        transpose_x(0, None)
        project(0, 0, 0)
        transpose_qk(0, 0)
        project(0, 1, 1)
        pe.wait_ge(cast_done, 2)
        sequence(0, True, False)
        with pe.Fori(1, B - 1) as b:
            sequence(b, False, False)
        sequence(B - 1, False, True)
        weigh_values(KV - 1, KV * B - 1)
        project_out(B - 1, KV - 1, KV * B - 1)

    def attn0_scalar(act):
        def copy_hi(dst, src, done):
            act.activation(dst, src, ACT.Copy).then_inc(done, 1)

        def output_hi(m):
            act.wait_ge(pv_done, m + 1)
            wait_from(act, wo_done, m)
            copy_hi(oT_h[:, :, :], ps_oT[:, :], ot_hi)

        def exps(g, m):
            act.wait_ge(max_done, m + 1)
            wait_from(act, pt_done, m - 1)
            for h in range(REP):
                last = act.activation(pr[:, g % 2, h, :], ps_s[:, h * S:(h + 1) * S], ACT.Exp,
                                      bias=nmax[:, g % 2, h:h + 1], accum_out=rsum[:, g % 2, h:h + 1])
            last.then_inc(exp_done, 1)

        def values_hi(g, n):
            act.wait_ge(rope_mul, n + 1)
            wait_from(act, pv_done, n - 3)
            copy_hi(v_h[:, g, :], ps_kv[:, HD:2 * HD], v_hi)

        def x_hi(b):
            act.wait_ge(xt_done, b + 1)
            copy_hi(xT_h[:, :, :], ps_xT, xt_hi)

        def probs_hi(m):
            act.wait_ge(pt_done, m + 1)
            wait_from(act, pv_done, m)
            copy_hi(pT_h[:, :], ps_pT[:, :], pt_hi)

        def qk_hi(g, n):
            act.wait_ge(tq_done, n + 1)
            wait_from(act, scores_done, n - 1)
            copy_hi(qkT_h[:, g % 2, :], ps_t[:, 0:GQ + HD], qkt_hi)

        def split_in(g):
            act.wait_ge(w_loaded[g % 2], 48 * (g // 2 + 1))
            copy_hi(w_h[:, :, g, :], w_raw[:, g % 2, :, :], w_hi)

        def split_out(g):
            act.wait_ge(wo_loaded[g % 2], 16 * (g // 2 + 1))
            copy_hi(wo_h[:, g * REP:(g + 1) * REP, :], wo_raw[:, g % 2, :, :], wo_hi)

        def sequence(b, head, tail):
            for g in range(KV):
                m = KV * b + g
                if not (head and g == 0):
                    probs_hi(m - 1)
                if g == KV - 2 and not tail:
                    x_hi(b + 1)
                if not (head and g == 0):
                    output_hi(m - 1)
                exps(g, m)
                if not (tail and g == KV - 1):
                    qk_hi((g + 1) % KV, m + 1)
                if head:
                    if g < 2:
                        split_in(g + 2)
                    split_out(g)
                if not (tail and g >= KV - 2):
                    values_hi((g + 2) % KV, m + 2)

        x_hi(0)
        split_in(0)
        act.wait_ge(const_loaded, 48)
        act.activation(ident_b[:, :], ident[:, :], ACT.Copy).then_inc(cast_done, 1)
        act.activation(mask[:, :], mask_f[:, :], ACT.Copy).then_inc(cast_done, 1)
        values_hi(0, 0)
        split_in(1)
        qk_hi(0, 0)
        values_hi(1, 1)
        sequence(0, True, False)
        with act.Fori(1, B - 1) as b:
            sequence(b, False, False)
        sequence(B - 1, False, True)
        probs_hi(KV * B - 1)
        output_hi(KV * B - 1)

    def attn0_gpsimd(pool):
        def rstd_of(b):
            pool.wait_ge(var_done, b + 1)
            wait_from(pool, xn_done, b)
            pool.tensor_tensor(rstd[:, :], vare[:, :], minus_half[:, :], ALU.pow).then_inc(rstd_done, 1)

        def add_rotated(n):
            pool.wait_ge(rope_mul, n + 1)
            wait_from(pool, tq_done, n)
            pool.tensor_tensor(qk[:, :], rc[:, :], rs[:, :], ALU.add).then_inc(roped, 1)

        def normalise(g, m):
            pool.wait_ge(recip_done, m + 1)
            pool.tensor_tensor(pr[:, g % 2, :, :], pr[:, g % 2, :, :],
                               rinv[:, g % 2, :].unsqueeze(2).to_broadcast([P, REP, S]),
                               ALU.mult).then_inc(norm_done, 1)

        def split_in(g):
            pool.wait_ge(w_hi, g + 1)
            sub_lo(pool, w_l[:, :, g, :], w_raw[:, g % 2, :, :], w_h[:, :, g, :]).then_inc(w_lo, 1)

        def split_out(g):
            pool.wait_ge(wo_hi, g + 1)
            gs = slice(g * REP, (g + 1) * REP)
            sub_lo(pool, wo_l[:, gs, :], wo_raw[:, g % 2, :, :], wo_h[:, gs, :]).then_inc(wo_lo, 1)

        def sequence(b, head, tail):
            for g in range(KV):
                m = KV * b + g
                if g == 1 and not tail:
                    rstd_of(b + 1)
                normalise(g, m)
                if head:
                    if g < 2:
                        split_in(g + 2)
                    split_out(g)
                if not (tail and g >= KV - 2):
                    add_rotated(m + 2)

        pool.memset(minus_half[:, :], -0.5).then_inc(half_set, 1)
        pool.wait_ge(half_set, 1)
        rstd_of(0)
        split_in(0)
        add_rotated(0)
        split_in(1)
        add_rotated(1)
        sequence(0, True, False)
        with pool.Fori(1, B - 1) as b:
            sequence(b, False, False)
        sequence(B - 1, False, True)

    def attn0_vector(dve):
        def lo(dst, src, hi, done):
            dve.tensor_tensor(dst, src, hi.bitcast(F32), ALU.subtract).then_inc(done, 1)

        def stats_x(b):
            tile = x[:, bass.ds(b, 1), :].rearrange("p a d -> p (a d)")
            dve.bn_stats(stats[:, :], tile).then_inc(stat_done, 1)

        def norm_x(b):
            tile = x[:, bass.ds(b, 1), :].rearrange("p a d -> p (a d)")
            dve.bn_aggr(mv[:, :], stats[:, :]).then_inc(stat_done, 1)
            dve.wait_ge(stat_done, 2 * b + 2)
            dve.tensor_scalar(vare[:, :], mv[:, 1:2], EPS, None, ALU.add).then_inc(var_done, 1)
            dve.wait_ge(rstd_done, b + 1)
            wait_from(dve, xt_done, b)
            dve.tensor_scalar(xn[:, :], tile, mv[:, 0:1], rstd[:, 0:1], ALU.subtract,
                              ALU.mult).then_inc(xn_done, 1)

        def x_lo(b):
            dve.wait_ge(xt_hi, b + 1)
            lo(xT_l[:, :, :].rearrange("p c s -> p (c s)"), ps_xT,
               xT_h[:, :, :].rearrange("p c s -> p (c s)"), xt_lo)

        def rotate(n):
            dve.wait_ge(proj_done, n + 1)
            wait_from(dve, roped, n)
            for o, w, src, cos, sin in ((0, REP, ps_q[:, :], rope[:, 0, :], rope[:, 1, :]),
                                        (GQ, 1, ps_kv[:, 0:HD], rope[:, 2, :], rope[:, 3, :])):
                halves = [P, w, 2, HD // 2]

                def table(t):
                    return t.rearrange("p (a d) -> p a d", a=2).unsqueeze(1).to_broadcast(halves)
                src4 = src.rearrange("p (h a d) -> p h a d", a=2, d=HD // 2)
                dve.tensor_tensor(rc[:, o:o + w * HD].rearrange("p (h a d) -> p h a d", a=2, d=HD // 2),
                                  src4, table(cos), ALU.mult)
                last = dve.tensor_tensor(
                    rs[:, o:o + w * HD].rearrange("p (h a d) -> p h a d", a=2, d=HD // 2),
                    src4[:, :, ::-1, :], table(sin), ALU.mult)
            last.then_inc(rope_mul, 1)

        def values_lo(g, n):
            dve.wait_ge(v_hi, n + 1)
            lo(v_l[:, g, :], ps_kv[:, HD:2 * HD], v_h[:, g, :], v_lo)

        def qk_lo(g, n):
            dve.wait_ge(qkt_hi, n + 1)
            lo(qkT_l[:, g % 2, :], ps_t[:, 0:GQ + HD], qkT_h[:, g % 2, :], qkt_lo)

        def row_max(g, m):
            dve.wait_ge(scores_done, m + 1)
            wait_from(dve, exp_done, m - 1)
            dve.tensor_reduce(nmax[:, g % 2, :], ps_s[:, :].rearrange("p (h k) -> p h k", h=REP),
                              AX.X, ALU.max, negate=True).then_inc(max_done, 1)

        def recip(g, m):
            dve.wait_ge(exp_done, m + 1)
            dve.reciprocal(rinv[:, g % 2, :], rsum[:, g % 2, :]).then_inc(recip_done, 1)

        def probs_lo(m):
            dve.wait_ge(pt_hi, m + 1)
            lo(pT_l[:, :], ps_pT[:, :], pT_h[:, :], pt_lo)

        def output_lo(m):
            dve.wait_ge(ot_hi, m + 1)
            lo(oT_l[:, :, :].rearrange("p h s -> p (h s)"), ps_oT[:, :],
               oT_h[:, :, :].rearrange("p h s -> p (h s)"), ot_lo)

        def add_y(b):
            dve.wait_ge(wo_done, KV * b + KV)
            tile = x[:, bass.ds(b, 1), :].rearrange("p a d -> p (a d)")
            dve.tensor_tensor(tile, tile, ps_y[:, 0:D], ALU.add).then_inc(y_added, 1)

        def sequence(b, head, tail):
            for g in range(KV):
                m = KV * b + g
                if not (head and g == 0):
                    probs_lo(m - 1)
                if g == 0 and not tail:
                    stats_x(b + 1)
                row_max(g, m)
                if g == KV - 2 and not tail:
                    x_lo(b + 1)
                if not (head and g == 0):
                    output_lo(m - 1)
                if g == 1 and not tail:
                    dve.wait_ge(stat_done, 2 * b + 3)
                recip(g, m)
                if not (tail and g == KV - 1):
                    qk_lo((g + 1) % KV, m + 1)
                if g == 1 and not tail:
                    norm_x(b + 1)
                if not (tail and g >= KV - 2):
                    rotate(m + 2)
                    values_lo((g + 2) % KV, m + 2)
                if g == 0 and not head:
                    add_y(b - 1)

        dve.wait_ge(x0_loaded, 16)
        stats_x(0)
        dve.wait_ge(stat_done, 1)
        norm_x(0)
        x_lo(0)
        dve.wait_ge(const_loaded, 48)
        rotate(0)
        values_lo(0, 0)
        qk_lo(0, 0)
        rotate(1)
        values_lo(1, 1)
        dve.wait_ge(x_loaded, 16)
        sequence(0, True, False)
        with dve.Fori(1, B - 1) as b:
            sequence(b, False, False)
        sequence(B - 1, False, True)
        probs_lo(KV * B - 1)
        output_lo(KV * B - 1)
        add_y(B - 1)

    return (attn0_sync, attn0_tensor, attn0_scalar, attn0_gpsimd, attn0_vector), (y_added, B)


def row_stats(core, ctx, tag):
    stats = core.sbuf(ctx, tag + "stats", [P, B, 6])
    mv = core.sbuf(ctx, tag + "mv", [P, B, 2])
    vare = core.sbuf(ctx, tag + "vare", [P, B])
    rstd = core.sbuf(ctx, tag + "rstd", [P, B])
    stat_done, var_done, rstd_done = core.layer_sems(tag[0] + "_", "stat_done var_done rstd_done")

    def vector(dve):
        for b in range(B):
            dve.bn_stats(stats[:, b, :], core.x[:, b, :]).then_inc(stat_done, 1)
        for b in range(B):
            dve.wait_ge(stat_done, b + 1)
            last = dve.bn_aggr(mv[:, b, :], stats[:, b, :])
        last.then_inc(stat_done, 1)
        dve.wait_ge(stat_done, B + 1)
        dve.tensor_scalar(vare[:, :], mv[:, :, 1], EPS, None, ALU.add).then_inc(var_done, 1)

    def gpsimd(pool):
        pool.wait_ge(var_done, 1)
        pool.tensor_tensor(rstd[:, :], vare[:, :], core.minus_half[:, :].to_broadcast([P, B]),
                           ALU.pow).then_inc(rstd_done, 1)

    def normalise(dve, dst, b):
        return dve.tensor_scalar(dst, core.tile(b), mv[:, bass.ds(b, 1), 0], rstd[:, bass.ds(b, 1)],
                                 ALU.subtract, ALU.mult)

    return vector, gpsimd, normalise, rstd_done


CH, CW = 16, 8
HB = B // 2
UN = HB * CW * CW


def convolution(core, ctx, gate, tag, taps, context_pairs):
    dram, x, ident, ctxT = core.dram, core.x, core.ident, core.ctxT
    nT = core.sbuf(ctx, tag + "nT", [P, DC, B * S])
    oT = core.sbuf(ctx, tag + "oT", [P, DC, B * S])
    xn = core.sbuf(ctx, tag + "xn", [P, 2, D])
    hankel = core.sbuf(ctx, tag + "hankel", [P, CH, D])
    t_raw = core.sbuf(ctx, tag + "t_raw", [P, CH, D])
    t_h = core.sbuf(ctx, tag + "t_h", [P, 2, D], F32R)
    t_l = core.sbuf(ctx, tag + "t_l", [P, 2, D], F32R)
    p = core.sbuf(ctx, tag + "p", [P, 2, DC, UN])
    p_h = core.sbuf(ctx, tag + "p_h", [P, 2, DC, UN], F32R)
    p_l = core.sbuf(ctx, tag + "p_l", [P, 2, DC, UN], F32R)
    z = core.sbuf(ctx, tag + "z", [P, DC, UN])
    ps_n = [core.psum(ctx, f"{tag}ps_n{k}", [P, 512]) for k in range(2)]
    ps_g = [core.psum(ctx, f"{tag}ps_g{k}", [P, 512]) for k in range(2)]
    ps_c = [[core.psum(ctx, f"{tag}ps_c{k}{c}", [P, 512]) for c in range(DC)] for k in range(2)]
    (taps_loaded, aux_loaded, xn_done, nt_done, nT_done, w_done, w_hi, w_lo, g_done, skip_done, x_skipped,
     diag_done, t_hi, t_lo, prod_done, p_hi, p_lo, conv_done, z_done, o_done, back_done, added, ones_done, t_done) = core.layer_sems(
        "c_", "taps_loaded aux_loaded xn_done nt_done nT_done w_done w_hi w_lo g_done skip_done x_skipped "
        "diag_done t_hi t_lo prod_done p_hi p_lo conv_done z_done o_done back_done added ones_done t_done")
    stats_vector, stats_gpsimd, normalise, rstd_done = row_stats(core, ctx, tag)
    enter, clear = core.start(gate)
    if context_pairs:
        a_of, b_of, c_of = ctxT, ctxT, nT
        dcol = core.sbuf(ctx, tag + "dcol", [P, CH])
    else:
        a_of, b_of, c_of = nT, ctxT, ctxT
        ctok = core.sbuf(ctx, tag + "ctok", [P, B, D])
        skip = core.sbuf(ctx, tag + "skip", [P, 1])
        ones_f = core.sbuf(ctx, tag + "ones_f", [P, P])
        ones = core.sbuf(ctx, tag + "ones", [P, P], F32R)
        w = core.sbuf(ctx, tag + "w", [P, 2, D])
        wh = core.sbuf(ctx, tag + "wh", [P, 2, D], F32R)
        wl = core.sbuf(ctx, tag + "wl", [P, 2, D], F32R)
        sk = core.sbuf(ctx, tag + "sk", [P, 2, D])

    def channels(t, c, h, half, spread):
        v = t[:, c, :].rearrange("p (b h i) -> p b h i", h=CH, i=CW)[:, half * HB:(half + 1) * HB, bass.ds(h, 1), :]
        v = v.rearrange("p b a i -> p b (a i)")
        shape = [P, HB, CW, CW]
        return v.unsqueeze(3).to_broadcast(shape) if spread == "j" else v.unsqueeze(2).to_broadcast(shape)

    def cube(t):
        return t.rearrange("p (b i j) -> p b i j", i=CW, j=CW)

    def toeplitz(h):
        return t_raw[:, bass.ds(h, 1), :].rearrange("p a d -> p (a d)")

    def sync(sp):
        enter(sp)
        rows = bass.AP(dram[taps].tensor, 0, [[1, P], [2 * D, CH], [1, D]])
        sp.dma_start(hankel[:, :, :], rows).then_inc(taps_loaded, 16)
        if context_pairs:
            d = dram["L1_xattn_D"]
            sp.dma_start(dcol[:, :], bass.AP(d.tensor, 0, [[0, P], [1, CH]])).then_inc(aux_loaded, 16)
        else:
            sp.dma_start(skip[:, :], dram["fside_S2_0"].rearrange("(s a) -> s a", a=1)).then_inc(aux_loaded, 16)
            sp.dma_start(ones_f[:, :], dram["same_head"]).then_inc(aux_loaded, 16)
            sp.dma_start(ctok[:, :, :], dram["ctx_2048"].rearrange("b s d -> s b d")).then_inc(aux_loaded, 16)

    def tensor(pe):
        enter(pe)
        pe.wait_ge(core.const_loaded, 48)

        def turn(b, k):
            pe.wait_ge(xn_done, b + 1)
            wait_from(pe, nT_done, b - 1)
            for c in range(DC):
                last = pe.transpose(ps_n[k][:, c * P:(c + 1) * P], xn[:, k, c * P:(c + 1) * P], ident[:, :])
            last.then_inc(nt_done, 1)
            if not context_pairs:
                pe.wait_ge(w_hi, b + 1)
                pe.wait_ge(w_lo, b + 1)
                wait_from(pe, skip_done, b - 1)
                pe.matmul(ps_g[k][:, 0:D], ones[:, :], wh[:, k, :], start=True, stop=False)
                pe.matmul(ps_g[k][:, 0:D], ones[:, :], wl[:, k, :], start=False, stop=True).then_inc(g_done, 1)

        if not context_pairs:
            pe.wait_ge(ones_done, 1)
        for k in range(2):
            turn(k, k)
        with pe.Fori(2, B - 1, 2) as b:
            for k in range(2):
                turn(b + k, k)

        def convolve(h, k, half):
            n = 2 * h + half
            if half == 0:
                pe.wait_ge(t_hi, h + 1)
                pe.wait_ge(t_lo, h + 1)
            pe.wait_ge(p_hi, n + 1)
            pe.wait_ge(p_lo, n + 1)
            wait_from(pe, z_done, 2 * (n - 1))
            near, far = ((t_h[:, k, s], t_l[:, k, s]) for s in (slice(0, P), slice(P, D)))
            pc = [(p_h[:, half, c, :], p_l[:, half, c, :]) for c in range(DC)]
            three_pass(pe, ps_c[half][0][:, :], near, pc[0], True, True)
            three_pass(pe, ps_c[half][1][:, :], far, pc[0], True, False)
            three_pass(pe, ps_c[half][1][:, :], near, pc[1], False, True).then_inc(conv_done, 1)

        for k in range(2):
            for half in range(2):
                convolve(k, k, half)
        with pe.Fori(2, CH - 1, 2) as h:
            for k in range(2):
                for half in range(2):
                    convolve(h + k, k, half)
        for pair in range(B // 2):
            if pair == 0:
                pe.wait_ge(o_done, 4 * CH)
                pe.wait_ge(z_done, 4 * CH)
            if pair >= 2:
                pe.wait_ge(added, pair - 1)
            for j in range(2):
                for c in range(DC):
                    t = (2 * pair + j) * S
                    last = pe.transpose(ps_n[pair % 2][:, j * D + c * P:j * D + (c + 1) * P],
                                        oT[:, c, t:t + S], ident[:, :])
            last.then_inc(back_done, 1)

    def scalar(act):
        enter(act)
        act.wait_ge(taps_loaded, 16)
        act.activation(t_raw[:, :, :], hankel[:, :, ::-1], ACT.Copy).then_inc(t_done, 1)
        if not context_pairs:
            act.wait_ge(aux_loaded, 48)
            copy_hi(act, ones[:, :], ones_f[:, :]).then_inc(ones_done, 1)

        def turn(b, k):
            if not context_pairs:
                act.wait_ge(w_done, b + 1)
                wait_from(act, g_done, b - 1)
                copy_hi(act, wh[:, k, :], w[:, k, :]).then_inc(w_hi, 1)
            act.wait_ge(nt_done, b + 1)
            act.activation(nT[:, :, bass.ds(b * S, S)], ps_n[k][:, 0:D].rearrange("p (c s) -> p c s", c=DC),
                           ACT.Copy).then_inc(nT_done, 1)

        for k in range(2):
            turn(k, k)
        with act.Fori(2, B - 1, 2) as b:
            for k in range(2):
                turn(b + k, k)

        def high(h, k, half):
            n = 2 * h + half
            if half == 0:
                wait_from(act, conv_done, 2 * h - 2)
                if context_pairs:
                    act.wait_ge(diag_done, h + 1)
                copy_hi(act, t_h[:, k, :], toeplitz(h)).then_inc(t_hi, 1)
            act.wait_ge(prod_done, n + 1)
            wait_from(act, conv_done, n - 1)
            copy_hi(act, p_h[:, half, :, :], p[:, half, :, :]).then_inc(p_hi, 1)

        act.wait_ge(t_done, 1)
        for k in range(2):
            for half in range(2):
                high(k, k, half)
        with act.Fori(2, CH - 1, 2) as h:
            for k in range(2):
                for half in range(2):
                    high(h + k, k, half)

    def gpsimd(pool):
        clear(pool)
        enter(pool)
        stats_gpsimd(pool)
        if not context_pairs:
            def add_skip(b, k):
                pool.wait_ge(skip_done, b + 1)
                pool.tensor_tensor(core.tile(b), core.tile(b), sk[:, k, :], ALU.add).then_inc(x_skipped, 1)
            for k in range(2):
                add_skip(k, k)
            with pool.Fori(2, B - 1, 2) as b:
                for k in range(2):
                    add_skip(b + k, k)

        def product(h, half):
            n = 2 * h + half
            wait_from(pool, p_lo, n - 1)
            for c in range(DC):
                last = pool.tensor_tensor(cube(p[:, half, c, :]), channels(a_of, c, h, half, "j"),
                                          channels(b_of, c, h, half, "i"), ALU.mult)
            last.then_inc(prod_done, 1)

        pool.wait_ge(nT_done, B)
        pool.wait_ge(core.ctx_loaded, 16)
        for h in range(2):
            for half in range(2):
                product(h, half)
        with pool.Fori(2, CH) as h:
            for half in range(2):
                product(h, half)

    def vector(dve):
        enter(dve)
        stats_vector(dve)
        dve.wait_ge(rstd_done, 1)

        def norm_tile(b, k):
            wait_from(dve, nt_done, b - 1)
            normalise(dve, xn[:, k, :], b).then_inc(xn_done, 1)
            if not context_pairs:
                dve.wait_ge(xn_done, b + 1)
                wait_from(dve, w_lo, b - 1)
                dve.scalar_tensor_tensor(out=w[:, k, :], in0=xn[:, k, :], scalar=skip[:, 0:1],
                                         in1=ctok[:, bass.ds(b, 1), :].rearrange("p a d -> p (a d)"),
                                         op0=ALU.mult, op1=ALU.mult).then_inc(w_done, 1)
                dve.wait_ge(w_hi, b + 1)
                wait_from(dve, g_done, b - 1)
                sub_lo(dve, wl[:, k, :], w[:, k, :], wh[:, k, :]).then_inc(w_lo, 1)

        def skip_tile(b, k):
            dve.wait_ge(g_done, b + 1)
            wait_from(dve, x_skipped, b - 1)
            dve.tensor_tensor(sk[:, k, :], ps_g[k][:, 0:D],
                              ctok[:, bass.ds(b, 1), :].rearrange("p a d -> p (a d)"), ALU.mult).then_inc(skip_done, 1)

        if not context_pairs:
            dve.wait_ge(aux_loaded, 48)

        def tiles(b):
            for k in range(2):
                norm_tile(b + k, k)
            if not context_pairs:
                for k in range(2):
                    skip_tile(b + k, k)

        tiles(0)
        with dve.Fori(2, B - 1, 2) as b:
            tiles(b)

        def low(h, k, half):
            n = 2 * h + half
            if half == 0:
                dve.wait_ge(t_hi, h + 1)
                wait_from(dve, conv_done, 2 * h - 2)
                sub_lo(dve, t_l[:, k, :], toeplitz(h),
                       t_h[:, k, :]).then_inc(t_lo, 1)
            dve.wait_ge(p_hi, n + 1)
            wait_from(dve, conv_done, n - 1)
            sub_lo(dve, p_l[:, half, :, :], p[:, half, :, :], p_h[:, half, :, :]).then_inc(p_lo, 1)

        def read_out(h, half):
            n = 2 * h + half
            dve.wait_ge(conv_done, n + 1)
            for c in range(DC):
                wait_from(dve, o_done, 2 * n - 1 + c)
                dve.tensor_tensor(cube(z[:, c, :]), cube(ps_c[half][c][:, :]),
                                  channels(c_of, c, h, half, "j"), ALU.mult).then_inc(z_done, 1)
            for c in range(DC):
                dve.wait_ge(z_done, 2 * n + 1 + c)
                dst = oT[:, c, :].rearrange("p (b h j) -> p b h j", h=CH, j=CW)[:, half * HB:(half + 1) * HB, bass.ds(h, 1), :]
                dve.tensor_reduce(dst.rearrange("p b a j -> p b (a j)"), z[:, c, :].rearrange("p (b i j) -> p b j i", i=CW, j=CW),
                                  AX.X, ALU.add).then_inc(o_done, 1)

        dve.wait_ge(t_done, 1)
        if context_pairs:
            dve.wait_ge(aux_loaded, 16)
            with dve.Fori(0, CH) as h:
                diagonal = toeplitz(h)[:, 0:P]
                dve.scalar_tensor_tensor(out=diagonal, in0=ident[:, :], scalar=dcol[:, bass.ds(h, 1)], in1=diagonal,
                                         op0=ALU.mult, op1=ALU.add).then_inc(diag_done, 1)
        low(0, 0, 0)
        for h in range(2):
            low(h, h, 1)
            read_out(h, 0)
            low(h + 1, (h + 1) % 2, 0)
            read_out(h, 1)
        with dve.Fori(2, CH - 2, 2) as h:
            for k in range(2):
                low(h + k, k, 1)
                read_out(h + k, 0)
                low(h + k + 1, (k + 1) % 2, 0)
                read_out(h + k, 1)
        for h in (CH - 2, CH - 1):
            low(h, h % 2, 1)
            read_out(h, 0)
            if h < CH - 1:
                low(h + 1, (h + 1) % 2, 0)
            read_out(h, 1)
        if not context_pairs:
            dve.wait_ge(x_skipped, B)
        for pair in range(B // 2):
            dve.wait_ge(back_done, pair + 1)
            two = x[:, 2 * pair:2 * pair + 2, :]
            dve.tensor_tensor(two, two, ps_n[pair % 2][:, :].rearrange("p (b d) -> p b d", b=2), ALU.add).then_inc(added, 1)

    return (sync, tensor, scalar, gpsimd, vector), (added, B // 2)


def convolution0(core, ctx, gate):
    return convolution(core, ctx, gate, "c0_", "taps0", False)


def convolution1(core, ctx, gate):
    return convolution(core, ctx, gate, "c1_", "taps1", True)


H1, HF = 16, 16
RC = slice(2 * H1, 9 * H1)
IC = slice(9 * H1, 16 * H1)


def transforms():
    forward, inverse = np.zeros((2, D, D))
    n = np.arange(HF)
    rows = [(k, 0) for k in (0, 8, *range(1, 8))] + [(k, 1) for k in range(1, 8)]
    for r, (k, imaginary) in enumerate(rows):
        turn = 2 * np.pi * k * n / HF
        wave = -np.sin(turn) if imaginary else np.cos(turn)
        for h in range(H1):
            forward[h * HF + n, r * H1 + h] = wave * (1 if k in (0, 8) else np.sqrt(2))
            inverse[h * HF + n, r * H1 + h] = wave / HF
    return forward.astype(np.float32), inverse.astype(np.float32)


def attention1(core, ctx, gate):
    dram, x, ident = core.dram, core.x, core.ident
    tag = "a1_"
    raw = core.sbuf(ctx, tag + "raw", [P, 5, DC, D])
    raw_h = core.sbuf(ctx, tag + "raw_h", [P, 5, DC, D], F32R)
    raw_l = core.sbuf(ctx, tag + "raw_l", [P, 5, DC, D], F32R)
    w_h = core.sbuf(ctx, tag + "w_h", [P, DC, 3 * D], F32R)
    w_l = core.sbuf(ctx, tag + "w_l", [P, DC, 3 * D], F32R)
    before_f = core.sbuf(ctx, tag + "before_f", [P, P])
    before = core.sbuf(ctx, tag + "before", [P, P], F32R)
    xn = core.sbuf(ctx, tag + "xn", [P, 2, D])
    xT_h = core.sbuf(ctx, tag + "xT_h", [P, 2, D], F32R)
    xT_l = core.sbuf(ctx, tag + "xT_l", [P, 2, D], F32R)
    sq = core.sbuf(ctx, tag + "sq", [P, 2, 2 * D])
    norm2 = core.sbuf(ctx, tag + "norm2", [P, 2, 2 * H1])
    rn = core.sbuf(ctx, tag + "rn", [P, 2, 2 * H1])
    qk = core.sbuf(ctx, tag + "qk", [P, 2, 2 * D])
    k_h = core.sbuf(ctx, tag + "k_h", [P, 2, D], F32R)
    k_l = core.sbuf(ctx, tag + "k_l", [P, 2, D], F32R)
    pp = core.sbuf(ctx, tag + "pp", [P, 2, D])
    ii = core.sbuf(ctx, tag + "ii", [P, 2, 7 * H1])
    ir = core.sbuf(ctx, tag + "ir", [P, 2, 7 * H1])
    pT_h = core.sbuf(ctx, tag + "pT_h", [P, 2, D], F32R)
    pT_l = core.sbuf(ctx, tag + "pT_l", [P, 2, D], F32R)
    ps_n = core.psum(ctx, tag + "ps_n", [P, 512])
    ps_qk = [core.psum(ctx, f"{tag}ps_qk{k}", [P, 512]) for k in range(2)]
    ps_c = [core.psum(ctx, f"{tag}ps_c{k}", [P, 512]) for k in range(2)]
    ps_p = core.psum(ctx, tag + "ps_p", [P, 512])
    ps_o = core.psum(ctx, tag + "ps_o", [P, 512])
    (raw_loaded, aux_loaded, raw_hi, raw_lo, fold_done, fold_hi, fold_lo, xn_done, xt_done, xt_hi, xt_lo,
     qk_done, sq_done, norm2_done, rn_done, scaled, k_hi, k_lo, sum_done, prod_done, pp_done, pt_done,
     pt_hi, pt_lo, out_done, added, before_done) = core.sems(
        tag, "raw_loaded aux_loaded raw_hi raw_lo fold_done fold_hi fold_lo xn_done xt_done xt_hi xt_lo "
        "qk_done sq_done norm2_done rn_done scaled k_hi k_lo sum_done prod_done pp_done pt_done "
        "pt_hi pt_lo out_done added before_done")
    stats_vector, stats_gpsimd, normalise, rstd_done = row_stats(core, ctx, tag)
    folds = ((0, 2), (1, 2), (3, 4))

    def each(eng, front, back):
        front(0, 0)
        front(1, 1)
        back(0, 0)
        with eng.Fori(1, B - 2, 2) as b:
            for j in range(2):
                front(b + j + 1, j % 2)
                back(b + j, (1 + j) % 2)
        back(B - 1, 1)

    def sync(sp):
        sp.wait_ge(*gate)
        for i, name in enumerate(("L1_attn_W_q", "L1_attn_W_kv", "forward", "inverse", "L1_WoT")):
            sp.dma_start(raw[:, i, :, :], dram[name].rearrange("(c p) n -> p c n", p=P)).then_inc(raw_loaded, 16)
        sp.dma_start(before_f[:, :], dram["before"]).then_inc(aux_loaded, 16)

    def tensor(pe):
        pe.wait_ge(*gate)
        pe.wait_ge(raw_hi, 1)
        pe.wait_ge(raw_lo, 1)
        for i, (left, right) in enumerate(folds):
            for m in range(DC):
                f = i * DC + m
                if f >= 2:
                    pe.wait_ge(fold_lo, f - 1)
                for c in range(DC):
                    s = slice(m * P, (m + 1) * P)
                    last = three_pass(pe, ps_qk[f % 2][:, 0:D], (raw_h[:, left, c, s], raw_l[:, left, c, s]),
                                      (raw_h[:, right, c, :], raw_l[:, right, c, :]), c == 0, c == DC - 1)
                last.then_inc(fold_done, 1)

        def front(b, k):
            pe.wait_ge(xn_done, b + 1)
            wait_from(pe, xt_lo, b)
            for c in range(DC):
                last = pe.transpose(ps_n[:, c * P:(c + 1) * P], xn[:, k, c * P:(c + 1) * P], ident[:, :])
            last.then_inc(xt_done, 1)
            pe.wait_ge(xt_hi, b + 1)
            pe.wait_ge(xt_lo, b + 1)
            wait_from(pe, scaled, b - 1)
            for c in range(DC):
                s = slice(c * P, (c + 1) * P)
                last = three_pass(pe, ps_qk[k][:, :], (xT_h[:, k, s], xT_l[:, k, s]),
                                  (w_h[:, c, 0:2 * D], w_l[:, c, 0:2 * D]), c == 0, c == DC - 1)
            last.then_inc(qk_done, 1)

        def back(b, k):
            pe.wait_ge(k_hi, b + 1)
            pe.wait_ge(k_lo, b + 1)
            wait_from(pe, prod_done, b - 1)
            pe.matmul(ps_c[k][:, 0:D], before[:, :], k_h[:, k, :], start=True, stop=False)
            pe.matmul(ps_c[k][:, 0:D], before[:, :], k_l[:, k, :], start=False, stop=True).then_inc(sum_done, 1)
            pe.wait_ge(pp_done, b + 1)
            wait_from(pe, pt_lo, b)
            for c in range(DC):
                last = pe.transpose(ps_p[:, c * P:(c + 1) * P], pp[:, k, c * P:(c + 1) * P], ident[:, :])
            last.then_inc(pt_done, 1)
            pe.wait_ge(pt_hi, b + 1)
            pe.wait_ge(pt_lo, b + 1)
            wait_from(pe, added, b)
            for c in range(DC):
                s = slice(c * P, (c + 1) * P)
                last = three_pass(pe, ps_o[:, 0:D], (pT_h[:, k, s], pT_l[:, k, s]),
                                  (w_h[:, c, 2 * D:3 * D], w_l[:, c, 2 * D:3 * D]), c == 0, c == DC - 1)
            last.then_inc(out_done, 1)

        pe.wait_ge(fold_hi, 6)
        pe.wait_ge(fold_lo, 6)
        pe.wait_ge(before_done, 1)
        each(pe, front, back)

    def scalar(act):
        act.wait_ge(*gate)
        act.wait_ge(raw_loaded, 80)
        copy_hi(act, raw_h[:, :, :, :], raw[:, :, :, :]).then_inc(raw_hi, 1)
        act.wait_ge(aux_loaded, 16)
        copy_hi(act, before[:, :], before_f[:, :]).then_inc(before_done, 1)
        for f in range(6):
            act.wait_ge(fold_done, f + 1)
            i, m = divmod(f, DC)
            copy_hi(act, w_h[:, m, i * D:(i + 1) * D], ps_qk[f % 2][:, 0:D]).then_inc(fold_hi, 1)

        def front(b, k):
            act.wait_ge(xt_done, b + 1)
            wait_from(act, qk_done, b - 1)
            copy_hi(act, xT_h[:, k, :], ps_n[:, 0:D]).then_inc(xt_hi, 1)
            act.wait_ge(qk_done, b + 1)
            wait_from(act, norm2_done, b - 1)
            act.activation(sq[:, k, :], ps_qk[k][:, :], ACT.Square).then_inc(sq_done, 1)

        def back(b, k):
            act.wait_ge(scaled, b + 1)
            wait_from(act, sum_done, b - 1)
            copy_hi(act, k_h[:, k, :], qk[:, k, D:2 * D]).then_inc(k_hi, 1)
            act.wait_ge(pt_done, b + 1)
            wait_from(act, out_done, b - 1)
            copy_hi(act, pT_h[:, k, :], ps_p[:, 0:D]).then_inc(pt_hi, 1)

        each(act, front, back)

    def gpsimd(pool):
        stats_gpsimd(pool)
        pool.wait_ge(raw_hi, 1)
        sub_lo(pool, raw_l[:, :, :, :], raw[:, :, :, :], raw_h[:, :, :, :]).then_inc(raw_lo, 1)

        def front(b, k):
            pool.wait_ge(norm2_done, b + 1)
            wait_from(pool, scaled, b - 1)
            pool.tensor_tensor(rn[:, k, :], norm2[:, k, :], core.minus_half[:, :].to_broadcast([P, 2 * H1]),
                               ALU.pow).then_inc(rn_done, 1)

        def back(b, k):
            pool.wait_ge(k_hi, b + 1)
            wait_from(pool, sum_done, b - 1)
            sub_lo(pool, k_l[:, k, :], qk[:, k, D:2 * D], k_h[:, k, :]).then_inc(k_lo, 1)
            pool.wait_ge(prod_done, b + 1)
            pool.tensor_tensor(pp[:, k, RC], pp[:, k, RC], ii[:, k, :], ALU.subtract)
            pool.tensor_tensor(pp[:, k, IC], pp[:, k, IC], ir[:, k, :], ALU.add).then_inc(pp_done, 1)

        each(pool, front, back)

    def vector(dve):
        dve.wait_ge(*gate)
        stats_vector(dve)
        for f in range(6):
            dve.wait_ge(fold_hi, f + 1)
            i, m = divmod(f, DC)
            cols = slice(i * D, (i + 1) * D)
            sub_lo(dve, w_l[:, m, cols], ps_qk[f % 2][:, 0:D], w_h[:, m, cols]).then_inc(fold_lo, 1)
        dve.wait_ge(rstd_done, 1)

        def front(b, k):
            wait_from(dve, xt_done, b - 1)
            normalise(dve, xn[:, k, :], b).then_inc(xn_done, 1)
            dve.wait_ge(xt_hi, b + 1)
            wait_from(dve, qk_done, b - 1)
            sub_lo(dve, xT_l[:, k, :], ps_n[:, 0:D], xT_h[:, k, :]).then_inc(xt_lo, 1)
            dve.wait_ge(sq_done, b + 1)
            wait_from(dve, rn_done, b - 1)
            dve.tensor_reduce(norm2[:, k, :].rearrange("p (a h) -> p a h", a=2),
                              sq[:, k, :].rearrange("p (a f h) -> p a h f", a=2, h=H1), AX.X,
                              ALU.add).then_inc(norm2_done, 1)

        def back(b, k):
            dve.wait_ge(rn_done, b + 1)
            wait_from(dve, pp_done, b - 1)
            scale = rn[:, k, :].rearrange("p (a h) -> p a h", a=2).unsqueeze(2).to_broadcast([P, 2, HF, H1])
            dve.tensor_tensor(qk[:, k, :].rearrange("p (a f h) -> p a f h", a=2, h=H1),
                              ps_qk[k][:, :].rearrange("p (a f h) -> p a f h", a=2, h=H1), scale,
                              ALU.mult).then_inc(scaled, 1)
            dve.wait_ge(sum_done, b + 1)
            wait_from(dve, pt_done, b - 1)
            c, q, both = ps_c[k], qk[:, k, :], slice(0, 9 * H1)
            dve.tensor_tensor(pp[:, k, both], q[:, both], c[:, both], ALU.mult)
            dve.tensor_tensor(ii[:, k, :], q[:, IC], c[:, IC], ALU.mult)
            dve.tensor_tensor(pp[:, k, IC], q[:, RC], c[:, IC], ALU.mult)
            dve.tensor_tensor(ir[:, k, :], q[:, IC], c[:, RC], ALU.mult).then_inc(prod_done, 1)
            dve.wait_ge(pt_hi, b + 1)
            wait_from(dve, out_done, b - 1)
            sub_lo(dve, pT_l[:, k, :], ps_p[:, 0:D], pT_h[:, k, :]).then_inc(pt_lo, 1)
            dve.wait_ge(out_done, b + 1)
            dve.tensor_tensor(core.tile(b), core.tile(b), ps_o[:, 0:D], ALU.add).then_inc(added, 1)

        each(dve, front, back)

    return (sync, tensor, scalar, gpsimd, vector), (added, B)


GT = 512
NG = B * S // GT


class Layer0:
    tag, experts, top, slots, chunks = "f0_", 16, 6, 9, (128, 128, 96)
    biased, limit, cells = True, None, 2 * 16 + 1
    names = dict(router="L0_routerT", in_="L0_in", out="L0_out", pick="pick0")


class Layer1:
    tag, experts, top, slots, chunks = "f1_", 8, 2, 8, (128, 128)
    biased, limit, cells = False, 7.0, 2 * 8
    names = dict(router="L1_ffn_Wr", in_="L1_in", out="L1_out", pick="pick1")


def pick(cfg):
    hidden = sum(cfg.chunks)
    per = hidden * cfg.slots // (cfg.experts + (2 if cfg.biased else 0))
    table = np.zeros((cfg.cells, cfg.slots, hidden), np.float32)
    for s in range(cfg.slots):
        for r in range(hidden):
            e = (s * hidden + r) // per
            if e < cfg.experts:
                table[e, s, r] = table[cfg.experts + e, s, r] = 1.0
            else:
                table[2 * cfg.experts, s, r] = 1.0
    return table


def expert_layer(core, ctx, gate, cfg):
    dram, x, ident, tag = core.dram, core.x, core.ident, cfg.tag
    E, NS, NC, hidden, cells = cfg.experts, cfg.slots, len(cfg.chunks), sum(cfg.chunks), cfg.cells
    UNITS = NG * NC
    xT_h = core.sbuf(ctx, tag + "xT_h", [P, DC, B * S], F32R)
    xT_l = core.sbuf(ctx, tag + "xT_l", [P, DC, B * S], F32R)
    xn = core.sbuf(ctx, tag + "xn", [P, 2, D])
    in_raw = core.sbuf(ctx, tag + "in_raw", [P, DC, 2 * hidden])
    out_raw = core.sbuf(ctx, tag + "out_raw", [P, NC, D])
    pick_raw = core.sbuf(ctx, tag + "pick_raw", [cells, hidden])
    in_h = core.sbuf(ctx, tag + "in_h", [P, 2, DC, 2 * hidden], F32R)
    in_l = core.sbuf(ctx, tag + "in_l", [P, 2, DC, 2 * hidden], F32R)
    out_h = core.sbuf(ctx, tag + "out_h", [P, 2, NC, D], F32R)
    out_l = core.sbuf(ctx, tag + "out_l", [P, 2, NC, D], F32R)
    picked = core.sbuf(ctx, tag + "picked", [cells, 2, hidden], F32R)
    r_raw = core.sbuf(ctx, tag + "r_raw", [P, DC, E])
    r_h = core.sbuf(ctx, tag + "r_h", [P, DC, E], F32R)
    r_l = core.sbuf(ctx, tag + "r_l", [P, DC, E], F32R)
    logitsT = core.sbuf(ctx, tag + "logitsT", [E, B * S])
    table = [P, B, E]
    logits, ex, prob, key, above, equal, run0, run1 = (core.sbuf(ctx, tag + n, table) for n in (
        "logits", "ex", "prob", "key", "above", "equal", "run0", "run1"))
    eight = core.sbuf(ctx, tag + "eight", [P, B, 8])
    row = core.sbuf(ctx, tag + "row", [P, B])
    row2 = core.sbuf(ctx, tag + "row2", [P, B])
    c_h = core.sbuf(ctx, tag + "c_h", table, F32R)
    cell = core.sbuf(ctx, tag + "cell", [P, B, cells])
    cellT = core.sbuf(ctx, tag + "cellT", [cells, B * S], F32R)
    s = core.sbuf(ctx, tag + "s", [P, 2, GT])
    m = core.sbuf(ctx, tag + "m", [P, 2, GT])
    h = core.sbuf(ctx, tag + "h", [P, 2, GT])
    h_h = core.sbuf(ctx, tag + "h_h", [P, 2, GT], F32R)
    h_l = core.sbuf(ctx, tag + "h_l", [P, 2, GT], F32R)
    if cfg.biased:
        bias_raw = core.sbuf(ctx, tag + "bias_raw", [P, 2, NC])
        bias = core.sbuf(ctx, tag + "bias", [P, 2, 2, NC])
        b2_raw = core.sbuf(ctx, tag + "b2_raw", [cells, D])
        b2_h = core.sbuf(ctx, tag + "b2_h", [cells, D], F32R)
        b2_l = core.sbuf(ctx, tag + "b2_l", [cells, D], F32R)
        router_b = core.sbuf(ctx, tag + "router_b", [P, E])
    ps_a, ps_u, ps_c, ps_y = ([core.psum(ctx, f"{tag}ps_{n}{k}", [P, 512]) for k in range(2)] for n in "aucy")
    (w0_loaded, w1_loaded, aux_loaded, router_hi, router_lo, b2_hi, b2_lo, xn_done, xt_done, xt_hi, xt_lo,
     logits_done, logits_copied, turned, exp_in, exp_done, routed, step, cell_done, cellT_done, bias_done,
     bias_added, w_hi, w_lo, in_done, silu_done, clipped, gated, h_done, h_hi, h_lo, out_done, added) = core.layer_sems(
        "f_", "w0_loaded w1_loaded aux_loaded router_hi router_lo b2_hi b2_lo xn_done xt_done xt_hi xt_lo "
        "logits_done logits_copied turned exp_in exp_done routed step cell_done cellT_done bias_done "
        "bias_added w_hi w_lo in_done silu_done clipped gated h_done h_hi h_lo out_done added")
    w_loaded = (w0_loaded, w1_loaded)
    aux = 16 * (3 if cfg.biased else 1)
    slot_loads = 16 * (4 if cfg.biased else 3)
    stats_vector, stats_gpsimd, normalise, rstd_done = row_stats(core, ctx, tag)
    enter, clear = core.start(gate)

    def tiles(eng, turn):
        for k in range(2):
            turn(k, k)
        with eng.Fori(2, B - 1, 2) as b:
            for k in range(2):
                turn(b + k, k)

    def each_slot(eng, slot):
        slot(0, 0, True)
        slot(1, 1, True)
        rest = NS - 1 if NS % 2 else NS - 2
        with eng.Fori(2, rest - 1, 2) as t:
            slot(t, 0, True)
            slot(t + 1, 1, True)
        for t in range(rest, NS):
            slot(t, t % 2, t < NS - 1)

    def units():
        return [(g, c, (g * NC + c) % 2) for g in range(NG) for c in range(NC)]

    def sync(sp):
        enter(sp)
        sp.dma_start(r_raw[:, :, :], dram[cfg.names["router"]].rearrange("(c p) e -> p c e", p=P)).then_inc(aux_loaded, 16)
        if cfg.biased:
            gb = dram["L0_ffn_gate_b"]
            sp.dma_start(router_b[:, :], bass.AP(gb.tensor, 0, [[0, P], [1, E]])).then_inc(aux_loaded, 16)
            sp.dma_start(b2_raw[:, :], dram["L0_b2"]).then_inc(aux_loaded, 16)

        def slot(t, k, more):
            wait_from(sp, w_lo, t)
            one = bass.ds(t, 1)
            sp.dma_start(in_raw[:, :, :], dram[cfg.names["in_"]][one].rearrange("a p c n -> p (a c) n")).then_inc(w_loaded[k], 16)
            sp.dma_start(out_raw[:, :, :], dram[cfg.names["out"]][one].rearrange("a p c n -> p (a c) n")).then_inc(w_loaded[k], 16)
            sp.dma_start(pick_raw[:, :], dram[cfg.names["pick"]][:, one, :].rearrange("e a r -> e (a r)")).then_inc(w_loaded[k], 16)
            if cfg.biased:
                sp.dma_start(bias_raw[:, :, :], dram["L0_b13"][one].rearrange("a p w c -> p (a w) c")).then_inc(w_loaded[k], 16)

        each_slot(sp, slot)

    def tensor(pe):
        enter(pe)

        def turn(b, k):
            pe.wait_ge(xn_done, b + 1)
            wait_from(pe, xt_lo, b - 1)
            for c in range(DC):
                last = pe.transpose(ps_a[k][:, c * P:(c + 1) * P], xn[:, k, c * P:(c + 1) * P], ident[:, :])
            last.then_inc(xt_done, 1)

        tiles(pe, turn)
        pe.wait_ge(router_hi, 1)
        pe.wait_ge(router_lo, 1)
        for g in range(NG):
            cols = slice(g * GT, (g + 1) * GT)
            pe.wait_ge(xt_hi, 4 * g + 4)
            pe.wait_ge(xt_lo, 4 * g + 4)
            if g >= 2:
                pe.wait_ge(logits_copied, g - 1)
            for c in range(DC):
                last = three_pass(pe, ps_u[g % 2][0:E, :], (r_h[:, c, :], r_l[:, c, :]),
                                  (xT_h[:, c, cols], xT_l[:, c, cols]), c == 0, c == DC - 1)
            last.then_inc(logits_done, 1)
        pe.wait_ge(logits_copied, NG)
        for b in range(B):
            last = pe.transpose(ps_c[0][:, b * E:(b + 1) * E], logitsT[:, b * S:(b + 1) * S], ident[0:E, 0:E])
        last.then_inc(turned, 1)
        pe.wait_ge(cell_done, 1)
        for b in range(B):
            g = b // 4
            if b % 4 == 0 and g >= 2:
                pe.wait_ge(cellT_done, g - 1)
            last = pe.transpose(ps_u[g % 2][0:cells, b % 4 * S:(b % 4 + 1) * S], cell[:, b, :], ident[:, :])
            if b % 4 == 3:
                last.then_inc(turned, 1)
        if cfg.biased:
            pe.wait_ge(b2_hi, 1)
            pe.wait_ge(b2_lo, 1)
            for b in range(B):
                pair = b // 2
                if b % 2 == 0:
                    pe.wait_ge(cellT_done, b // 4 + 1)
                    if pair >= 2:
                        pe.wait_ge(bias_added, pair - 1)
                for w in (b2_h, b2_l):
                    last = pe.matmul(ps_y[pair % 2][:, b % 2 * D:(b % 2 + 1) * D], cellT[:, b * S:(b + 1) * S], w[:, :],
                                     start=b % 2 == 0 and w is b2_h, stop=b % 2 == 1 and w is b2_l,
                                     skip_group_check=True)
                if b % 2:
                    last.then_inc(bias_done, 1)
        pe.wait_ge(cellT_done, NG)
        if cfg.biased:
            pe.wait_ge(bias_added, B // 2)

        def hidden_sums(t, k, n, g, c, q):
            if (g, c) == (0, 0):
                pe.wait_ge(w_hi, t + 1)
                pe.wait_ge(w_lo, t + 1)
            wait_from(pe, silu_done, n - 1)
            wait_from(pe, gated, n - 1)
            wait_from(pe, h_done, n - 1)
            R, cols = cfg.chunks[c], slice(g * GT, (g + 1) * GT)
            for dst, first in ((ps_a, 0), (ps_u, hidden)):
                rows = slice(first + c * P, first + c * P + R)
                for d in range(DC):
                    three_pass(pe, dst[q][0:R, :], (in_h[:, k, d, rows], in_l[:, k, d, rows]),
                               (xT_h[:, d, cols], xT_l[:, d, cols]), d == 0, d == DC - 1)
            pe.matmul(ps_c[q][0:R, :], picked[:, k, c * P:c * P + R], cellT[:, cols], start=True,
                      stop=True).then_inc(in_done, 1)

        def output_sums(t, k, n, g, c, q):
            pe.wait_ge(h_hi, n + 1)
            pe.wait_ge(h_lo, n + 1)
            if c == 0:
                wait_from(pe, added, NG * t + g)
            R = cfg.chunks[c]
            for b in range(4):
                s4, out = slice(b * S, (b + 1) * S), ps_y[b // 2][:, b % 2 * D:(b % 2 + 1) * D]
                passes = ((h_h, out_h), (h_h, out_l), (h_l, out_h))
                for i, (a, w) in enumerate(passes):
                    last = pe.matmul(out, a[0:R, q, s4], w[0:R, k, c, :],
                                     start=c == 0 and b % 2 == 0 and i == 0,
                                     stop=c == NC - 1 and b % 2 == 1 and i == 2, skip_group_check=True)
            last.then_inc(out_done, 1)

        def slot(t, k, more):
            todo = units()
            for i, (g, c, q) in enumerate(todo):
                n, ahead = UNITS * t + i, i + 2
                if ahead < UNITS:
                    hidden_sums(t, k, n + 2, *todo[ahead])
                elif more:
                    hidden_sums(t + 1, 1 - k, n + 2, *todo[ahead - UNITS])
                output_sums(t, k, n, g, c, q)

        for i in range(2):
            hidden_sums(0, 0, i, *units()[i])
        each_slot(pe, slot)

    def split_hi(act, t, k):
        act.wait_ge(w_loaded[k], slot_loads // 2 * (t - k) + slot_loads)
        wait_from(act, out_done, UNITS * (t - 1))
        copy_hi(act, in_h[:, k, :, :], in_raw[:, :, :])
        copy_hi(act, out_h[:, k, :, :], out_raw[:, :, :])
        if cfg.biased:
            act.activation(bias[:, k, :, :], bias_raw[:, :, :], ACT.Copy)
        copy_hi(act, picked[:, k, :], pick_raw[:, :]).then_inc(w_hi, 1)

    def scalar(act):
        enter(act)
        act.wait_ge(aux_loaded, aux)
        copy_hi(act, r_h[:, :, :], r_raw[:, :, :]).then_inc(router_hi, 1)
        if cfg.biased:
            copy_hi(act, b2_h[:, :], b2_raw[:, :]).then_inc(b2_hi, 1)

        def turn(b, k):
            act.wait_ge(xt_done, b + 1)
            copy_hi(act, xT_h[:, :, bass.ds(b * S, S)], ps_a[k][:, 0:D].rearrange("p (c s) -> p c s", c=DC)).then_inc(xt_hi, 1)

        tiles(act, turn)
        split_hi(act, 0, 0)
        for g in range(NG):
            act.wait_ge(logits_done, g + 1)
            act.activation(logitsT[:, g * GT:(g + 1) * GT], ps_u[g % 2][0:E, :], ACT.Copy).then_inc(logits_copied, 1)
        act.wait_ge(exp_in, 1)
        act.activation(ex[:, :, :], ex[:, :, :], ACT.Exp).then_inc(exp_done, 1)
        for g in range(NG):
            act.wait_ge(turned, g + 2)
            copy_hi(act, cellT[:, g * GT:(g + 1) * GT], ps_u[g % 2][0:cells, :]).then_inc(cellT_done, 1)

        def silu(k, n, g, c, q):
            act.wait_ge(in_done, n + 1)
            wait_from(act, gated, n - 1)
            R = cfg.chunks[c]
            offset = dict(bias=bias[0:R, k, 0, c:c + 1]) if cfg.biased else {}
            act.activation(s[0:R, q, :], ps_a[q][0:R, :], ACT.Silu, **offset).then_inc(silu_done, 1)

        def slot(t, k, more):
            todo = units()
            for i, (g, c, q) in enumerate(todo):
                n = UNITS * t + i
                if i + 1 < UNITS:
                    silu(k, n + 1, *todo[i + 1])
                elif more:
                    silu(1 - k, n + 1, *todo[0])
                act.wait_ge(h_done, n + 1)
                wait_from(act, out_done, n - 1)
                R = cfg.chunks[c]
                copy_hi(act, h_h[0:R, q, :], h[0:R, q, :]).then_inc(h_hi, 1)
                if i == 2 and more:
                    split_hi(act, t + 1, 1 - k)

        silu(0, 0, 0, 0, 0)
        each_slot(act, slot)

    def gpsimd(pool):
        clear(pool)
        enter(pool)
        stats_gpsimd(pool)
        pool.wait_ge(router_hi, 1)
        sub_lo(pool, r_l[:, :, :], r_raw[:, :, :], r_h[:, :, :]).then_inc(router_lo, 1)
        if cfg.biased:
            pool.wait_ge(b2_hi, 1)
            sub_lo(pool, b2_l[:, :], b2_raw[:, :], b2_h[:, :]).then_inc(b2_lo, 1)

        def split_lo(t, k):
            pool.wait_ge(w_hi, t + 1)
            sub_lo(pool, in_l[:, k, :, :], in_raw[:, :, :], in_h[:, k, :, :])
            sub_lo(pool, out_l[:, k, :, :], out_raw[:, :, :], out_h[:, k, :, :]).then_inc(w_lo, 1)

        split_lo(0, 0)

        def slot(t, k, more):
            for i, (g, c, q) in enumerate(units()):
                n = UNITS * t + i
                pool.wait_ge(h_hi, n + 1)
                wait_from(pool, out_done, n - 1)
                R = cfg.chunks[c]
                sub_lo(pool, h_l[0:R, q, :], h[0:R, q, :], h_h[0:R, q, :]).then_inc(h_lo, 1)
                if i == 2 and more:
                    split_lo(t + 1, 1 - k)

        each_slot(pool, slot)

    def vector(dve):
        enter(dve)
        stats_vector(dve)
        dve.wait_ge(rstd_done, 1)

        def turn(b, k):
            wait_from(dve, xt_done, b - 1)
            normalise(dve, xn[:, k, :], b).then_inc(xn_done, 1)
            dve.wait_ge(xt_hi, b + 1)
            to = xT_l[:, :, bass.ds(b * S, S)]
            sub_lo(dve, to, ps_a[k][:, 0:D].rearrange("p (c s) -> p c s", c=DC), xT_h[:, :, bass.ds(b * S, S)]).then_inc(xt_lo, 1)

        tiles(dve, turn)

        done = [0]

        def chain(ins):
            done[0] += 1
            ins.then_inc(step, 1)
            dve.wait_ge(step, done[0])

        def wide(v, n=E):
            return v.unsqueeze(2).to_broadcast([P, B, n])

        def choose(values):
            for b in range(B):
                last = dve.max(eight[:, b, :], values[:, b, :])
            chain(last)
            least = wide(eight[:, :, cfg.top - 1])
            dve.tensor_tensor(equal[:, :, :], values[:, :, :], least, ALU.is_equal)
            chain(dve.tensor_tensor(above[:, :, :], values[:, :, :], least, ALU.is_gt))
            chain(dve.tensor_reduce(row[:, :], above[:, :, :], AX.X, ALU.add))
            chain(dve.tensor_scalar(row[:, :], row[:, :], -1.0, float(cfg.top), ALU.mult, ALU.add))
            src, shift, spare = equal, 1, [run0, run1]
            while shift < E:
                dst = spare[0]
                dve.tensor_copy(dst[:, :, 0:shift], src[:, :, 0:shift])
                chain(dve.tensor_tensor(dst[:, :, shift:E], src[:, :, shift:E], src[:, :, 0:E - shift], ALU.add))
                src, spare, shift = dst, spare[::-1], 2 * shift
            dst = spare[0]
            chain(dve.tensor_tensor(dst[:, :, :], src[:, :, :], wide(row[:, :]), ALU.is_le))
            chain(dve.tensor_tensor(dst[:, :, :], dst[:, :, :], equal[:, :, :], ALU.mult))
            chain(dve.tensor_tensor(above[:, :, :], above[:, :, :], dst[:, :, :], ALU.add))

        dve.wait_ge(turned, 1)
        chain(dve.tensor_copy(logits[:, :, :], ps_c[0][:, 0:B * E].rearrange("p (b e) -> p b e", e=E)))
        chain(dve.tensor_reduce(row2[:, :], logits[:, :, :], AX.X, ALU.max))
        dve.tensor_tensor(ex[:, :, :], logits[:, :, :], wide(row2[:, :]), ALU.subtract).then_inc(exp_in, 1)
        if not cfg.biased:
            choose(logits)
        dve.wait_ge(exp_done, 1)
        if not cfg.biased:
            chain(dve.tensor_tensor(ex[:, :, :], ex[:, :, :], above[:, :, :], ALU.mult))
        chain(dve.tensor_reduce(row2[:, :], ex[:, :, :], AX.X, ALU.add))
        chain(dve.reciprocal(row2[:, :], row2[:, :]))
        chain(dve.tensor_tensor(prob[:, :, :], ex[:, :, :], wide(row2[:, :]), ALU.mult))
        if cfg.biased:
            dve.wait_ge(aux_loaded, aux)
            chain(dve.tensor_tensor(key[:, :, :], prob[:, :, :], router_b[:, :].unsqueeze(1).to_broadcast(table), ALU.add))
            choose(key)
            chain(dve.tensor_tensor(prob[:, :, :], prob[:, :, :], above[:, :, :], ALU.mult))
        chain(dve.tensor_copy(c_h[:, :, :], prob[:, :, :]))
        dve.tensor_copy(cell[:, :, 0:E], c_h[:, :, :].bitcast(F32))
        if cfg.biased:
            dve.memset(cell[:, :, 2 * E:cells], 1.0)
        dve.tensor_tensor(cell[:, :, E:2 * E], prob[:, :, :], c_h[:, :, :].bitcast(F32), ALU.subtract).then_inc(cell_done, 1)
        if cfg.biased:
            for pair in range(B // 2):
                dve.wait_ge(bias_done, pair + 1)
                two = x[:, 2 * pair:2 * pair + 2, :]
                dve.tensor_tensor(two, two, ps_y[pair % 2][:, :].rearrange("p (b d) -> p b d", b=2), ALU.add).then_inc(bias_added, 1)
            dve.wait_ge(bias_added, B // 2)

        def gate_unit(k, n, g, c, q):
            R = cfg.chunks[c]
            dve.wait_ge(silu_done, n + 1)
            if cfg.limit is not None:
                dve.tensor_scalar(s[0:R, q, :], s[0:R, q, :], -cfg.limit, cfg.limit, ALU.max, ALU.min).then_inc(clipped, 1)
                dve.wait_ge(clipped, n + 1)
                dve.tensor_tensor(m[0:R, q, :], ps_u[q][0:R, :], s[0:R, q, :], ALU.mult).then_inc(gated, 1)
            else:
                dve.scalar_tensor_tensor(out=m[0:R, q, :], in0=ps_u[q][0:R, :], scalar=bias[0:R, k, 1, c:c + 1],
                                         in1=s[0:R, q, :], op0=ALU.add, op1=ALU.mult).then_inc(gated, 1)
            dve.wait_ge(gated, n + 1)
            wait_from(dve, h_lo, n - 1)
            dve.tensor_tensor(h[0:R, q, :], m[0:R, q, :], ps_c[q][0:R, :], ALU.mult).then_inc(h_done, 1)

        def add_group(t, g):
            dve.wait_ge(out_done, UNITS * t + NC * (g + 1))
            for j in range(2):
                two = x[:, 4 * g + 2 * j:4 * g + 2 * j + 2, :]
                last = dve.tensor_tensor(two, two, ps_y[j][:, :].rearrange("p (b d) -> p b d", b=2), ALU.add)
            last.then_inc(added, 1)

        def slot(t, k, more):
            for i, (g, c, q) in enumerate(units()):
                gate_unit(k, UNITS * t + i, g, c, q)
                if c == 0:
                    if g > 0:
                        add_group(t, g - 1)
                    elif not (isinstance(t, int) and t == 0):
                        add_group(t - 1, NG - 1)

        each_slot(dve, slot)
        add_group(NS - 1, NG - 1)

    return (sync, tensor, scalar, gpsimd, vector), (added, NG * NS)


def experts0(core, ctx, gate):
    return expert_layer(core, ctx, gate, Layer0)


def experts1(core, ctx, gate):
    return expert_layer(core, ctx, gate, Layer1)


PHASES = (attention0, convolution0, experts0, attention1, convolution1, experts1,)


def build(nc, dram, out):
    with ExitStack() as stack:
        core = Core(nc, stack, dram)
        programs, gate = [], None
        for phase in PHASES:
            with ExitStack() as ctx:
                engines, done = phase(core, ctx) if gate is None else phase(core, ctx, gate)
            programs.append(engines)
            gate = done

        with nc.Block() as block:
            @block.sync
            def _(sp):
                for sync, _, _, _, _ in programs:
                    sync(sp)
                sp.wait_ge(*gate)
                sp.dma_start(out.rearrange("b s d -> s b d"), core.x[:, :, :]).then_inc(core.stored, 16)
                sp.wait_ge(core.stored, 16)

            @block.tensor
            def _(pe):
                for _, tensor, _, _, _ in programs:
                    tensor(pe)

            @block.scalar
            def _(act):
                for _, _, scalar, _, _ in programs:
                    scalar(act)

            @block.gpsimd
            def _(pool):
                for _, _, _, gpsimd, _ in programs:
                    gpsimd(pool)

            @block.vector
            def _(dve):
                for _, _, _, _, vector in programs:
                    vector(dve)


def lay_out(inputs):
    a = {k: np.asarray(v) for k, v in inputs.items()}
    out = {k: a[k] for k in ("x", "ctx_2048", "fside_S2_0", "L0_attn_Wq", "L0_attn_Wk", "L0_attn_Wv", "L0_attn_Wo",
                             "L1_xattn_D", "L1_attn_W_q", "L1_attn_W_kv", "L0_ffn_gate_b", "L1_ffn_Wr")}
    out["ctxT"] = a["ctx_2048"].reshape(B * S, D).T
    out["L1_WoT"] = a["L1_attn_W_o"].T
    for name, taps in (("taps0", a["L0_xattn_k"]), ("taps1", a["L1_xattn_ssm_kernel"])):
        padded = np.zeros((CH, 2 * D), np.float32)
        padded[:, D:] = taps
        out[name] = padded[:, ::-1]

    def hidden_first(w):
        return w.reshape(-1, w.shape[0] // NS, DC, P).transpose(0, 3, 2, 1)

    def by_chunk(v, cfg):
        NC, n = len(cfg.chunks), sum(cfg.chunks)
        full = np.zeros((cfg.slots, NC * P) + v.shape[1:], np.float32)
        full[:, :n] = v.reshape((cfg.slots, n) + v.shape[1:])
        full = full.reshape((cfg.slots, NC, P) + v.shape[1:])
        return np.moveaxis(full, 2, 1)

    NS = Layer0.slots
    w1, w3 = (np.concatenate([a["L0_ffn_" + n].reshape(-1, D), a["L0_ffn_ws" + n[1]]]) for n in ("w1", "w3"))
    w2 = np.concatenate([a["L0_ffn_w2"].transpose(0, 2, 1).reshape(-1, D), a["L0_ffn_ws2"].T])
    out["L0_in"] = np.concatenate([hidden_first(w1), hidden_first(w3)], -1)
    out["L0_out"] = by_chunk(w2, Layer0)
    out["L0_b13"] = np.stack([by_chunk(np.concatenate([a["L0_ffn_b" + n].reshape(-1), a["L0_ffn_bs" + n]]), Layer0)
                              for n in "13"], 2)
    out["L0_b2"] = np.concatenate([a["L0_ffn_b2"], a["L0_ffn_b2"], a["L0_ffn_bs2"][None]])
    out["L0_routerT"] = a["L0_ffn_gate_w"].T
    NS = Layer1.slots
    inputs1 = [a["L1_ffn_" + n].reshape(NS, DC, P, -1).transpose(0, 2, 1, 3) for n in ("Wg", "Wu")]
    out["L1_in"] = np.concatenate(inputs1, -1)
    out["L1_out"] = by_chunk(a["L1_ffn_Wd"].reshape(-1, D), Layer1)
    return out


def kernel(**inputs):
    import concourse.bacc as bacc
    from concourse.bass_utils import run_bass_kernel_spmd

    nc = bacc.Bacc("TRN2", target_bir_lowering=False, num_devices=1)
    arrays, dram = {}, {}
    for name, a in {**lay_out(inputs), **constants()}.items():
        a = np.ascontiguousarray(a)
        arrays["in_" + name] = a
        dram[name] = nc.dram_tensor("in_" + name, a.shape, mybir.dt.from_np(a.dtype), kind="ExternalInput").ap()
    out = nc.dram_tensor("out_x", (B, S, D), F32, kind="ExternalOutput").ap()
    build(nc, dram, out)
    r = run_bass_kernel_spmd(nc, [arrays], core_ids=[0])
    return r.results[0]["out_x"]
```

```python
from contextlib import ExitStack

import numpy as np
import concourse.bass as bass
from concourse import mybir

F32 = mybir.dt.float32
F32R = mybir.dt.float32r
BF16 = mybir.dt.bfloat16
ALU = mybir.AluOpType
ACT = mybir.ActivationFunctionType
AX = mybir.AxisListType

P = 128
B = 16
S = 128
D = 256
DC = D // P
EPS = 1e-5

HEADS, KV, HD = 16, 4, 128
REP = HEADS // KV
GQ = REP * HD
GC = GQ + 2 * HD
MASKED = -1e30


def three_pass(pe, out, lhs, rhs, start, stop):
    (lh, ll), (rh, rl) = lhs, rhs
    pe.matmul(out, lh, rh, start=start, stop=False)
    pe.matmul(out, lh, rl, start=False, stop=False)
    return pe.matmul(out, ll, rh, start=False, stop=stop)


def wait_from(eng, semaphore, count):
    if not isinstance(count, int) or count > 0:
        eng.wait_ge(semaphore, count)


def copy_hi(act, dst, src):
    return act.activation(dst, src, ACT.Copy)


def sub_lo(eng, dst, src, hi):
    return eng.tensor_tensor(dst, src, hi.bitcast(F32), ALU.subtract)


class Core:

    def __init__(self, nc, stack, dram):
        self.nc, self.stack, self.dram = nc, stack, dram
        self.x = self.sbuf(stack, "x", [P, B, D])
        self.ctxT = self.sbuf(stack, "ctxT_sb", [P, DC, B * S])
        self.ident = self.sbuf(stack, "ident_sb", [P, P])
        self.mark = self.sbuf(stack, "mark", [P, 1])
        self.kinds, self.used_again = {}, []
        self.minus_half = self.sbuf(stack, "minus_half", [P, 1])
        (self.x0_loaded, self.x_loaded, self.const_loaded, self.ctx_loaded, self.half_set,
         self.stored) = self.sems("", "x0_loaded x_loaded const_loaded ctx_loaded half_set stored")

    def sems(self, tag, names):
        return [self.stack.enter_context(self.nc.semaphore(tag + n)) for n in names.split()]

    def layer_sems(self, kind, names):
        if (kind, names) in self.kinds:
            self.used_again += self.kinds[kind, names]
        else:
            self.kinds[kind, names] = self.sems(kind, names)
        return self.kinds[kind, names]

    def start(self, gate):
        again, self.used_again = self.used_again, []
        if not again:
            return lambda eng: eng.wait_ge(*gate), lambda pool: None
        cleared, entered = self.sems(f"{len(again)}_", "cleared entered")

        def clear(pool):
            pool.wait_ge(*gate)
            for s in again:
                pool.sem_clear(s)
            pool.memset(self.mark[:, :], 0.0).then_inc(cleared, 1)

        def enter(eng):
            eng.wait_ge(cleared, 1)
            eng.sem_inc(entered, 1)

        return enter, clear

    def sbuf(self, ctx, name, shape, dt=F32):
        return ctx.enter_context(self.nc.sbuf_tensor(name, shape, dt))

    def psum(self, ctx, name, shape, dt=F32):
        return ctx.enter_context(self.nc.psum_tensor(name, shape, dt))

    def tile(self, b):
        return self.x[:, bass.ds(b, 1), :].rearrange("p a d -> p (a d)")


def pipeline(eng, stages):
    deepest = max(lag for lag, _ in stages)
    first = min(lag for lag, _ in stages)

    start = deepest + 2
    loops = max(0, (B + first - start) // 2)
    for s in range(first, start):
        for lag, stage in stages:
            if 0 <= s - lag < B:
                stage(s - lag, (s - lag) % 2)
    if loops:
        with eng.Fori(start, start + 2 * loops - 1, 2) as s:
            for j in range(2):
                for lag, stage in stages:
                    stage(s + (j - lag), (start + j - lag) % 2)
    for s in range(start + 2 * loops, B + deepest):
        for lag, stage in stages:
            if 0 <= s - lag < B:
                stage(s - lag, (s - lag) % 2)


def constants():
    half = HD // 2
    inv = (1.0 / 10000.0 ** (np.arange(half, dtype=np.float64) / half))
    ang = np.outer(np.arange(S), inv)
    cos = np.concatenate([np.cos(ang)] * 2, -1)
    sin = np.concatenate([-np.sin(ang), np.sin(ang)], -1)
    s = (np.arange(S) + 32.0) / 64.0
    xs = np.where(np.arange(HD) % 2 == 0, s[:, None], 1.0 / s[:, None])
    q = xs / np.sqrt(HD)
    rope = np.concatenate([cos * q, sin * q, cos / xs, sin / xs], -1)
    mask = np.where(np.arange(S)[None, :] > np.arange(S)[:, None], MASKED, 0.0)
    forward, inverse = transforms()
    return {
        "forward": forward,
        "inverse": inverse,
        "before": np.triu(np.ones((S, S), np.float32)),
        "pick0": pick(Layer0),
        "pick1": pick(Layer1),
        "same_head": np.kron(np.eye(S // 8), np.ones((8, 8))).astype(np.float32),
        "ident": np.eye(P, dtype=np.float32),
        "rope": rope.astype(np.float32),
        "mask": mask.astype(np.float32),
    }


def attention0(core, ctx):
    dram, x, ident, minus_half = core.dram, core.x, core.ident, core.minus_half
    x0_loaded, x_loaded, const_loaded, half_set = core.x0_loaded, core.x_loaded, core.const_loaded, core.half_set
    w_h = core.sbuf(ctx, "a0_w_h", [P, DC, KV, GC], F32R)
    w_l = core.sbuf(ctx, "a0_w_l", [P, DC, KV, GC], F32R)
    wo_h = core.sbuf(ctx, "a0_wo_h", [P, HEADS, D], F32R)
    wo_l = core.sbuf(ctx, "a0_wo_l", [P, HEADS, D], F32R)
    w_raw = core.sbuf(ctx, "a0_w_raw", [P, 2, DC, GC])
    wo_raw = core.sbuf(ctx, "a0_wo_raw", [P, 2, REP, D])
    rope = core.sbuf(ctx, "a0_rope", [P, 4, HD])
    mask_f = core.sbuf(ctx, "a0_mask_f", [P, S])
    mask = core.sbuf(ctx, "a0_mask", [P, S], BF16)
    ident_b = core.sbuf(ctx, "a0_ident_b", [P, P], BF16)
    stats = core.sbuf(ctx, "a0_stats", [P, 6])
    mv = core.sbuf(ctx, "a0_mv", [P, 2])
    vare = core.sbuf(ctx, "a0_vare", [P, 1])
    rstd = core.sbuf(ctx, "a0_rstd", [P, 1])
    xn = core.sbuf(ctx, "a0_xn", [P, D])
    xT_h = core.sbuf(ctx, "a0_xT_h", [P, DC, P], F32R)
    xT_l = core.sbuf(ctx, "a0_xT_l", [P, DC, P], F32R)
    rc = core.sbuf(ctx, "a0_rc", [P, GQ + HD])
    rs = core.sbuf(ctx, "a0_rs", [P, GQ + HD])
    qk = core.sbuf(ctx, "a0_qk", [P, GQ + HD])
    v = core.sbuf(ctx, "a0_v", [P, KV, HD])
    qkT = core.sbuf(ctx, "a0_qkT", [P, 2, GQ + HD])
    nmax = core.sbuf(ctx, "a0_nmax", [P, 2, REP])
    rsum = core.sbuf(ctx, "a0_rsum", [P, 2, REP])
    rinv = core.sbuf(ctx, "a0_rinv", [P, 2, REP])
    pr = core.sbuf(ctx, "a0_pr", [P, 2, REP, S])
    pT = core.sbuf(ctx, "a0_pT", [P, REP * S])
    oT_h = core.sbuf(ctx, "a0_oT_h", [P, REP, S], F32R)
    oT_l = core.sbuf(ctx, "a0_oT_l", [P, REP, S], F32R)

    ps_q = core.psum(ctx, "a0_ps_q", [P, 512])
    ps_kvx = core.psum(ctx, "a0_ps_kvx", [P, 512])
    ps_t = core.psum(ctx, "a0_ps_t", [P, 1024])
    ps_s = core.psum(ctx, "a0_ps_s", [P, 512])
    ps_pT = core.psum(ctx, "a0_ps_pT", [P, 512])
    ps_oT = core.psum(ctx, "a0_ps_oT", [P, 512])
    ps_y = core.psum(ctx, "a0_ps_y", [P, 512])
    ps_kv, ps_xT = ps_kvx[:, 0:2 * HD], ps_kvx[:, 2 * HD:512]

    w_loaded = core.sems("a0_", "w_loaded_even w_loaded_odd")
    wo_loaded = core.sems("a0_", "wo_loaded_even wo_loaded_odd")
    (w_hi, w_lo, wo_hi, wo_lo, stat_done, var_done, rstd_done, xn_done,
     xt_done, xt_hi, xt_lo, proj_done, rope_mul, roped, v_done, tq_done, qkT_done,
     scores_done, max_done, exp_done, recip_done, norm_done, pt_done, pT_done, pv_done,
     ot_hi, ot_lo, wo_done, y_added, cast_done) = core.sems("a0_", (
         "w_hi w_lo wo_hi wo_lo stat_done var_done rstd_done xn_done "
         "xt_done xt_hi xt_lo proj_done rope_mul roped v_done tq_done qkT_done "
         "scores_done max_done exp_done recip_done norm_done pt_done pT_done pv_done "
         "ot_hi ot_lo wo_done y_added cast_done"))

    w_q = dram["L0_attn_Wq"].rearrange("(c p) n -> p c n", p=P)
    w_k = dram["L0_attn_Wk"].rearrange("(c p) n -> p c n", p=P)
    w_v = dram["L0_attn_Wv"].rearrange("(c p) n -> p c n", p=P)
    w_o = dram["L0_attn_Wo"].rearrange("(h p) n -> p h n", p=P)


    def attn0_sync(sp):
        xs = dram["x"].rearrange("b s d -> s b d")
        sp.dma_start(x[:, 0:1, :], xs[:, 0:1, :]).then_inc(x0_loaded, 16)
        sp.dma_start(ident[:, :], dram["ident"]).then_inc(const_loaded, 16)
        sp.dma_start(rope[:, :, :], dram["rope"].rearrange("s (a d) -> s a d", a=4)).then_inc(const_loaded, 16)
        sp.dma_start(mask_f[:, :], dram["mask"]).then_inc(const_loaded, 16)
        def load_out(g):
            if g >= 2:
                sp.wait_ge(wo_lo, g - 1)
            sp.dma_start(wo_raw[:, g % 2, :, :], w_o[:, g * REP:(g + 1) * REP, :]).then_inc(wo_loaded[g % 2], 16)

        for g in range(KV):
            if g >= 2:
                sp.wait_ge(w_lo, g - 1)
            sp.dma_start(w_raw[:, g % 2, :, 0:GQ], w_q[:, :, g * GQ:(g + 1) * GQ]).then_inc(w_loaded[g % 2], 16)
            sp.dma_start(w_raw[:, g % 2, :, GQ:GQ + HD], w_k[:, :, g * HD:(g + 1) * HD]).then_inc(w_loaded[g % 2], 16)
            sp.dma_start(w_raw[:, g % 2, :, GQ + HD:GC], w_v[:, :, g * HD:(g + 1) * HD]).then_inc(w_loaded[g % 2], 16)
            if g == 1:
                sp.dma_start(x[:, 1:B, :], xs[:, 1:B, :]).then_inc(x_loaded, 16)
            if g >= 1:
                load_out(g - 1)
        load_out(KV - 1)
        sp.dma_start(core.ctxT[:, :, :], dram["ctxT"].rearrange("(c p) t -> p c t", p=P)).then_inc(core.ctx_loaded, 16)

    def attn0_tensor(pe):
        def transpose_x(b, n):
            pe.wait_ge(xn_done, b + 1)
            if n is not None:
                pe.wait_ge(v_done, n)
            for c in range(DC):
                last = pe.transpose(ps_xT[:, c * P:(c + 1) * P], xn[:, c * P:(c + 1) * P], ident[:, :])
            last.then_inc(xt_done, 1)

        def project(b, g, n):
            if isinstance(n, int) and n < KV:
                pe.wait_ge(w_hi, g + 1)
                pe.wait_ge(w_lo, g + 1)
            if g == 0:
                pe.wait_ge(xt_hi, b + 1)
                pe.wait_ge(xt_lo, b + 1)
            for lo, hi, dst, read in ((0, GQ, ps_q[:, :], rope_mul), (GQ, GC, ps_kv, v_done)):
                wait_from(pe, read, n)
                for c in range(DC):
                    last = three_pass(pe, dst, (xT_h[:, c, :], xT_l[:, c, :]),
                                      (w_h[:, c, g, lo:hi], w_l[:, c, g, lo:hi]), c == 0, c == DC - 1)
            last.then_inc(proj_done, 1)

        def transpose_qk(g, n):
            pe.wait_ge(roped, n + 1)
            wait_from(pe, qkT_done, n)
            for h in range(REP + 1):
                last = pe.transpose(ps_t[:, h * P:(h + 1) * P], qk[:, h * HD:(h + 1) * HD], ident[:, :])
            last.then_inc(tq_done, 1)

        def scores(g, m):
            pe.wait_ge(qkT_done, m + 1)
            wait_from(pe, exp_done, m)
            pe.matmul(ps_s[:, :], ident_b[:, :], mask[:, :].unsqueeze(1).to_broadcast([P, REP, S]),
                      start=True, stop=False, skip_group_check=True)
            k = slice(GQ, GQ + HD)
            for h in range(REP):
                q = slice(h * HD, (h + 1) * HD)
                last = pe.matmul(ps_s[:, h * S:(h + 1) * S], qkT[:, g % 2, q], qkT[:, g % 2, k], start=False,
                                 stop=h == REP - 1, skip_group_check=True)
            last.then_inc(scores_done, 1)

        def transpose_p(g, m):
            pe.wait_ge(norm_done, m + 1)
            wait_from(pe, pT_done, m)
            for h in range(REP):
                last = pe.transpose(ps_pT[:, h * P:(h + 1) * P], pr[:, g % 2, h, :], ident[:, :])
            last.then_inc(pt_done, 1)

        def weigh_values(g, m):
            pe.wait_ge(pT_done, m + 1)
            pe.wait_ge(v_done, m + 1)
            wait_from(pe, ot_lo, m)
            pe.matmul(ps_oT[:, :], v[:, g, :], pT[:, :], start=True, stop=True).then_inc(pv_done, 1)

        def project_out(b, g, m):
            if isinstance(m, int) and m < KV:
                pe.wait_ge(wo_hi, g + 1)
                pe.wait_ge(wo_lo, g + 1)
            pe.wait_ge(ot_hi, m + 1)
            pe.wait_ge(ot_lo, m + 1)
            if g == 0:
                wait_from(pe, y_added, b)
            for h in range(REP):
                last = three_pass(pe, ps_y[:, 0:D], (oT_h[:, h, :], oT_l[:, h, :]),
                                  (wo_h[:, g * REP + h, :], wo_l[:, g * REP + h, :]),
                                  g == 0 and h == 0, g == KV - 1 and h == REP - 1)
            last.then_inc(wo_done, 1)

        def sequence(b, head, tail):
            for g in range(KV):
                m = KV * b + g
                before, back = (b, g - 1) if g else (b - 1, KV - 1), not (head and g == 0)
                scores(g, m)
                if g == KV - 2 and not tail:
                    transpose_x(b + 1, m + 2)
                if back:
                    weigh_values(before[1], m - 1)
                if not (tail and g == KV - 1):
                    transpose_qk((g + 1) % KV, m + 1)
                if not (tail and g >= KV - 2):
                    project(b + (g + 2) // KV, (g + 2) % KV, m + 2)
                if back:
                    project_out(*before, m - 1)
                transpose_p(g, m)

        pe.wait_ge(const_loaded, 48)
        transpose_x(0, None)
        project(0, 0, 0)
        transpose_qk(0, 0)
        project(0, 1, 1)
        pe.wait_ge(cast_done, 2)
        sequence(0, True, False)
        with pe.Fori(1, B - 1) as b:
            sequence(b, False, False)
        sequence(B - 1, False, True)
        weigh_values(KV - 1, KV * B - 1)
        project_out(B - 1, KV - 1, KV * B - 1)

    def attn0_scalar(act):
        def copy_hi(dst, src, done):
            act.activation(dst, src, ACT.Copy).then_inc(done, 1)

        def output_hi(m):
            act.wait_ge(pv_done, m + 1)
            wait_from(act, wo_done, m)
            copy_hi(oT_h[:, :, :], ps_oT[:, :], ot_hi)

        def exps(g, m):
            act.wait_ge(max_done, m + 1)
            wait_from(act, pt_done, m - 1)
            for h in range(REP):
                last = act.activation(pr[:, g % 2, h, :], ps_s[:, h * S:(h + 1) * S], ACT.Exp,
                                      bias=nmax[:, g % 2, h:h + 1], accum_out=rsum[:, g % 2, h:h + 1])
            last.then_inc(exp_done, 1)

        def x_hi(b):
            act.wait_ge(xt_done, b + 1)
            copy_hi(xT_h[:, :, :], ps_xT, xt_hi)

        def copy_probs(m):
            act.wait_ge(pt_done, m + 1)
            wait_from(act, pv_done, m)
            act.activation(pT[:, :], ps_pT[:, :], ACT.Copy).then_inc(pT_done, 1)

        def copy_qk(g, n):
            act.wait_ge(tq_done, n + 1)
            wait_from(act, scores_done, n - 1)
            act.activation(qkT[:, g % 2, :], ps_t[:, 0:GQ + HD], ACT.Copy).then_inc(qkT_done, 1)

        def split_in(g):
            act.wait_ge(w_loaded[g % 2], 48 * (g // 2 + 1))
            copy_hi(w_h[:, :, g, :], w_raw[:, g % 2, :, :], w_hi)

        def split_out(g):
            act.wait_ge(wo_loaded[g % 2], 16 * (g // 2 + 1))
            copy_hi(wo_h[:, g * REP:(g + 1) * REP, :], wo_raw[:, g % 2, :, :], wo_hi)

        def sequence(b, head, tail):
            for g in range(KV):
                m = KV * b + g
                if not (head and g == 0):
                    copy_probs(m - 1)
                if g == KV - 2 and not tail:
                    x_hi(b + 1)
                if not (head and g == 0):
                    output_hi(m - 1)
                exps(g, m)
                if not (tail and g == KV - 1):
                    copy_qk((g + 1) % KV, m + 1)
                if head:
                    if g < 2:
                        split_in(g + 2)
                    split_out(g)

        x_hi(0)
        split_in(0)
        act.wait_ge(const_loaded, 48)
        act.activation(ident_b[:, :], ident[:, :], ACT.Copy).then_inc(cast_done, 1)
        act.activation(mask[:, :], mask_f[:, :], ACT.Copy).then_inc(cast_done, 1)
        split_in(1)
        copy_qk(0, 0)
        sequence(0, True, False)
        with act.Fori(1, B - 1) as b:
            sequence(b, False, False)
        sequence(B - 1, False, True)
        copy_probs(KV * B - 1)
        output_hi(KV * B - 1)

    def attn0_gpsimd(pool):
        def rstd_of(b):
            pool.wait_ge(var_done, b + 1)
            wait_from(pool, xn_done, b)
            pool.tensor_tensor(rstd[:, :], vare[:, :], minus_half[:, :], ALU.pow).then_inc(rstd_done, 1)

        def add_rotated(n):
            pool.wait_ge(rope_mul, n + 1)
            wait_from(pool, tq_done, n)
            pool.tensor_tensor(qk[:, :], rc[:, :], rs[:, :], ALU.add).then_inc(roped, 1)

        def normalise(g, m):
            pool.wait_ge(recip_done, m + 1)
            pool.tensor_tensor(pr[:, g % 2, :, :], pr[:, g % 2, :, :],
                               rinv[:, g % 2, :].unsqueeze(2).to_broadcast([P, REP, S]),
                               ALU.mult).then_inc(norm_done, 1)

        def split_in(g):
            pool.wait_ge(w_hi, g + 1)
            sub_lo(pool, w_l[:, :, g, :], w_raw[:, g % 2, :, :], w_h[:, :, g, :]).then_inc(w_lo, 1)

        def split_out(g):
            pool.wait_ge(wo_hi, g + 1)
            gs = slice(g * REP, (g + 1) * REP)
            sub_lo(pool, wo_l[:, gs, :], wo_raw[:, g % 2, :, :], wo_h[:, gs, :]).then_inc(wo_lo, 1)

        def sequence(b, head, tail):
            for g in range(KV):
                m = KV * b + g
                if g == 1 and not tail:
                    rstd_of(b + 1)
                normalise(g, m)
                if head:
                    if g < 2:
                        split_in(g + 2)
                    split_out(g)
                if not (tail and g >= KV - 2):
                    add_rotated(m + 2)

        pool.memset(minus_half[:, :], -0.5).then_inc(half_set, 1)
        pool.wait_ge(half_set, 1)
        rstd_of(0)
        split_in(0)
        add_rotated(0)
        split_in(1)
        add_rotated(1)
        sequence(0, True, False)
        with pool.Fori(1, B - 1) as b:
            sequence(b, False, False)
        sequence(B - 1, False, True)

    def attn0_vector(dve):
        def lo(dst, src, hi, done):
            dve.tensor_tensor(dst, src, hi.bitcast(F32), ALU.subtract).then_inc(done, 1)

        def stats_x(b):
            tile = x[:, bass.ds(b, 1), :].rearrange("p a d -> p (a d)")
            dve.bn_stats(stats[:, :], tile).then_inc(stat_done, 1)

        def norm_x(b):
            tile = x[:, bass.ds(b, 1), :].rearrange("p a d -> p (a d)")
            dve.bn_aggr(mv[:, :], stats[:, :]).then_inc(stat_done, 1)
            dve.wait_ge(stat_done, 2 * b + 2)
            dve.tensor_scalar(vare[:, :], mv[:, 1:2], EPS, None, ALU.add).then_inc(var_done, 1)
            dve.wait_ge(rstd_done, b + 1)
            wait_from(dve, xt_done, b)
            dve.tensor_scalar(xn[:, :], tile, mv[:, 0:1], rstd[:, 0:1], ALU.subtract,
                              ALU.mult).then_inc(xn_done, 1)

        def x_lo(b):
            dve.wait_ge(xt_hi, b + 1)
            lo(xT_l[:, :, :].rearrange("p c s -> p (c s)"), ps_xT,
               xT_h[:, :, :].rearrange("p c s -> p (c s)"), xt_lo)

        def rotate(n):
            dve.wait_ge(proj_done, n + 1)
            wait_from(dve, roped, n)
            for o, w, src, cos, sin in ((0, REP, ps_q[:, :], rope[:, 0, :], rope[:, 1, :]),
                                        (GQ, 1, ps_kv[:, 0:HD], rope[:, 2, :], rope[:, 3, :])):
                halves = [P, w, 2, HD // 2]

                def table(t):
                    return t.rearrange("p (a d) -> p a d", a=2).unsqueeze(1).to_broadcast(halves)
                src4 = src.rearrange("p (h a d) -> p h a d", a=2, d=HD // 2)
                dve.tensor_tensor(rc[:, o:o + w * HD].rearrange("p (h a d) -> p h a d", a=2, d=HD // 2),
                                  src4, table(cos), ALU.mult)
                last = dve.tensor_tensor(
                    rs[:, o:o + w * HD].rearrange("p (h a d) -> p h a d", a=2, d=HD // 2),
                    src4[:, :, ::-1, :], table(sin), ALU.mult)
            last.then_inc(rope_mul, 1)

        def keep_values(g, n):
            wait_from(dve, pv_done, n - 3)
            dve.tensor_copy(v[:, g, :], ps_kv[:, HD:2 * HD]).then_inc(v_done, 1)

        def row_max(g, m):
            dve.wait_ge(scores_done, m + 1)
            wait_from(dve, exp_done, m - 1)
            dve.tensor_reduce(nmax[:, g % 2, :], ps_s[:, :].rearrange("p (h k) -> p h k", h=REP),
                              AX.X, ALU.max, negate=True).then_inc(max_done, 1)

        def recip(g, m):
            dve.wait_ge(exp_done, m + 1)
            dve.reciprocal(rinv[:, g % 2, :], rsum[:, g % 2, :]).then_inc(recip_done, 1)

        def output_lo(m):
            dve.wait_ge(ot_hi, m + 1)
            lo(oT_l[:, :, :].rearrange("p h s -> p (h s)"), ps_oT[:, :],
               oT_h[:, :, :].rearrange("p h s -> p (h s)"), ot_lo)

        def add_y(b):
            dve.wait_ge(wo_done, KV * b + KV)
            tile = x[:, bass.ds(b, 1), :].rearrange("p a d -> p (a d)")
            dve.tensor_tensor(tile, tile, ps_y[:, 0:D], ALU.add).then_inc(y_added, 1)

        def sequence(b, head, tail):
            for g in range(KV):
                m = KV * b + g
                if g == 0 and not tail:
                    stats_x(b + 1)
                row_max(g, m)
                if g == KV - 2 and not tail:
                    x_lo(b + 1)
                if not (head and g == 0):
                    output_lo(m - 1)
                if g == 1 and not tail:
                    dve.wait_ge(stat_done, 2 * b + 3)
                recip(g, m)
                if g == 1 and not tail:
                    norm_x(b + 1)
                if not (tail and g >= KV - 2):
                    rotate(m + 2)
                    keep_values((g + 2) % KV, m + 2)
                if g == 0 and not head:
                    add_y(b - 1)

        dve.wait_ge(x0_loaded, 16)
        stats_x(0)
        dve.wait_ge(stat_done, 1)
        norm_x(0)
        x_lo(0)
        dve.wait_ge(const_loaded, 48)
        rotate(0)
        keep_values(0, 0)
        rotate(1)
        keep_values(1, 1)
        dve.wait_ge(x_loaded, 16)
        sequence(0, True, False)
        with dve.Fori(1, B - 1) as b:
            sequence(b, False, False)
        sequence(B - 1, False, True)
        output_lo(KV * B - 1)
        add_y(B - 1)

    return (attn0_sync, attn0_tensor, attn0_scalar, attn0_gpsimd, attn0_vector), (y_added, B)


def row_stats(core, ctx, tag):
    stats = core.sbuf(ctx, tag + "stats", [P, B, 6])
    mv = core.sbuf(ctx, tag + "mv", [P, B, 2])
    vare = core.sbuf(ctx, tag + "vare", [P, B])
    rstd = core.sbuf(ctx, tag + "rstd", [P, B])
    stat_done, var_done, rstd_done = core.layer_sems(tag[0] + "_", "stat_done var_done rstd_done")

    def vector(dve):
        for b in range(B):
            dve.bn_stats(stats[:, b, :], core.x[:, b, :]).then_inc(stat_done, 1)
        for b in range(B):
            dve.wait_ge(stat_done, b + 1)
            last = dve.bn_aggr(mv[:, b, :], stats[:, b, :])
        last.then_inc(stat_done, 1)
        dve.wait_ge(stat_done, B + 1)
        dve.tensor_scalar(vare[:, :], mv[:, :, 1], EPS, None, ALU.add).then_inc(var_done, 1)

    def gpsimd(pool):
        pool.wait_ge(var_done, 1)
        pool.tensor_tensor(rstd[:, :], vare[:, :], core.minus_half[:, :].to_broadcast([P, B]),
                           ALU.pow).then_inc(rstd_done, 1)

    def normalise(dve, dst, b):
        return dve.tensor_scalar(dst, core.tile(b), mv[:, bass.ds(b, 1), 0], rstd[:, bass.ds(b, 1)],
                                 ALU.subtract, ALU.mult)

    return vector, gpsimd, normalise, rstd_done


CH, CW = 16, 8
HB = B // 2
UN = HB * CW * CW


def convolution(core, ctx, gate, tag, taps, context_pairs):
    dram, x, ident, ctxT = core.dram, core.x, core.ident, core.ctxT
    nT = core.sbuf(ctx, tag + "nT", [P, DC, B * S])
    oT = core.sbuf(ctx, tag + "oT", [P, DC, B * S])
    xn = core.sbuf(ctx, tag + "xn", [P, 2, D])
    hankel = core.sbuf(ctx, tag + "hankel", [P, CH, D])
    all_taps = core.sbuf(ctx, tag + "all_taps", [P, CH, D])
    t = core.sbuf(ctx, tag + "t", [P, 2, D])
    p = core.sbuf(ctx, tag + "p", [P, 2, DC, UN])
    z = core.sbuf(ctx, tag + "z", [P, DC, UN])
    ps_n = [core.psum(ctx, f"{tag}ps_n{k}", [P, 512]) for k in range(2)]
    ps_g = [core.psum(ctx, f"{tag}ps_g{k}", [P, 512]) for k in range(2)]
    ps_c = [[core.psum(ctx, f"{tag}ps_c{k}{c}", [P, 512]) for c in range(DC)] for k in range(2)]
    (taps_loaded, aux_loaded, xn_done, nt_done, nT_done, w_done, g_done, skip_done, x_skipped, turned_taps,
     diag_done, t_done, prod_done, conv_done, z_done, o_done, back_done, added) = core.layer_sems(
        "c_", "taps_loaded aux_loaded xn_done nt_done nT_done w_done g_done skip_done x_skipped turned_taps "
        "diag_done t_done prod_done conv_done z_done o_done back_done added")
    stats_vector, stats_gpsimd, normalise, rstd_done = row_stats(core, ctx, tag)
    enter, clear = core.start(gate)
    if context_pairs:
        a_of, b_of, c_of = ctxT, ctxT, nT
        dcol = core.sbuf(ctx, tag + "dcol", [P, CH])
    else:
        a_of, b_of, c_of = nT, ctxT, ctxT
        ctok = core.sbuf(ctx, tag + "ctok", [P, B, D])
        skip = core.sbuf(ctx, tag + "skip", [P, 1])
        ones = core.sbuf(ctx, tag + "ones", [P, P])
        w = core.sbuf(ctx, tag + "w", [P, 2, D])
        sk = core.sbuf(ctx, tag + "sk", [P, 2, D])


    def each_unit(eng, unit, between=None):
        for half in range(2):
            for h in range(2):
                unit(half, h, h)
            if half == 1 and between:
                between()
            with eng.Fori(2, CH - 1, 2) as h:
                for k in range(2):
                    unit(half, h + k, k)

    def channels(v, c, h, half, spread):
        v = v[:, c, :].rearrange("p (b h i) -> p b h i", h=CH, i=CW)[:, half * HB:(half + 1) * HB, bass.ds(h, 1), :]
        v = v.rearrange("p b a i -> p b (a i)")
        shape = [P, HB, CW, CW]
        return v.unsqueeze(3).to_broadcast(shape) if spread == "j" else v.unsqueeze(2).to_broadcast(shape)

    def cube(v):
        return v.rearrange("p (b i j) -> p b i j", i=CW, j=CW)

    def toeplitz(h):
        return all_taps[:, bass.ds(h, 1), :].rearrange("p a d -> p (a d)")

    def sync(sp):
        enter(sp)
        rows = bass.AP(dram[taps].tensor, 0, [[1, P], [2 * D, CH], [1, D]])
        if context_pairs:
            d = dram["L1_xattn_D"]
            sp.dma_start(dcol[:, :], bass.AP(d.tensor, 0, [[0, P], [1, CH]])).then_inc(aux_loaded, 16)
        else:
            sp.dma_start(ctok[:, :, :], dram["ctx_2048"].rearrange("b s d -> s b d")).then_inc(aux_loaded, 16)
            sp.dma_start(skip[:, :], dram["fside_S2_0"].rearrange("(s a) -> s a", a=1)).then_inc(aux_loaded, 16)
            sp.dma_start(ones[:, :], dram["same_head"]).then_inc(aux_loaded, 16)
        sp.dma_start(hankel[:, :, :], rows).then_inc(taps_loaded, 16)

    def tensor(pe):
        enter(pe)
        pe.wait_ge(core.const_loaded, 48)

        def turn(b, k):
            pe.wait_ge(xn_done, b + 1)
            wait_from(pe, nT_done, b - 1)
            for c in range(DC):
                last = pe.transpose(ps_n[k][:, c * P:(c + 1) * P], xn[:, k, c * P:(c + 1) * P], ident[:, :])
            last.then_inc(nt_done, 1)

        def sum_channels(b, k):
            pe.wait_ge(w_done, b + 1)
            wait_from(pe, skip_done, b - 1)
            pe.matmul(ps_g[k][:, 0:D], ones[:, :], w[:, k, :], start=True, stop=True).then_inc(g_done, 1)

        if context_pairs:
            pipeline(pe, ((1, turn),))
        else:
            pe.wait_ge(aux_loaded, 48)
            pipeline(pe, ((2, sum_channels), (1, turn)))

        def convolve(half, h, k):
            n = CH * half + h
            pe.wait_ge(t_done, n + 1)
            pe.wait_ge(prod_done, n + 1)
            wait_from(pe, z_done, 2 * (n - 1))
            near, far = t[:, k, 0:P], t[:, k, P:D]
            pe.matmul(ps_c[k][0][:, :], near, p[:, k, 0, :], start=True, stop=True)
            pe.matmul(ps_c[k][1][:, :], far, p[:, k, 0, :], start=True, stop=False)
            pe.matmul(ps_c[k][1][:, :], near, p[:, k, 1, :], start=False, stop=True).then_inc(conv_done, 1)

        def turn_back(half):
            pe.wait_ge(o_done, 2 * CH * (half + 1))
            for pair in range(HB // 2 * half, HB // 2 * (half + 1)):
                if pair >= 2:
                    pe.wait_ge(added, pair - 1)
                for j in range(2):
                    for c in range(DC):
                        at = (2 * pair + j) * S
                        last = pe.transpose(ps_n[pair % 2][:, j * D + c * P:j * D + (c + 1) * P],
                                            oT[:, c, at:at + S], ident[:, :])
                last.then_inc(back_done, 1)

        each_unit(pe, convolve, lambda: turn_back(0))
        turn_back(1)

    def scalar(act):
        enter(act)
        act.wait_ge(taps_loaded, 16)
        act.activation(all_taps[:, :, :], hankel[:, :, ::-1], ACT.Copy).then_inc(turned_taps, 1)

        def copy_turned(b, k):
            act.wait_ge(nt_done, b + 1)
            act.activation(nT[:, :, bass.ds(b * S, S)], ps_n[k][:, 0:D].rearrange("p (c s) -> p c s", c=DC),
                           ACT.Copy).then_inc(nT_done, 1)

        pipeline(act, ((1, copy_turned),))

        def place_taps(half, h, k):
            n = CH * half + h
            wait_from(act, conv_done, n - 1)
            act.activation(t[:, k, :], toeplitz(h), ACT.Copy).then_inc(t_done, 1)

        act.wait_ge(turned_taps, 1)
        if context_pairs:
            act.wait_ge(diag_done, CH)
        each_unit(act, place_taps)

    def gpsimd(pool):
        clear(pool)
        enter(pool)
        stats_gpsimd(pool)
        if not context_pairs:
            def add_skip(b, k):
                pool.wait_ge(skip_done, b + 1)
                pool.tensor_tensor(core.tile(b), core.tile(b), sk[:, k, :], ALU.add).then_inc(x_skipped, 1)

            pipeline(pool, ((3, add_skip),))

        def product(half, h, k):
            n = CH * half + h
            wait_from(pool, conv_done, n - 1)
            for c in range(DC):
                last = pool.tensor_tensor(cube(p[:, k, c, :]), channels(a_of, c, h, half, "j"),
                                          channels(b_of, c, h, half, "i"), ALU.mult)
            last.then_inc(prod_done, 1)

        if not context_pairs:
            pool.wait_ge(nT_done, B)
        pool.wait_ge(core.ctx_loaded, 16)
        each_unit(pool, product)

    def vector(dve):
        enter(dve)
        stats_vector(dve)
        dve.wait_ge(rstd_done, 1)

        def norm_tile(b, k):
            wait_from(dve, nt_done, b - 1)
            normalise(dve, xn[:, k, :], b).then_inc(xn_done, 1)

        def context(b):
            return ctok[:, bass.ds(b, 1), :].rearrange("p a d -> p (a d)")

        def weigh_skip(b, k):
            dve.wait_ge(xn_done, b + 1)
            wait_from(dve, g_done, b - 1)
            dve.scalar_tensor_tensor(out=w[:, k, :], in0=xn[:, k, :], scalar=skip[:, 0:1], in1=context(b),
                                     op0=ALU.mult, op1=ALU.mult).then_inc(w_done, 1)

        def skip_tile(b, k):
            dve.wait_ge(g_done, b + 1)
            wait_from(dve, x_skipped, b - 1)
            dve.tensor_tensor(sk[:, k, :], ps_g[k][:, 0:D], context(b), ALU.mult).then_inc(skip_done, 1)

        if context_pairs:
            pipeline(dve, ((0, norm_tile),))
            dve.wait_ge(turned_taps, 1)
            dve.wait_ge(aux_loaded, 16)
            with dve.Fori(0, CH) as h:
                diagonal = toeplitz(h)[:, 0:P]
                dve.scalar_tensor_tensor(out=diagonal, in0=ident[:, :], scalar=dcol[:, bass.ds(h, 1)], in1=diagonal,
                                         op0=ALU.mult, op1=ALU.add).then_inc(diag_done, 1)
            dve.wait_ge(nT_done, B)
        else:
            dve.wait_ge(aux_loaded, 48)
            pipeline(dve, ((1, weigh_skip), (3, skip_tile), (0, norm_tile)))

        def read_out(half, h, k):
            n = CH * half + h
            dve.wait_ge(conv_done, n + 1)
            for c in range(DC):
                wait_from(dve, o_done, 2 * n - 1 + c)
                dve.tensor_tensor(cube(z[:, c, :]), cube(ps_c[k][c][:, :]),
                                  channels(c_of, c, h, half, "j"), ALU.mult).then_inc(z_done, 1)
            for c in range(DC):
                dve.wait_ge(z_done, 2 * n + 1 + c)
                dst = oT[:, c, :].rearrange("p (b h j) -> p b h j", h=CH, j=CW)[:, half * HB:(half + 1) * HB, bass.ds(h, 1), :]
                dve.tensor_reduce(dst.rearrange("p b a j -> p b (a j)"), z[:, c, :].rearrange("p (b i j) -> p b j i", i=CW, j=CW),
                                  AX.X, ALU.add).then_inc(o_done, 1)

        def add_half(half):
            if not context_pairs and half == 0:
                dve.wait_ge(x_skipped, B)
            for pair in range(HB // 2 * half, HB // 2 * (half + 1)):
                dve.wait_ge(back_done, pair + 1)
                two = x[:, 2 * pair:2 * pair + 2, :]
                dve.tensor_tensor(two, two, ps_n[pair % 2][:, :].rearrange("p (b d) -> p b d", b=2),
                                  ALU.add).then_inc(added, 1)

        each_unit(dve, read_out, lambda: add_half(0))
        add_half(1)

    return (sync, tensor, scalar, gpsimd, vector), (added, B // 2)


def convolution0(core, ctx, gate):
    return convolution(core, ctx, gate, "c0_", "taps0", False)


def convolution1(core, ctx, gate):
    return convolution(core, ctx, gate, "c1_", "taps1", True)


H1, HF = 16, 16
RC = slice(2 * H1, 9 * H1)
IC = slice(9 * H1, 16 * H1)


def transforms():
    forward, inverse = np.zeros((2, D, D))
    n = np.arange(HF)
    rows = [(k, 0) for k in (0, 8, *range(1, 8))] + [(k, 1) for k in range(1, 8)]
    for r, (k, imaginary) in enumerate(rows):
        turn = 2 * np.pi * k * n / HF
        wave = -np.sin(turn) if imaginary else np.cos(turn)
        for h in range(H1):
            forward[h * HF + n, r * H1 + h] = wave * (1 if k in (0, 8) else np.sqrt(2))
            inverse[h * HF + n, r * H1 + h] = wave / HF
    return forward.astype(np.float32), inverse.astype(np.float32)


def attention1(core, ctx, gate):
    dram, x, ident = core.dram, core.x, core.ident
    tag = "a1_"
    raw = core.sbuf(ctx, tag + "raw", [P, 5, DC, D])
    w = core.sbuf(ctx, tag + "w", [P, DC, 3 * D])
    before = core.sbuf(ctx, tag + "before", [P, P])
    xn = core.sbuf(ctx, tag + "xn", [P, 2, D])
    xT = core.sbuf(ctx, tag + "xT", [P, 2, D])
    sq = core.sbuf(ctx, tag + "sq", [P, 2, 2 * D])
    norm2 = core.sbuf(ctx, tag + "norm2", [P, 2, 2 * H1])
    rn = core.sbuf(ctx, tag + "rn", [P, 2, 2 * H1])
    qk = core.sbuf(ctx, tag + "qk", [P, 2, 2 * D])
    pp = core.sbuf(ctx, tag + "pp", [P, 2, D])
    ii = core.sbuf(ctx, tag + "ii", [P, 2, 7 * H1])
    ir = core.sbuf(ctx, tag + "ir", [P, 2, 7 * H1])
    pT = core.sbuf(ctx, tag + "pT", [P, 2, D])
    ps_n = core.psum(ctx, tag + "ps_n", [P, 512])
    ps_p = core.psum(ctx, tag + "ps_p", [P, 512])
    ps_qk = [core.psum(ctx, f"{tag}ps_qk{k}", [P, 512]) for k in range(2)]
    ps_c = [core.psum(ctx, f"{tag}ps_c{k}", [P, 512]) for k in range(2)]
    ps_o = [core.psum(ctx, f"{tag}ps_o{k}", [P, 512]) for k in range(2)]
    (raw_loaded, before_loaded, fold_done, folded, xn_done, xt_done, xT_done, qk_done, sq_done, norm2_done,
     rn_done, scaled, sum_done, prod_done, pp_done, pt_done, pT_done, out_done, added) = core.sems(
        tag, "raw_loaded before_loaded fold_done folded xn_done xt_done xT_done qk_done sq_done norm2_done "
        "rn_done scaled sum_done prod_done pp_done pt_done pT_done out_done added")
    stats_vector, stats_gpsimd, normalise, rstd_done = row_stats(core, ctx, tag)
    folds = ((0, 2), (1, 2), (3, 4))

    def sync(sp):
        sp.wait_ge(*gate)
        for i, name in enumerate(("L1_attn_W_q", "L1_attn_W_kv", "forward", "inverse", "L1_WoT")):
            sp.dma_start(raw[:, i, :, :], dram[name].rearrange("(c p) n -> p c n", p=P)).then_inc(raw_loaded, 16)
        sp.dma_start(before[:, :], dram["before"]).then_inc(before_loaded, 16)

    def tensor(pe):
        pe.wait_ge(*gate)
        pe.wait_ge(raw_loaded, 80)
        for i, (left, right) in enumerate(folds):
            for m in range(DC):
                f = i * DC + m
                if f >= 2:
                    pe.wait_ge(folded, f - 1)
                for c in range(DC):
                    last = pe.matmul(ps_qk[f % 2][:, 0:D], raw[:, left, c, m * P:(m + 1) * P], raw[:, right, c, :],
                                     start=c == 0, stop=c == DC - 1)
                last.then_inc(fold_done, 1)
        pe.wait_ge(folded, 6)
        pe.wait_ge(before_loaded, 16)

        def turn(b, k):
            pe.wait_ge(xn_done, b + 1)
            wait_from(pe, xT_done, b)
            for c in range(DC):
                last = pe.transpose(ps_n[:, c * P:(c + 1) * P], xn[:, k, c * P:(c + 1) * P], ident[:, :])
            last.then_inc(xt_done, 1)

        def project(b, k):
            pe.wait_ge(xT_done, b + 1)
            wait_from(pe, scaled, b - 1)
            for c in range(DC):
                last = pe.matmul(ps_qk[k][:, :], xT[:, k, c * P:(c + 1) * P], w[:, c, 0:2 * D],
                                 start=c == 0, stop=c == DC - 1)
            last.then_inc(qk_done, 1)

        def running_sum(b, k):
            pe.wait_ge(scaled, b + 1)
            wait_from(pe, prod_done, b - 1)
            pe.matmul(ps_c[k][:, 0:D], before[:, :], qk[:, k, D:2 * D], start=True, stop=True).then_inc(sum_done, 1)

        def turn_products(b, k):
            pe.wait_ge(pp_done, b + 1)
            wait_from(pe, pT_done, b)
            for c in range(DC):
                last = pe.transpose(ps_p[:, c * P:(c + 1) * P], pp[:, k, c * P:(c + 1) * P], ident[:, :])
            last.then_inc(pt_done, 1)

        def output(b, k):
            pe.wait_ge(pT_done, b + 1)
            wait_from(pe, added, b - 1)
            for c in range(DC):
                last = pe.matmul(ps_o[k][:, 0:D], pT[:, k, c * P:(c + 1) * P], w[:, c, 2 * D:3 * D],
                                 start=c == 0, stop=c == DC - 1)
            last.then_inc(out_done, 1)

        pipeline(pe, ((6, turn_products), (7, output), (1, turn), (2, project), (4, running_sum)))

    def scalar(act):
        act.wait_ge(*gate)
        for f in range(6):
            act.wait_ge(fold_done, f + 1)
            i, m = divmod(f, DC)
            act.activation(w[:, m, i * D:(i + 1) * D], ps_qk[f % 2][:, 0:D], ACT.Copy).then_inc(folded, 1)

        def copy_turned(b, k):
            act.wait_ge(xt_done, b + 1)
            wait_from(act, qk_done, b - 1)
            act.activation(xT[:, k, :], ps_n[:, 0:D], ACT.Copy).then_inc(xT_done, 1)

        def square(b, k):
            act.wait_ge(qk_done, b + 1)
            wait_from(act, norm2_done, b - 1)
            act.activation(sq[:, k, :], ps_qk[k][:, :], ACT.Square).then_inc(sq_done, 1)

        def copy_products(b, k):
            act.wait_ge(pt_done, b + 1)
            wait_from(act, out_done, b - 1)
            act.activation(pT[:, k, :], ps_p[:, 0:D], ACT.Copy).then_inc(pT_done, 1)

        pipeline(act, ((6, copy_products), (1, copy_turned), (2, square)))

    def gpsimd(pool):
        stats_gpsimd(pool)

        def norms(b, k):
            pool.wait_ge(norm2_done, b + 1)
            wait_from(pool, scaled, b - 1)
            pool.tensor_tensor(rn[:, k, :], norm2[:, k, :], core.minus_half[:, :].to_broadcast([P, 2 * H1]),
                               ALU.pow).then_inc(rn_done, 1)

        def join_products(b, k):
            pool.wait_ge(prod_done, b + 1)
            pool.tensor_tensor(pp[:, k, RC], pp[:, k, RC], ii[:, k, :], ALU.subtract)
            pool.tensor_tensor(pp[:, k, IC], pp[:, k, IC], ir[:, k, :], ALU.add).then_inc(pp_done, 1)

        pipeline(pool, ((5, join_products), (3, norms)))

    def vector(dve):
        dve.wait_ge(*gate)
        stats_vector(dve)
        dve.wait_ge(rstd_done, 1)

        def norm_tile(b, k):
            wait_from(dve, xt_done, b - 1)
            normalise(dve, xn[:, k, :], b).then_inc(xn_done, 1)

        def sum_squares(b, k):
            dve.wait_ge(sq_done, b + 1)
            wait_from(dve, rn_done, b - 1)
            dve.tensor_reduce(norm2[:, k, :].rearrange("p (a h) -> p a h", a=2),
                              sq[:, k, :].rearrange("p (a f h) -> p a h f", a=2, h=H1), AX.X,
                              ALU.add).then_inc(norm2_done, 1)

        def scale_unit(b, k):
            dve.wait_ge(rn_done, b + 1)
            wait_from(dve, prod_done, b - 1)
            scale = rn[:, k, :].rearrange("p (a h) -> p a h", a=2).unsqueeze(2).to_broadcast([P, 2, HF, H1])
            dve.tensor_tensor(qk[:, k, :].rearrange("p (a f h) -> p a f h", a=2, h=H1),
                              ps_qk[k][:, :].rearrange("p (a f h) -> p a f h", a=2, h=H1), scale,
                              ALU.mult).then_inc(scaled, 1)

        def products(b, k):
            dve.wait_ge(sum_done, b + 1)
            wait_from(dve, pt_done, b - 1)
            c, q, both = ps_c[k], qk[:, k, :], slice(0, 9 * H1)
            dve.tensor_tensor(pp[:, k, both], q[:, both], c[:, both], ALU.mult)
            dve.tensor_tensor(ii[:, k, :], q[:, IC], c[:, IC], ALU.mult)
            dve.tensor_tensor(pp[:, k, IC], q[:, RC], c[:, IC], ALU.mult)
            dve.tensor_tensor(ir[:, k, :], q[:, IC], c[:, RC], ALU.mult).then_inc(prod_done, 1)

        def add_tile(b, k):
            dve.wait_ge(out_done, b + 1)
            dve.tensor_tensor(core.tile(b), core.tile(b), ps_o[k][:, 0:D], ALU.add).then_inc(added, 1)

        pipeline(dve, ((4, scale_unit), (5, products), (3, sum_squares), (8, add_tile), (0, norm_tile)))

    return (sync, tensor, scalar, gpsimd, vector), (added, B)


GT = 512
NG = B * S // GT


class Layer0:
    tag, experts, top, slots, chunks = "f0_", 16, 6, 9, (128, 128, 96)
    biased, limit, cells = True, None, 2 * 16 + 1
    names = dict(router="L0_routerT", in_="L0_in", out="L0_out", pick="pick0")


class Layer1:
    tag, experts, top, slots, chunks = "f1_", 8, 2, 8, (128, 128)
    biased, limit, cells = False, 7.0, 2 * 8
    names = dict(router="L1_ffn_Wr", in_="L1_in", out="L1_out", pick="pick1")


def pick(cfg):
    hidden = sum(cfg.chunks)
    per = hidden * cfg.slots // (cfg.experts + (2 if cfg.biased else 0))
    table = np.zeros((cfg.cells, cfg.slots, hidden), np.float32)
    for s in range(cfg.slots):
        for r in range(hidden):
            e = (s * hidden + r) // per
            if e < cfg.experts:
                table[e, s, r] = table[cfg.experts + e, s, r] = 1.0
            else:
                table[2 * cfg.experts, s, r] = 1.0
    return table


def expert_layer(core, ctx, gate, cfg):
    dram, x, ident, tag = core.dram, core.x, core.ident, cfg.tag
    E, NS, NC, hidden, cells = cfg.experts, cfg.slots, len(cfg.chunks), sum(cfg.chunks), cfg.cells
    UNITS = NG * NC
    xT_h = core.sbuf(ctx, tag + "xT_h", [P, DC, B * S], F32R)
    xT_l = core.sbuf(ctx, tag + "xT_l", [P, DC, B * S], F32R)
    xn = core.sbuf(ctx, tag + "xn", [P, 2, D])
    in_raw = core.sbuf(ctx, tag + "in_raw", [P, DC, 2 * hidden])
    out_raw = core.sbuf(ctx, tag + "out_raw", [P, NC, D])
    pick_raw = core.sbuf(ctx, tag + "pick_raw", [cells, hidden])
    in_h = core.sbuf(ctx, tag + "in_h", [P, 2, DC, 2 * hidden], F32R)
    in_l = core.sbuf(ctx, tag + "in_l", [P, 2, DC, 2 * hidden], F32R)
    out_h = core.sbuf(ctx, tag + "out_h", [P, 2, NC, D], F32R)
    out_l = core.sbuf(ctx, tag + "out_l", [P, 2, NC, D], F32R)
    picked = core.sbuf(ctx, tag + "picked", [cells, 2, hidden], F32R)
    r_raw = core.sbuf(ctx, tag + "r_raw", [P, DC, E])
    r_h = core.sbuf(ctx, tag + "r_h", [P, DC, E], F32R)
    r_l = core.sbuf(ctx, tag + "r_l", [P, DC, E], F32R)
    logitsT = core.sbuf(ctx, tag + "logitsT", [E, B * S])
    table = [P, B, E]
    logits, ex, prob, key, above, equal, run0, run1 = (core.sbuf(ctx, tag + n, table) for n in (
        "logits", "ex", "prob", "key", "above", "equal", "run0", "run1"))
    eight = core.sbuf(ctx, tag + "eight", [P, B, 8])
    row = core.sbuf(ctx, tag + "row", [P, B])
    row2 = core.sbuf(ctx, tag + "row2", [P, B])
    c_h = core.sbuf(ctx, tag + "c_h", table, F32R)
    cell = core.sbuf(ctx, tag + "cell", [P, B, cells])
    cellT = core.sbuf(ctx, tag + "cellT", [cells, B * S], F32R)
    s = core.sbuf(ctx, tag + "s", [P, 2, GT])
    m = core.sbuf(ctx, tag + "m", [P, 2, GT])
    h = core.sbuf(ctx, tag + "h", [P, 2, GT])
    h_h = core.sbuf(ctx, tag + "h_h", [P, 2, GT], F32R)
    h_l = core.sbuf(ctx, tag + "h_l", [P, 2, GT], F32R)
    if cfg.biased:
        bias_raw = core.sbuf(ctx, tag + "bias_raw", [P, 2, NC])
        bias = core.sbuf(ctx, tag + "bias", [P, 2, 2, NC])
        b2_raw = core.sbuf(ctx, tag + "b2_raw", [cells, D])
        b2_h = core.sbuf(ctx, tag + "b2_h", [cells, D], F32R)
        b2_l = core.sbuf(ctx, tag + "b2_l", [cells, D], F32R)
        router_b = core.sbuf(ctx, tag + "router_b", [P, E])
    ps_a, ps_u, ps_c, ps_y = ([core.psum(ctx, f"{tag}ps_{n}{k}", [P, 512]) for k in range(2)] for n in "aucy")
    (w0_loaded, w1_loaded, aux_loaded, router_hi, router_lo, b2_hi, b2_lo, xn_done, xt_done, xt_hi, xt_lo,
     logits_done, logits_copied, turned, exp_in, exp_done, routed, step, cell_done, cellT_done, bias_done,
     bias_added, w_hi, w_lo, in_done, silu_done, clipped, gated, h_done, h_hi, h_lo, out_done, added) = core.layer_sems(
        "f_", "w0_loaded w1_loaded aux_loaded router_hi router_lo b2_hi b2_lo xn_done xt_done xt_hi xt_lo "
        "logits_done logits_copied turned exp_in exp_done routed step cell_done cellT_done bias_done "
        "bias_added w_hi w_lo in_done silu_done clipped gated h_done h_hi h_lo out_done added")
    w_loaded = (w0_loaded, w1_loaded)
    aux = 16 * (3 if cfg.biased else 1)
    slot_loads = 16 * (4 if cfg.biased else 3)
    stats_vector, stats_gpsimd, normalise, rstd_done = row_stats(core, ctx, tag)
    enter, clear = core.start(gate)

    def tiles(eng, turn):
        for k in range(2):
            turn(k, k)
        with eng.Fori(2, B - 1, 2) as b:
            for k in range(2):
                turn(b + k, k)

    def each_slot(eng, slot):
        slot(0, 0, True)
        slot(1, 1, True)
        rest = NS - 1 if NS % 2 else NS - 2
        with eng.Fori(2, rest - 1, 2) as t:
            slot(t, 0, True)
            slot(t + 1, 1, True)
        for t in range(rest, NS):
            slot(t, t % 2, t < NS - 1)

    def units():
        return [(g, c, (g * NC + c) % 2) for g in range(NG) for c in range(NC)]

    def sync(sp):
        enter(sp)
        sp.dma_start(r_raw[:, :, :], dram[cfg.names["router"]].rearrange("(c p) e -> p c e", p=P)).then_inc(aux_loaded, 16)
        if cfg.biased:
            gb = dram["L0_ffn_gate_b"]
            sp.dma_start(router_b[:, :], bass.AP(gb.tensor, 0, [[0, P], [1, E]])).then_inc(aux_loaded, 16)
            sp.dma_start(b2_raw[:, :], dram["L0_b2"]).then_inc(aux_loaded, 16)

        def slot(t, k, more):
            wait_from(sp, w_lo, t)
            one = bass.ds(t, 1)
            sp.dma_start(in_raw[:, :, :], dram[cfg.names["in_"]][one].rearrange("a p c n -> p (a c) n")).then_inc(w_loaded[k], 16)
            sp.dma_start(out_raw[:, :, :], dram[cfg.names["out"]][one].rearrange("a p c n -> p (a c) n")).then_inc(w_loaded[k], 16)
            sp.dma_start(pick_raw[:, :], dram[cfg.names["pick"]][:, one, :].rearrange("e a r -> e (a r)")).then_inc(w_loaded[k], 16)
            if cfg.biased:
                sp.dma_start(bias_raw[:, :, :], dram["L0_b13"][one].rearrange("a p w c -> p (a w) c")).then_inc(w_loaded[k], 16)

        each_slot(sp, slot)

    def tensor(pe):
        enter(pe)

        def turn(b, k):
            pe.wait_ge(xn_done, b + 1)
            wait_from(pe, xt_lo, b - 1)
            for c in range(DC):
                last = pe.transpose(ps_a[k][:, c * P:(c + 1) * P], xn[:, k, c * P:(c + 1) * P], ident[:, :])
            last.then_inc(xt_done, 1)

        tiles(pe, turn)
        pe.wait_ge(router_hi, 1)
        pe.wait_ge(router_lo, 1)
        for g in range(NG):
            cols = slice(g * GT, (g + 1) * GT)
            pe.wait_ge(xt_hi, 4 * g + 4)
            pe.wait_ge(xt_lo, 4 * g + 4)
            if g >= 2:
                pe.wait_ge(logits_copied, g - 1)
            for c in range(DC):
                last = three_pass(pe, ps_u[g % 2][0:E, :], (r_h[:, c, :], r_l[:, c, :]),
                                  (xT_h[:, c, cols], xT_l[:, c, cols]), c == 0, c == DC - 1)
            last.then_inc(logits_done, 1)
        pe.wait_ge(logits_copied, NG)
        for b in range(B):
            last = pe.transpose(ps_c[0][:, b * E:(b + 1) * E], logitsT[:, b * S:(b + 1) * S], ident[0:E, 0:E])
        last.then_inc(turned, 1)
        pe.wait_ge(cell_done, 1)
        for b in range(B):
            g = b // 4
            if b % 4 == 0 and g >= 2:
                pe.wait_ge(cellT_done, g - 1)
            last = pe.transpose(ps_u[g % 2][0:cells, b % 4 * S:(b % 4 + 1) * S], cell[:, b, :], ident[:, :])
            if b % 4 == 3:
                last.then_inc(turned, 1)
        if cfg.biased:
            pe.wait_ge(b2_hi, 1)
            pe.wait_ge(b2_lo, 1)
            for b in range(B):
                pair = b // 2
                if b % 2 == 0:
                    pe.wait_ge(cellT_done, b // 4 + 1)
                    if pair >= 2:
                        pe.wait_ge(bias_added, pair - 1)
                for w in (b2_h, b2_l):
                    last = pe.matmul(ps_y[pair % 2][:, b % 2 * D:(b % 2 + 1) * D], cellT[:, b * S:(b + 1) * S], w[:, :],
                                     start=b % 2 == 0 and w is b2_h, stop=b % 2 == 1 and w is b2_l,
                                     skip_group_check=True)
                if b % 2:
                    last.then_inc(bias_done, 1)
        pe.wait_ge(cellT_done, NG)
        if cfg.biased:
            pe.wait_ge(bias_added, B // 2)

        def hidden_sums(t, k, n, g, c, q):
            if (g, c) == (0, 0):
                pe.wait_ge(w_hi, t + 1)
                pe.wait_ge(w_lo, t + 1)
            wait_from(pe, silu_done, n - 1)
            wait_from(pe, gated, n - 1)
            wait_from(pe, h_done, n - 1)
            R, cols = cfg.chunks[c], slice(g * GT, (g + 1) * GT)
            for dst, first in ((ps_a, 0), (ps_u, hidden)):
                rows = slice(first + c * P, first + c * P + R)
                for d in range(DC):
                    three_pass(pe, dst[q][0:R, :], (in_h[:, k, d, rows], in_l[:, k, d, rows]),
                               (xT_h[:, d, cols], xT_l[:, d, cols]), d == 0, d == DC - 1)
            pe.matmul(ps_c[q][0:R, :], picked[:, k, c * P:c * P + R], cellT[:, cols], start=True,
                      stop=True).then_inc(in_done, 1)

        def output_sums(t, k, n, g, c, q):
            pe.wait_ge(h_hi, n + 1)
            pe.wait_ge(h_lo, n + 1)
            if c == 0:
                wait_from(pe, added, NG * t + g)
            R = cfg.chunks[c]
            for b in range(4):
                s4, out = slice(b * S, (b + 1) * S), ps_y[b // 2][:, b % 2 * D:(b % 2 + 1) * D]
                passes = ((h_h, out_h), (h_h, out_l), (h_l, out_h))
                for i, (a, w) in enumerate(passes):
                    last = pe.matmul(out, a[0:R, q, s4], w[0:R, k, c, :],
                                     start=c == 0 and b % 2 == 0 and i == 0,
                                     stop=c == NC - 1 and b % 2 == 1 and i == 2, skip_group_check=True)
            last.then_inc(out_done, 1)

        def slot(t, k, more):
            todo = units()
            for i, (g, c, q) in enumerate(todo):
                n, ahead = UNITS * t + i, i + 2
                if ahead < UNITS:
                    hidden_sums(t, k, n + 2, *todo[ahead])
                elif more:
                    hidden_sums(t + 1, 1 - k, n + 2, *todo[ahead - UNITS])
                output_sums(t, k, n, g, c, q)

        for i in range(2):
            hidden_sums(0, 0, i, *units()[i])
        each_slot(pe, slot)

    def split_hi(act, t, k):
        act.wait_ge(w_loaded[k], slot_loads // 2 * (t - k) + slot_loads)
        wait_from(act, out_done, UNITS * (t - 1))
        copy_hi(act, in_h[:, k, :, :], in_raw[:, :, :])
        copy_hi(act, out_h[:, k, :, :], out_raw[:, :, :])
        if cfg.biased:
            act.activation(bias[:, k, :, :], bias_raw[:, :, :], ACT.Copy)
        copy_hi(act, picked[:, k, :], pick_raw[:, :]).then_inc(w_hi, 1)

    def scalar(act):
        enter(act)
        act.wait_ge(aux_loaded, aux)
        copy_hi(act, r_h[:, :, :], r_raw[:, :, :]).then_inc(router_hi, 1)
        if cfg.biased:
            copy_hi(act, b2_h[:, :], b2_raw[:, :]).then_inc(b2_hi, 1)

        def turn(b, k):
            act.wait_ge(xt_done, b + 1)
            copy_hi(act, xT_h[:, :, bass.ds(b * S, S)], ps_a[k][:, 0:D].rearrange("p (c s) -> p c s", c=DC)).then_inc(xt_hi, 1)

        tiles(act, turn)
        split_hi(act, 0, 0)
        for g in range(NG):
            act.wait_ge(logits_done, g + 1)
            act.activation(logitsT[:, g * GT:(g + 1) * GT], ps_u[g % 2][0:E, :], ACT.Copy).then_inc(logits_copied, 1)
        act.wait_ge(exp_in, 1)
        act.activation(ex[:, :, :], ex[:, :, :], ACT.Exp).then_inc(exp_done, 1)
        for g in range(NG):
            act.wait_ge(turned, g + 2)
            copy_hi(act, cellT[:, g * GT:(g + 1) * GT], ps_u[g % 2][0:cells, :]).then_inc(cellT_done, 1)

        def silu(k, n, g, c, q):
            act.wait_ge(in_done, n + 1)
            wait_from(act, gated, n - 1)
            R = cfg.chunks[c]
            offset = dict(bias=bias[0:R, k, 0, c:c + 1]) if cfg.biased else {}
            act.activation(s[0:R, q, :], ps_a[q][0:R, :], ACT.Silu, **offset).then_inc(silu_done, 1)

        def slot(t, k, more):
            todo = units()
            for i, (g, c, q) in enumerate(todo):
                n = UNITS * t + i
                if i + 1 < UNITS:
                    silu(k, n + 1, *todo[i + 1])
                elif more:
                    silu(1 - k, n + 1, *todo[0])
                act.wait_ge(h_done, n + 1)
                wait_from(act, out_done, n - 1)
                R = cfg.chunks[c]
                copy_hi(act, h_h[0:R, q, :], h[0:R, q, :]).then_inc(h_hi, 1)
                if i == 2 and more:
                    split_hi(act, t + 1, 1 - k)

        silu(0, 0, 0, 0, 0)
        each_slot(act, slot)

    def gpsimd(pool):
        clear(pool)
        enter(pool)
        stats_gpsimd(pool)
        pool.wait_ge(router_hi, 1)
        sub_lo(pool, r_l[:, :, :], r_raw[:, :, :], r_h[:, :, :]).then_inc(router_lo, 1)
        if cfg.biased:
            pool.wait_ge(b2_hi, 1)
            sub_lo(pool, b2_l[:, :], b2_raw[:, :], b2_h[:, :]).then_inc(b2_lo, 1)

        def split_lo(t, k):
            pool.wait_ge(w_hi, t + 1)
            sub_lo(pool, in_l[:, k, :, :], in_raw[:, :, :], in_h[:, k, :, :])
            sub_lo(pool, out_l[:, k, :, :], out_raw[:, :, :], out_h[:, k, :, :]).then_inc(w_lo, 1)

        split_lo(0, 0)

        def slot(t, k, more):
            for i, (g, c, q) in enumerate(units()):
                n = UNITS * t + i
                pool.wait_ge(h_hi, n + 1)
                wait_from(pool, out_done, n - 1)
                R = cfg.chunks[c]
                sub_lo(pool, h_l[0:R, q, :], h[0:R, q, :], h_h[0:R, q, :]).then_inc(h_lo, 1)
                if i == 2 and more:
                    split_lo(t + 1, 1 - k)

        each_slot(pool, slot)

    def vector(dve):
        enter(dve)
        stats_vector(dve)
        dve.wait_ge(rstd_done, 1)

        def turn(b, k):
            wait_from(dve, xt_done, b - 1)
            normalise(dve, xn[:, k, :], b).then_inc(xn_done, 1)
            dve.wait_ge(xt_hi, b + 1)
            to = xT_l[:, :, bass.ds(b * S, S)]
            sub_lo(dve, to, ps_a[k][:, 0:D].rearrange("p (c s) -> p c s", c=DC), xT_h[:, :, bass.ds(b * S, S)]).then_inc(xt_lo, 1)

        tiles(dve, turn)

        done = [0]

        def chain(ins):
            done[0] += 1
            ins.then_inc(step, 1)
            dve.wait_ge(step, done[0])

        def wide(v, n=E):
            return v.unsqueeze(2).to_broadcast([P, B, n])

        def choose(values):
            for b in range(B):
                last = dve.max(eight[:, b, :], values[:, b, :])
            chain(last)
            least = wide(eight[:, :, cfg.top - 1])
            dve.tensor_tensor(equal[:, :, :], values[:, :, :], least, ALU.is_equal)
            chain(dve.tensor_tensor(above[:, :, :], values[:, :, :], least, ALU.is_gt))
            chain(dve.tensor_reduce(row[:, :], above[:, :, :], AX.X, ALU.add))
            chain(dve.tensor_scalar(row[:, :], row[:, :], -1.0, float(cfg.top), ALU.mult, ALU.add))
            src, shift, spare = equal, 1, [run0, run1]
            while shift < E:
                dst = spare[0]
                dve.tensor_copy(dst[:, :, 0:shift], src[:, :, 0:shift])
                chain(dve.tensor_tensor(dst[:, :, shift:E], src[:, :, shift:E], src[:, :, 0:E - shift], ALU.add))
                src, spare, shift = dst, spare[::-1], 2 * shift
            dst = spare[0]
            chain(dve.tensor_tensor(dst[:, :, :], src[:, :, :], wide(row[:, :]), ALU.is_le))
            chain(dve.tensor_tensor(dst[:, :, :], dst[:, :, :], equal[:, :, :], ALU.mult))
            chain(dve.tensor_tensor(above[:, :, :], above[:, :, :], dst[:, :, :], ALU.add))

        dve.wait_ge(turned, 1)
        chain(dve.tensor_copy(logits[:, :, :], ps_c[0][:, 0:B * E].rearrange("p (b e) -> p b e", e=E)))
        chain(dve.tensor_reduce(row2[:, :], logits[:, :, :], AX.X, ALU.max))
        dve.tensor_tensor(ex[:, :, :], logits[:, :, :], wide(row2[:, :]), ALU.subtract).then_inc(exp_in, 1)
        if not cfg.biased:
            choose(logits)
        dve.wait_ge(exp_done, 1)
        if not cfg.biased:
            chain(dve.tensor_tensor(ex[:, :, :], ex[:, :, :], above[:, :, :], ALU.mult))
        chain(dve.tensor_reduce(row2[:, :], ex[:, :, :], AX.X, ALU.add))
        chain(dve.reciprocal(row2[:, :], row2[:, :]))
        chain(dve.tensor_tensor(prob[:, :, :], ex[:, :, :], wide(row2[:, :]), ALU.mult))
        if cfg.biased:
            dve.wait_ge(aux_loaded, aux)
            chain(dve.tensor_tensor(key[:, :, :], prob[:, :, :], router_b[:, :].unsqueeze(1).to_broadcast(table), ALU.add))
            choose(key)
            chain(dve.tensor_tensor(prob[:, :, :], prob[:, :, :], above[:, :, :], ALU.mult))
        chain(dve.tensor_copy(c_h[:, :, :], prob[:, :, :]))
        dve.tensor_copy(cell[:, :, 0:E], c_h[:, :, :].bitcast(F32))
        if cfg.biased:
            dve.memset(cell[:, :, 2 * E:cells], 1.0)
        dve.tensor_tensor(cell[:, :, E:2 * E], prob[:, :, :], c_h[:, :, :].bitcast(F32), ALU.subtract).then_inc(cell_done, 1)
        if cfg.biased:
            for pair in range(B // 2):
                dve.wait_ge(bias_done, pair + 1)
                two = x[:, 2 * pair:2 * pair + 2, :]
                dve.tensor_tensor(two, two, ps_y[pair % 2][:, :].rearrange("p (b d) -> p b d", b=2), ALU.add).then_inc(bias_added, 1)
            dve.wait_ge(bias_added, B // 2)

        def gate_unit(k, n, g, c, q):
            R = cfg.chunks[c]
            dve.wait_ge(silu_done, n + 1)
            if cfg.limit is not None:
                dve.tensor_scalar(s[0:R, q, :], s[0:R, q, :], -cfg.limit, cfg.limit, ALU.max, ALU.min).then_inc(clipped, 1)
                dve.wait_ge(clipped, n + 1)
                dve.tensor_tensor(m[0:R, q, :], ps_u[q][0:R, :], s[0:R, q, :], ALU.mult).then_inc(gated, 1)
            else:
                dve.scalar_tensor_tensor(out=m[0:R, q, :], in0=ps_u[q][0:R, :], scalar=bias[0:R, k, 1, c:c + 1],
                                         in1=s[0:R, q, :], op0=ALU.add, op1=ALU.mult).then_inc(gated, 1)
            dve.wait_ge(gated, n + 1)
            wait_from(dve, h_lo, n - 1)
            dve.tensor_tensor(h[0:R, q, :], m[0:R, q, :], ps_c[q][0:R, :], ALU.mult).then_inc(h_done, 1)

        def add_group(t, g):
            dve.wait_ge(out_done, UNITS * t + NC * (g + 1))
            for j in range(2):
                two = x[:, 4 * g + 2 * j:4 * g + 2 * j + 2, :]
                last = dve.tensor_tensor(two, two, ps_y[j][:, :].rearrange("p (b d) -> p b d", b=2), ALU.add)
            last.then_inc(added, 1)

        def slot(t, k, more):
            for i, (g, c, q) in enumerate(units()):
                gate_unit(k, UNITS * t + i, g, c, q)
                if c == 0:
                    if g > 0:
                        add_group(t, g - 1)
                    elif not (isinstance(t, int) and t == 0):
                        add_group(t - 1, NG - 1)

        each_slot(dve, slot)
        add_group(NS - 1, NG - 1)

    return (sync, tensor, scalar, gpsimd, vector), (added, NG * NS)


def experts0(core, ctx, gate):
    return expert_layer(core, ctx, gate, Layer0)


def experts1(core, ctx, gate):
    return expert_layer(core, ctx, gate, Layer1)


PHASES = (attention0, convolution0, experts0, attention1, convolution1, experts1,)


def build(nc, dram, out):
    with ExitStack() as stack:
        core = Core(nc, stack, dram)
        programs, gate = [], None
        for phase in PHASES:
            with ExitStack() as ctx:
                engines, done = phase(core, ctx) if gate is None else phase(core, ctx, gate)
            programs.append(engines)
            gate = done

        with nc.Block() as block:
            @block.sync
            def _(sp):
                for sync, _, _, _, _ in programs:
                    sync(sp)
                sp.wait_ge(*gate)
                sp.dma_start(out.rearrange("b s d -> s b d"), core.x[:, :, :]).then_inc(core.stored, 16)
                sp.wait_ge(core.stored, 16)

            @block.tensor
            def _(pe):
                for _, tensor, _, _, _ in programs:
                    tensor(pe)

            @block.scalar
            def _(act):
                for _, _, scalar, _, _ in programs:
                    scalar(act)

            @block.gpsimd
            def _(pool):
                for _, _, _, gpsimd, _ in programs:
                    gpsimd(pool)

            @block.vector
            def _(dve):
                for _, _, _, _, vector in programs:
                    vector(dve)


def lay_out(inputs):
    a = {k: np.asarray(v) for k, v in inputs.items()}
    out = {k: a[k] for k in ("x", "ctx_2048", "fside_S2_0", "L0_attn_Wq", "L0_attn_Wk", "L0_attn_Wv", "L0_attn_Wo",
                             "L1_xattn_D", "L1_attn_W_q", "L1_attn_W_kv", "L0_ffn_gate_b", "L1_ffn_Wr")}
    out["ctxT"] = a["ctx_2048"].reshape(B * S, D).T
    out["L1_WoT"] = a["L1_attn_W_o"].T
    for name, taps in (("taps0", a["L0_xattn_k"]), ("taps1", a["L1_xattn_ssm_kernel"])):
        padded = np.zeros((CH, 2 * D), np.float32)
        padded[:, D:] = taps
        out[name] = padded[:, ::-1]

    def hidden_first(w):
        return w.reshape(-1, w.shape[0] // NS, DC, P).transpose(0, 3, 2, 1)

    def by_chunk(v, cfg):
        NC, n = len(cfg.chunks), sum(cfg.chunks)
        full = np.zeros((cfg.slots, NC * P) + v.shape[1:], np.float32)
        full[:, :n] = v.reshape((cfg.slots, n) + v.shape[1:])
        full = full.reshape((cfg.slots, NC, P) + v.shape[1:])
        return np.moveaxis(full, 2, 1)

    NS = Layer0.slots
    w1, w3 = (np.concatenate([a["L0_ffn_" + n].reshape(-1, D), a["L0_ffn_ws" + n[1]]]) for n in ("w1", "w3"))
    w2 = np.concatenate([a["L0_ffn_w2"].transpose(0, 2, 1).reshape(-1, D), a["L0_ffn_ws2"].T])
    out["L0_in"] = np.concatenate([hidden_first(w1), hidden_first(w3)], -1)
    out["L0_out"] = by_chunk(w2, Layer0)
    out["L0_b13"] = np.stack([by_chunk(np.concatenate([a["L0_ffn_b" + n].reshape(-1), a["L0_ffn_bs" + n]]), Layer0)
                              for n in "13"], 2)
    out["L0_b2"] = np.concatenate([a["L0_ffn_b2"], a["L0_ffn_b2"], a["L0_ffn_bs2"][None]])
    out["L0_routerT"] = a["L0_ffn_gate_w"].T
    NS = Layer1.slots
    inputs1 = [a["L1_ffn_" + n].reshape(NS, DC, P, -1).transpose(0, 2, 1, 3) for n in ("Wg", "Wu")]
    out["L1_in"] = np.concatenate(inputs1, -1)
    out["L1_out"] = by_chunk(a["L1_ffn_Wd"].reshape(-1, D), Layer1)
    return out


def kernel(**inputs):
    import concourse.bacc as bacc
    from concourse.bass_utils import run_bass_kernel_spmd

    nc = bacc.Bacc("TRN2", target_bir_lowering=False, num_devices=1)
    arrays, dram = {}, {}
    for name, a in {**lay_out(inputs), **constants()}.items():
        a = np.ascontiguousarray(a)
        arrays["in_" + name] = a
        dram[name] = nc.dram_tensor("in_" + name, a.shape, mybir.dt.from_np(a.dtype), kind="ExternalInput").ap()
    out = nc.dram_tensor("out_x", (B, S, D), F32, kind="ExternalOutput").ap()
    build(nc, dram, out)
    r = run_bass_kernel_spmd(nc, [arrays], core_ids=[0])
    return r.results[0]["out_x"]
```

```python
from contextlib import ExitStack

import numpy as np
import concourse.bass as bass
from concourse import mybir

F32 = mybir.dt.float32
F32R = mybir.dt.float32r
ALU = mybir.AluOpType
ACT = mybir.ActivationFunctionType
AX = mybir.AxisListType

P = 128
B = 16
S = 128
D = 256
DC = D // P
EPS = 1e-5

HEADS, KV, HD = 16, 4, 128
REP = HEADS // KV
GQ = REP * HD
GC = GQ + 2 * HD
MASKED = -1e30


def three_pass(pe, out, lhs, rhs, start, stop):
    (lh, ll), (rh, rl) = lhs, rhs
    pe.matmul(out, lh, rh, start=start, stop=False)
    pe.matmul(out, lh, rl, start=False, stop=False)
    return pe.matmul(out, ll, rh, start=False, stop=stop)


def wait_from(eng, semaphore, count):
    if not isinstance(count, int) or count > 0:
        eng.wait_ge(semaphore, count)


def copy_hi(act, dst, src):
    return act.activation(dst, src, ACT.Copy)


def sub_lo(eng, dst, src, hi):
    return eng.tensor_tensor(dst, src, hi.bitcast(F32), ALU.subtract)


def inverse_root(dve, out, scratch, a, root, waits):
    waits(dve.reciprocal(out, root))
    waits(dve.tensor_tensor(scratch, out, out, ALU.mult))
    waits(dve.tensor_tensor(scratch, scratch, a, ALU.mult))
    waits(dve.tensor_scalar(scratch, scratch, -0.5, 1.5, ALU.mult, ALU.add))
    return dve.tensor_tensor(out, out, scratch, ALU.mult)


class Core:

    def __init__(self, nc, stack, dram):
        self.nc, self.stack, self.dram = nc, stack, dram
        self.x = self.sbuf(stack, "x", [P, B, D])
        self.ctxT = self.sbuf(stack, "ctxT_sb", [P, DC, B * S])
        self.ident = self.sbuf(stack, "ident_sb", [P, P])
        self.stats = self.sbuf(stack, "stats", [P, B, 6])
        self.kinds, self.phases_normed = {}, 0
        self.minus_half = self.sbuf(stack, "minus_half", [P, 1])
        self.three_halves = self.sbuf(stack, "three_halves", [P, 1])
        (self.x0_loaded, self.x_loaded, self.const_loaded, self.ctx_loaded, self.half_set,
         self.stats_done, self.stored) = self.sems(
             "", "x0_loaded x_loaded const_loaded ctx_loaded half_set stats_done stored")

    def sems(self, tag, names):
        return [self.stack.enter_context(self.nc.semaphore(tag + n)) for n in names.split()]

    def layer_sems(self, kind, names):
        of_kind = self.kinds.setdefault(kind, {})
        if names not in of_kind:
            of_kind[names] = self.sems(kind, names)
        return of_kind[names]

    def clear(self, pool, kind):
        for semaphores in self.kinds[kind].values():
            for s in semaphores:
                pool.sem_clear(s)

    def tile_stats(self, dve, b, added, count):
        dve.wait_ge(added, count)
        tile_stats = self.stats[:, bass.ds(b, 1), :].rearrange("p a s -> p (a s)")
        dve.bn_stats(tile_stats, self.tile(b)).then_inc(self.stats_done, 1)

    def sbuf(self, ctx, name, shape, dt=F32):
        return ctx.enter_context(self.nc.sbuf_tensor(name, shape, dt))

    def psum(self, ctx, name, shape, dt=F32):
        return ctx.enter_context(self.nc.psum_tensor(name, shape, dt))

    def tile(self, b):
        return self.x[:, bass.ds(b, 1), :].rearrange("p a d -> p (a d)")


def pipeline(eng, stages, looped=True):
    deepest = max(lag for lag, _ in stages)
    first = min(lag for lag, _ in stages)

    start = deepest + 2
    loops = max(0, (B + first - start) // 2) if looped else 0
    for s in range(first, start):
        for lag, stage in stages:
            if 0 <= s - lag < B:
                stage(s - lag, (s - lag) % 2)
    if loops:
        with eng.Fori(start, start + 2 * loops - 1, 2) as s:
            for j in range(2):
                for lag, stage in stages:
                    stage(s + (j - lag), (start + j - lag) % 2)
    for s in range(start + 2 * loops, B + deepest):
        for lag, stage in stages:
            if 0 <= s - lag < B:
                stage(s - lag, (s - lag) % 2)


def constants():
    half = HD // 2
    inv = (1.0 / 10000.0 ** (np.arange(half, dtype=np.float64) / half))
    ang = np.outer(np.arange(S), inv)
    cos = np.concatenate([np.cos(ang)] * 2, -1)
    sin = np.concatenate([-np.sin(ang), np.sin(ang)], -1)
    s = (np.arange(S) + 32.0) / 64.0
    xs = np.where(np.arange(HD) % 2 == 0, s[:, None], 1.0 / s[:, None])
    q = xs / np.sqrt(HD)
    rope = np.concatenate([cos * q, sin * q, cos / xs, sin / xs], -1)
    mask = np.where(np.arange(S)[None, :] > np.arange(S)[:, None], MASKED, 0.0)
    forward, inverse = transforms()
    return {
        "forward": forward,
        "inverse": inverse,
        "before": np.triu(np.ones((S, S), np.float32)),
        "pick0": pick(Layer0),
        "pick1": pick(Layer1),
        "same_head": np.kron(np.eye(S // 8), np.ones((8, 8))).astype(np.float32),
        "ident": np.eye(P, dtype=np.float32),
        "rope": rope.astype(np.float32),
        "mask": mask.astype(np.float32),
    }


def attention0(core, ctx):
    dram, x, ident, minus_half = core.dram, core.x, core.ident, core.minus_half
    x0_loaded, x_loaded, const_loaded, half_set = core.x0_loaded, core.x_loaded, core.const_loaded, core.half_set
    w_h = core.sbuf(ctx, "a0_w_h", [P, DC, KV, GC], F32R)
    w_l = core.sbuf(ctx, "a0_w_l", [P, DC, KV, GC], F32R)
    wo_h = core.sbuf(ctx, "a0_wo_h", [P, HEADS, D], F32R)
    wo_l = core.sbuf(ctx, "a0_wo_l", [P, HEADS, D], F32R)
    w_raw = core.sbuf(ctx, "a0_w_raw", [P, KV, DC, GC])
    wo_raw = core.sbuf(ctx, "a0_wo_raw", [P, KV, REP, D])
    rope = core.sbuf(ctx, "a0_rope", [P, 4, HD])
    mask = core.sbuf(ctx, "a0_mask", [P, S])
    stats = core.sbuf(ctx, "a0_stats", [P, 6])
    mv = core.sbuf(ctx, "a0_mv", [P, 2])
    vare = core.sbuf(ctx, "a0_vare", [P, 1])
    rstd = core.sbuf(ctx, "a0_rstd", [P, 1])
    xn = core.sbuf(ctx, "a0_xn", [P, D])
    xT_h = core.sbuf(ctx, "a0_xT_h", [P, DC, P], F32R)
    xT_l = core.sbuf(ctx, "a0_xT_l", [P, DC, P], F32R)
    rc = core.sbuf(ctx, "a0_rc", [P, GQ + HD])
    rs = core.sbuf(ctx, "a0_rs", [P, GQ + HD])
    qk = core.sbuf(ctx, "a0_qk", [P, GQ + HD])
    v = core.sbuf(ctx, "a0_v", [P, KV, HD])
    v_h = core.sbuf(ctx, "a0_v_h", [P, KV, HD], F32R)
    v_l = core.sbuf(ctx, "a0_v_l", [P, KV, HD], F32R)
    qkT = core.sbuf(ctx, "a0_qkT", [P, 2, GQ + HD])
    masked = core.sbuf(ctx, "a0_masked", [P, REP, S])
    nmax = core.sbuf(ctx, "a0_nmax", [P, 2, REP])
    rsum = core.sbuf(ctx, "a0_rsum", [P, 2, REP])
    rinv = core.sbuf(ctx, "a0_rinv", [P, 2, REP])
    pr = core.sbuf(ctx, "a0_pr", [P, 2, REP, S])
    pT_h = core.sbuf(ctx, "a0_pT_h", [P, REP * S], F32R)
    pT_l = core.sbuf(ctx, "a0_pT_l", [P, REP * S], F32R)
    oT_h = core.sbuf(ctx, "a0_oT_h", [P, REP, S], F32R)
    oT_l = core.sbuf(ctx, "a0_oT_l", [P, REP, S], F32R)

    ps_q = core.psum(ctx, "a0_ps_q", [P, 512])
    ps_kvx = core.psum(ctx, "a0_ps_kvx", [P, 512])
    ps_t = core.psum(ctx, "a0_ps_t", [P, 1024])
    ps_s = core.psum(ctx, "a0_ps_s", [P, 512])
    ps_pT = core.psum(ctx, "a0_ps_pT", [P, 512])
    ps_oT = core.psum(ctx, "a0_ps_oT", [P, 512])
    ps_y = core.psum(ctx, "a0_ps_y", [P, 512])
    ps_kv, ps_xT = ps_kvx[:, 0:2 * HD], ps_kvx[:, 2 * HD:512]

    w_loaded = core.sems("a0_", " ".join(f"w_loaded{g}" for g in range(KV)))
    wo_loaded = core.sems("a0_", " ".join(f"wo_loaded{g}" for g in range(KV)))
    (w_hi, w_lo, wo_hi, wo_lo, stat_done, var_done, rstd_done, xn_done,
     xt_done, xt_hi, xt_lo, proj_done, rope_mul, roped, v_done, v_hi, v_lo, tq_done, qkT_done,
     scores_done, mask_done, max_done, exp_done, recip_done, norm_done, pt_done, pt_hi, pt_lo, pv_done,
     ot_hi, ot_lo, wo_done, y_added) = core.sems("a0_", (
         "w_hi w_lo wo_hi wo_lo stat_done var_done rstd_done xn_done "
         "xt_done xt_hi xt_lo proj_done rope_mul roped v_done v_hi v_lo tq_done qkT_done "
         "scores_done mask_done max_done exp_done recip_done norm_done pt_done pt_hi pt_lo pv_done "
         "ot_hi ot_lo wo_done y_added"))

    w_q = dram["L0_attn_Wq"].rearrange("(c p) n -> p c n", p=P)
    w_k = dram["L0_attn_Wk"].rearrange("(c p) n -> p c n", p=P)
    w_v = dram["L0_attn_Wv"].rearrange("(c p) n -> p c n", p=P)
    w_o = dram["L0_attn_Wo"].rearrange("(h p) n -> p h n", p=P)


    def attn0_sync(sp):
        xs = dram["x"].rearrange("b s d -> s b d")
        sp.dma_start(x[:, 0:1, :], xs[:, 0:1, :]).then_inc(x0_loaded, 16)

        def load_out(g):
            sp.dma_start(wo_raw[:, g, :, :], w_o[:, g * REP:(g + 1) * REP, :]).then_inc(wo_loaded[g], 16)

        for g in range(KV):
            sp.dma_start(w_raw[:, g, :, 0:GQ], w_q[:, :, g * GQ:(g + 1) * GQ]).then_inc(w_loaded[g], 16)
            sp.dma_start(w_raw[:, g, :, GQ:GQ + HD], w_k[:, :, g * HD:(g + 1) * HD]).then_inc(w_loaded[g], 16)
            sp.dma_start(w_raw[:, g, :, GQ + HD:GC], w_v[:, :, g * HD:(g + 1) * HD]).then_inc(w_loaded[g], 16)
            if g == 0:
                sp.dma_start(ident[:, :], dram["ident"]).then_inc(const_loaded, 16)
                sp.dma_start(rope[:, :, :], dram["rope"].rearrange("s (a d) -> s a d", a=4)).then_inc(const_loaded, 16)
                sp.dma_start(mask[:, :], dram["mask"]).then_inc(const_loaded, 16)
            if g == 2:
                sp.dma_start(x[:, 1:B, :], xs[:, 1:B, :]).then_inc(x_loaded, 16)
            load_out(g)
        sp.dma_start(core.ctxT[:, :, :], dram["ctxT"].rearrange("(c p) t -> p c t", p=P)).then_inc(core.ctx_loaded, 16)

    def attn0_tensor(pe):
        def transpose_x(b, n):
            pe.wait_ge(xn_done, b + 1)
            if n is not None:
                pe.wait_ge(v_done, n)
            for c in range(DC):
                last = pe.transpose(ps_xT[:, c * P:(c + 1) * P], xn[:, c * P:(c + 1) * P], ident[:, :])
            last.then_inc(xt_done, 1)

        def project(b, g, n):
            if isinstance(n, int) and n < KV:
                pe.wait_ge(w_hi, g + 1)
                pe.wait_ge(w_lo, g + 1)
            if g == 0:
                pe.wait_ge(xt_hi, b + 1)
                pe.wait_ge(xt_lo, b + 1)
            for lo, hi, dst, read in ((0, GQ, ps_q[:, :], rope_mul), (GQ, GC, ps_kv, v_done)):
                wait_from(pe, read, n)
                for c in range(DC):
                    last = three_pass(pe, dst, (xT_h[:, c, :], xT_l[:, c, :]),
                                      (w_h[:, c, g, lo:hi], w_l[:, c, g, lo:hi]), c == 0, c == DC - 1)
            last.then_inc(proj_done, 1)

        def transpose_qk(g, n):
            pe.wait_ge(roped, n + 1)
            wait_from(pe, qkT_done, n)
            for h in range(REP + 1):
                last = pe.transpose(ps_t[:, h * P:(h + 1) * P], qk[:, h * HD:(h + 1) * HD], ident[:, :])
            last.then_inc(tq_done, 1)

        def scores(g, m):
            pe.wait_ge(qkT_done, m + 1)
            wait_from(pe, mask_done, m)
            k = slice(GQ, GQ + HD)
            for h in range(REP):
                q = slice(h * HD, (h + 1) * HD)
                last = pe.matmul(ps_s[:, h * S:(h + 1) * S], qkT[:, g % 2, q], qkT[:, g % 2, k], start=True,
                                 stop=True)
            last.then_inc(scores_done, 1)

        def transpose_p(g, m):
            pe.wait_ge(norm_done, m + 1)
            wait_from(pe, pt_lo, m)
            for h in range(REP):
                last = pe.transpose(ps_pT[:, h * P:(h + 1) * P], pr[:, g % 2, h, :], ident[:, :])
            last.then_inc(pt_done, 1)

        def weigh_values(g, m):
            pe.wait_ge(pt_hi, m + 1)
            pe.wait_ge(pt_lo, m + 1)
            pe.wait_ge(v_hi, m + 1)
            pe.wait_ge(v_lo, m + 1)
            wait_from(pe, ot_lo, m)
            three_pass(pe, ps_oT[:, :], (v_h[:, g, :], v_l[:, g, :]), (pT_h[:, :], pT_l[:, :]),
                       True, True).then_inc(pv_done, 1)

        def project_out(b, g, m):
            if isinstance(m, int) and m < KV:
                pe.wait_ge(wo_hi, g + 1)
                pe.wait_ge(wo_lo, g + 1)
            pe.wait_ge(ot_hi, m + 1)
            pe.wait_ge(ot_lo, m + 1)
            if g == 0:
                wait_from(pe, y_added, b)
            for h in range(REP):
                last = three_pass(pe, ps_y[:, 0:D], (oT_h[:, h, :], oT_l[:, h, :]),
                                  (wo_h[:, g * REP + h, :], wo_l[:, g * REP + h, :]),
                                  g == 0 and h == 0, g == KV - 1 and h == REP - 1)
            last.then_inc(wo_done, 1)

        def sequence(b, head, tail):
            for g in range(KV):
                m = KV * b + g
                if g == KV - 2 and not tail:
                    transpose_x(b + 1, m + 2)
                scores(g, m)
                if not (head and g == 0):
                    transpose_p((g - 1) % KV, m - 1)
                if not (tail and g >= KV - 2):
                    project(b + (g + 2) // KV, (g + 2) % KV, m + 2)
                if not (tail and g == KV - 1):
                    transpose_qk((g + 1) % KV, m + 1)
                if not (head and g == 0):
                    weigh_values((g - 1) % KV, m - 1)
                if not (head and g < 2):
                    project_out(b + (g - 2) // KV, (g - 2) % KV, m - 2)

        pe.wait_ge(const_loaded, 48)
        transpose_x(0, None)
        project(0, 0, 0)
        transpose_qk(0, 0)
        project(0, 1, 1)
        sequence(0, True, False)
        with pe.Fori(1, B - 1) as b:
            sequence(b, False, False)
        sequence(B - 1, False, True)
        transpose_p(KV - 1, KV * B - 1)
        project_out(B - 1, KV - 2, KV * B - 2)
        weigh_values(KV - 1, KV * B - 1)
        project_out(B - 1, KV - 1, KV * B - 1)

    def attn0_scalar(act):
        def copy_hi(dst, src, done):
            act.activation(dst, src, ACT.Copy).then_inc(done, 1)

        def output_hi(m):
            act.wait_ge(pv_done, m + 1)
            wait_from(act, wo_done, m)
            copy_hi(oT_h[:, :, :], ps_oT[:, :], ot_hi)

        def exps(g, m):
            act.wait_ge(max_done, m + 1)
            wait_from(act, pt_done, m - 1)
            for h in range(REP):
                last = act.activation(pr[:, g % 2, h, :], masked[:, h, :], ACT.Exp,
                                      bias=nmax[:, g % 2, h:h + 1], accum_out=rsum[:, g % 2, h:h + 1])
            last.then_inc(exp_done, 1)

        def x_hi(b):
            act.wait_ge(xt_done, b + 1)
            copy_hi(xT_h[:, :, :], ps_xT, xt_hi)

        def copy_probs(m):
            act.wait_ge(pt_done, m + 1)
            wait_from(act, pv_done, m)
            copy_hi(pT_h[:, :], ps_pT[:, :], pt_hi)

        def values_hi(g, n):
            act.wait_ge(v_done, n + 1)
            wait_from(act, pv_done, n - 3)
            copy_hi(v_h[:, g, :], v[:, g, :], v_hi)

        def copy_qk(g, n):
            act.wait_ge(tq_done, n + 1)
            wait_from(act, scores_done, n - 1)
            act.activation(qkT[:, g % 2, :], ps_t[:, 0:GQ + HD], ACT.Copy).then_inc(qkT_done, 1)

        def split_in(g):
            act.wait_ge(w_loaded[g], 48)
            copy_hi(w_h[:, :, g, :], w_raw[:, g, :, :], w_hi)

        def split_out(g):
            act.wait_ge(wo_loaded[g], 16)
            copy_hi(wo_h[:, g * REP:(g + 1) * REP, :], wo_raw[:, g, :, :], wo_hi)

        def sequence(b, head, tail):
            for g in range(KV):
                m = KV * b + g
                if g == KV - 2 and not tail:
                    x_hi(b + 1)
                if not (head and g < 2):
                    output_hi(m - 2)
                if not (head and g == 0):
                    copy_probs(m - 1)
                exps(g, m)
                if not (tail and g == KV - 1):
                    copy_qk((g + 1) % KV, m + 1)
                    values_hi((g + 1) % KV, m + 1)
                if head and g == 0:
                    split_in(3)
                if head and g < KV - 1:
                    split_out(g + 1)

        x_hi(0)
        split_in(0)
        split_in(1)
        split_out(0)
        copy_qk(0, 0)
        values_hi(0, 0)
        split_in(2)
        sequence(0, True, False)
        with act.Fori(1, B - 1) as b:
            sequence(b, False, False)
        sequence(B - 1, False, True)
        output_hi(KV * B - 2)
        copy_probs(KV * B - 1)
        output_hi(KV * B - 1)

    def attn0_gpsimd(pool):
        def rstd_of(b):
            pool.wait_ge(var_done, b + 1)
            wait_from(pool, xn_done, b)
            pool.tensor_tensor(rstd[:, :], vare[:, :], minus_half[:, :], ALU.pow).then_inc(rstd_done, 1)

        def add_rotated(n):
            pool.wait_ge(rope_mul, n + 1)
            wait_from(pool, tq_done, n)
            pool.tensor_tensor(qk[:, :], rc[:, :], rs[:, :], ALU.add).then_inc(roped, 1)

        def values_lo(g, n):
            pool.wait_ge(v_hi, n + 1)
            wait_from(pool, pv_done, n - 3)
            sub_lo(pool, v_l[:, g, :], v[:, g, :], v_h[:, g, :]).then_inc(v_lo, 1)

        def normalise(g, m):
            pool.wait_ge(recip_done, m + 1)
            pool.tensor_tensor(pr[:, g % 2, :, :], pr[:, g % 2, :, :],
                               rinv[:, g % 2, :].unsqueeze(2).to_broadcast([P, REP, S]),
                               ALU.mult).then_inc(norm_done, 1)

        def split_out(g):
            pool.wait_ge(wo_hi, g + 1)
            gs = slice(g * REP, (g + 1) * REP)
            sub_lo(pool, wo_l[:, gs, :], wo_raw[:, g, :, :], wo_h[:, gs, :]).then_inc(wo_lo, 1)

        def sequence(b, head, tail):
            for g in range(KV):
                m = KV * b + g
                if g == 1 and not tail:
                    rstd_of(b + 1)
                normalise(g, m)
                if not (tail and g == KV - 1):
                    values_lo((g + 1) % KV, m + 1)
                if not (tail and g >= KV - 2):
                    add_rotated(m + 2)
                if head and g < KV - 1:
                    split_out(g + 1)

        pool.memset(core.three_halves[:, :], 1.5)
        pool.memset(minus_half[:, :], -0.5).then_inc(half_set, 1)
        pool.wait_ge(half_set, 1)
        rstd_of(0)
        add_rotated(0)
        values_lo(0, 0)
        split_out(0)
        add_rotated(1)
        sequence(0, True, False)
        with pool.Fori(1, B - 1) as b:
            sequence(b, False, False)
        sequence(B - 1, False, True)

    def attn0_vector(dve):
        def lo(dst, src, hi, done):
            dve.tensor_tensor(dst, src, hi.bitcast(F32), ALU.subtract).then_inc(done, 1)

        def stats_x(b):
            tile = x[:, bass.ds(b, 1), :].rearrange("p a d -> p (a d)")
            dve.bn_stats(stats[:, :], tile).then_inc(stat_done, 1)

        def aggregate_x():
            dve.bn_aggr(mv[:, :], stats[:, :]).then_inc(stat_done, 1)

        def variance_x(b):
            dve.wait_ge(stat_done, 2 * b + 2)
            dve.tensor_scalar(vare[:, :], mv[:, 1:2], EPS, None, ALU.add).then_inc(var_done, 1)

        def norm_x(b):
            tile = x[:, bass.ds(b, 1), :].rearrange("p a d -> p (a d)")
            dve.wait_ge(rstd_done, b + 1)
            wait_from(dve, xt_done, b)
            dve.tensor_scalar(xn[:, :], tile, mv[:, 0:1], rstd[:, 0:1], ALU.subtract,
                              ALU.mult).then_inc(xn_done, 1)

        def x_lo(b):
            dve.wait_ge(xt_hi, b + 1)
            lo(xT_l[:, :, :].rearrange("p c s -> p (c s)"), ps_xT,
               xT_h[:, :, :].rearrange("p c s -> p (c s)"), xt_lo)

        def split_in(g):
            dve.wait_ge(w_hi, g + 1)
            sub_lo(dve, w_l[:, :, g, :], w_raw[:, g, :, :], w_h[:, :, g, :]).then_inc(w_lo, 1)

        def take_projected(g, n):
            dve.wait_ge(proj_done, n + 1)
            wait_from(dve, roped, n)
            for o, w, src, cos, sin in ((GQ, 1, ps_kv[:, 0:HD], rope[:, 2, :], rope[:, 3, :]),
                                        (0, REP, ps_q[:, :], rope[:, 0, :], rope[:, 1, :])):
                halves = [P, w, 2, HD // 2]

                def table(t):
                    return t.rearrange("p (a d) -> p a d", a=2).unsqueeze(1).to_broadcast(halves)
                src4 = src.rearrange("p (h a d) -> p h a d", a=2, d=HD // 2)
                dve.tensor_tensor(rc[:, o:o + w * HD].rearrange("p (h a d) -> p h a d", a=2, d=HD // 2),
                                  src4, table(cos), ALU.mult)
                last = dve.tensor_tensor(
                    rs[:, o:o + w * HD].rearrange("p (h a d) -> p h a d", a=2, d=HD // 2),
                    src4[:, :, ::-1, :], table(sin), ALU.mult)
                if o == GQ:
                    wait_from(dve, v_lo, n - 3)
                    dve.tensor_copy(v[:, g, :], ps_kv[:, HD:2 * HD]).then_inc(v_done, 1)
            last.then_inc(rope_mul, 1)

        def mask_scores(m):
            dve.wait_ge(scores_done, m + 1)
            wait_from(dve, exp_done, m)
            dve.tensor_tensor(masked[:, :, :], ps_s[:, :].rearrange("p (h k) -> p h k", h=REP),
                              mask[:, :].unsqueeze(1).to_broadcast([P, REP, S]), ALU.add).then_inc(mask_done, 1)

        def row_max(g, m):
            dve.wait_ge(mask_done, m + 1)
            dve.tensor_reduce(nmax[:, g % 2, :], masked[:, :, :], AX.X, ALU.max, negate=True).then_inc(max_done, 1)

        def recip(g, m):
            dve.wait_ge(exp_done, m + 1)
            dve.reciprocal(rinv[:, g % 2, :], rsum[:, g % 2, :]).then_inc(recip_done, 1)

        def probs_lo(m):
            dve.wait_ge(pt_hi, m + 1)
            wait_from(dve, pv_done, m)
            lo(pT_l[:, :], ps_pT[:, :], pT_h[:, :], pt_lo)

        def output_lo(m):
            dve.wait_ge(ot_hi, m + 1)
            lo(oT_l[:, :, :].rearrange("p h s -> p (h s)"), ps_oT[:, :],
               oT_h[:, :, :].rearrange("p h s -> p (h s)"), ot_lo)

        def add_y(b):
            dve.wait_ge(wo_done, KV * b + KV)
            tile = x[:, bass.ds(b, 1), :].rearrange("p a d -> p (a d)")
            dve.tensor_tensor(tile, tile, ps_y[:, 0:D], ALU.add).then_inc(y_added, 1)

        def sequence(b, head, tail):
            for g in range(KV):
                m = KV * b + g
                if g == 0 and not tail:
                    stats_x(b + 1)
                if g == KV - 2 and not tail:
                    x_lo(b + 1)
                mask_scores(m)
                row_max(g, m)
                if not (head and g == 0):
                    probs_lo(m - 1)
                if not (head and g < 2):
                    output_lo(m - 2)
                if g == 2 and not head:
                    add_y(b - 1)
                if g == 3 and not head:
                    core.tile_stats(dve, b - 1, y_added, b)
                if g == 0 and not tail:
                    dve.wait_ge(stat_done, 2 * b + 3)
                recip(g, m)
                if g == 0 and not tail:
                    aggregate_x()
                if g == 1 and not tail:
                    norm_x(b + 1)
                if head and g == 0:
                    split_in(3)
                if not (tail and g >= KV - 2):
                    take_projected((g + 2) % KV, m + 2)
                if g == 0 and not tail:
                    variance_x(b + 1)

        dve.wait_ge(x0_loaded, 16)
        stats_x(0)
        dve.wait_ge(stat_done, 1)
        aggregate_x()
        variance_x(0)
        norm_x(0)
        x_lo(0)
        split_in(0)
        split_in(1)
        dve.wait_ge(const_loaded, 48)
        take_projected(0, 0)
        split_in(2)
        take_projected(1, 1)
        dve.wait_ge(x_loaded, 16)
        sequence(0, True, False)
        with dve.Fori(1, B - 1) as b:
            sequence(b, False, False)
        sequence(B - 1, False, True)
        output_lo(KV * B - 2)
        probs_lo(KV * B - 1)
        output_lo(KV * B - 1)
        add_y(B - 1)
        core.tile_stats(dve, B - 1, y_added, B)

    return (attn0_sync, attn0_tensor, attn0_scalar, attn0_gpsimd, attn0_vector), (y_added, B)


def row_stats(core, ctx, tag):
    mv = core.sbuf(ctx, tag + "mv", [P, B, 2])
    vare, root, scratch, rstd = (core.sbuf(ctx, tag + n, [P, B]) for n in ("vare", "vroot", "vscratch", "rstd"))
    aggregated, var_done, root_done, rstd_done = core.layer_sems(
        tag[0] + "_", "aggregated var_done root_done rstd_done")

    core.phases_normed += 1
    stats_ready = B * core.phases_normed

    def vector(dve):
        dve.wait_ge(core.stats_done, stats_ready)
        for b in range(B):
            last = dve.bn_aggr(mv[:, b, :], core.stats[:, b, :])
        last.then_inc(aggregated, 1)
        dve.wait_ge(aggregated, 1)
        dve.tensor_scalar(vare[:, :], mv[:, :, 1], EPS, None, ALU.add).then_inc(var_done, 1)
        dve.wait_ge(root_done, 1)
        done = [1]

        def waits(ins):
            done[0] += 1
            ins.then_inc(aggregated, 1)
            dve.wait_ge(aggregated, done[0])

        inverse_root(dve, rstd[:, :], scratch[:, :], vare[:, :], root[:, :], waits).then_inc(rstd_done, 1)

    def scalar(act):
        act.wait_ge(var_done, 1)
        act.activation(root[:, :], vare[:, :], ACT.Sqrt).then_inc(root_done, 1)

    def normalise(dve, dst, b):
        return dve.tensor_scalar(dst, core.tile(b), mv[:, bass.ds(b, 1), 0], rstd[:, bass.ds(b, 1)],
                                 ALU.subtract, ALU.mult)

    return vector, scalar, normalise, rstd_done


CH, CW = 16, 8
HB = B // 2
FIRST = 4
UN = HB * CW * CW


def convolution(core, ctx, gate, tag, taps, context_pairs):
    dram, x, ident, ctxT = core.dram, core.x, core.ident, core.ctxT
    nT = core.sbuf(ctx, tag + "nT", [P, DC, B * S])
    oT = core.sbuf(ctx, tag + "oT", [P, DC, B * S])
    xn = core.sbuf(ctx, tag + "xn", [P, 2, D])
    hankel = core.sbuf(ctx, tag + "hankel", [P, CH, D])
    all_taps = core.sbuf(ctx, tag + "all_taps", [P, CH, D])
    t = core.sbuf(ctx, tag + "t", [P, 2, D])
    p = core.sbuf(ctx, tag + "p", [P, 2, DC, UN])
    z = core.sbuf(ctx, tag + "z", [P, DC, UN])
    ps_n = [core.psum(ctx, f"{tag}ps_n{k}", [P, 512]) for k in range(2)]
    ps_g = [core.psum(ctx, f"{tag}ps_g{k}", [P, 512]) for k in range(2)]
    ps_c = [[core.psum(ctx, f"{tag}ps_c{k}{c}", [P, 512]) for c in range(DC)] for k in range(2)]
    (taps_loaded, aux_loaded, rest_loaded, xn_done, nt_done, nT_done, w_done, g_done, skip_done, x_skipped, turned_taps,
     diagonal_made, diag_done, t_done, prod_done, conv_done, z_done, o_done, back_done, added) = core.layer_sems(
        "c_", "taps_loaded aux_loaded rest_loaded xn_done nt_done nT_done w_done g_done skip_done x_skipped turned_taps "
        "diagonal_made diag_done t_done prod_done conv_done z_done o_done back_done added")
    stats_vector, stats_scalar, normalise, rstd_done = row_stats(core, ctx, tag)
    if context_pairs:
        a_of, b_of, c_of = ctxT, ctxT, nT
        dcol = core.sbuf(ctx, tag + "dcol", [P, CH])
        diagonal = core.sbuf(ctx, tag + "diagonal", [P, CH, P])
    else:
        a_of, b_of, c_of = nT, ctxT, ctxT
        ctok = core.sbuf(ctx, tag + "ctok", [P, B, D])
        skip = core.sbuf(ctx, tag + "skip", [P, 1])
        ones = core.sbuf(ctx, tag + "ones", [P, P])
        w = core.sbuf(ctx, tag + "w", [P, 2, D])
        sk = core.sbuf(ctx, tag + "sk", [P, 2, D])


    def each_unit(eng, unit, between=None):
        for half in range(2):
            for h in range(2):
                unit(half, h, h)
            if half == 1 and between:
                between()
            with eng.Fori(2, CH - 1, 2) as h:
                for k in range(2):
                    unit(half, h + k, k)

    def channels(v, c, h, half, spread):
        v = v[:, c, :].rearrange("p (b h i) -> p b h i", h=CH, i=CW)[:, half * HB:(half + 1) * HB, bass.ds(h, 1), :]
        v = v.rearrange("p b a i -> p b (a i)")
        shape = [P, HB, CW, CW]
        return v.unsqueeze(3).to_broadcast(shape) if spread == "j" else v.unsqueeze(2).to_broadcast(shape)

    def cube(v):
        return v.rearrange("p (b i j) -> p b i j", i=CW, j=CW)

    def toeplitz(h):
        return all_taps[:, bass.ds(h, 1), :].rearrange("p a d -> p (a d)")

    def sync(sp):
        sp.wait_ge(*gate)
        rows = bass.AP(dram[taps].tensor, 0, [[1, P], [2 * D, CH], [1, D]])
        if context_pairs:
            d = dram["L1_xattn_D"]
            sp.dma_start(dcol[:, :], bass.AP(d.tensor, 0, [[0, P], [1, CH]])).then_inc(aux_loaded, 16)
        else:
            sp.dma_start(skip[:, :], dram["fside_S2_0"].rearrange("(s a) -> s a", a=1)).then_inc(aux_loaded, 16)
            sp.dma_start(ones[:, :], dram["same_head"]).then_inc(aux_loaded, 16)
            tokens = dram["ctx_2048"].rearrange("b s d -> s b d")
            sp.dma_start(ctok[:, 0:FIRST, :], tokens[:, 0:FIRST, :]).then_inc(aux_loaded, 16)
            sp.dma_start(ctok[:, FIRST:B, :], tokens[:, FIRST:B, :]).then_inc(rest_loaded, 16)
        sp.dma_start(hankel[:, :, :], rows).then_inc(taps_loaded, 16)

    def tensor(pe):
        pe.wait_ge(*gate)
        pe.wait_ge(core.const_loaded, 48)

        def turn(b, k):
            pe.wait_ge(xn_done, b + 1)
            wait_from(pe, nT_done, b - 1)
            for c in range(DC):
                last = pe.transpose(ps_n[k][:, c * P:(c + 1) * P], xn[:, k, c * P:(c + 1) * P], ident[:, :])
            last.then_inc(nt_done, 1)

        def sum_channels(b, k):
            pe.wait_ge(w_done, b + 1)
            wait_from(pe, skip_done, b - 1)
            pe.matmul(ps_g[k][:, 0:D], ones[:, :], w[:, k, :], start=True, stop=True).then_inc(g_done, 1)

        if context_pairs:
            pipeline(pe, ((1, turn),))
        else:
            pe.wait_ge(aux_loaded, 48)
            pipeline(pe, ((2, sum_channels), (1, turn)))

        def convolve(half, h, k):
            n = CH * half + h
            pe.wait_ge(t_done, n + 1)
            pe.wait_ge(prod_done, n + 1)
            wait_from(pe, z_done, 2 * (n - 1))
            near, far = t[:, k, 0:P], t[:, k, P:D]
            pe.matmul(ps_c[k][0][:, :], near, p[:, k, 0, :], start=True, stop=True)
            pe.matmul(ps_c[k][1][:, :], far, p[:, k, 0, :], start=True, stop=False)
            pe.matmul(ps_c[k][1][:, :], near, p[:, k, 1, :], start=False, stop=True).then_inc(conv_done, 1)

        def turn_back(half):
            pe.wait_ge(o_done, 2 * CH * (half + 1))
            for pair in range(HB // 2 * half, HB // 2 * (half + 1)):
                if pair >= 2:
                    pe.wait_ge(added, pair - 1)
                for j in range(2):
                    for c in range(DC):
                        at = (2 * pair + j) * S
                        last = pe.transpose(ps_n[pair % 2][:, j * D + c * P:j * D + (c + 1) * P],
                                            oT[:, c, at:at + S], ident[:, :])
                last.then_inc(back_done, 1)

        each_unit(pe, convolve, lambda: turn_back(0))
        turn_back(1)

    def scalar(act):
        act.wait_ge(*gate)
        stats_scalar(act)

        def turn_taps(heads):
            act.activation(all_taps[:, heads, :], hankel[:, heads, ::-1], ACT.Copy).then_inc(turned_taps, 1)

        def copy_turned(b, k):
            act.wait_ge(nt_done, b + 1)
            act.activation(nT[:, :, bass.ds(b * S, S)], ps_n[k][:, 0:D].rearrange("p (c s) -> p c s", c=DC),
                           ACT.Copy).then_inc(nT_done, 1)

        pipeline(act, ((1, copy_turned),))
        act.wait_ge(taps_loaded, 16)
        turn_taps(slice(0, 2))

        def place_taps(half, h, k):
            n = CH * half + h
            wait_from(act, conv_done, n - 1)
            act.activation(t[:, k, :], toeplitz(h), ACT.Copy).then_inc(t_done, 1)
            if isinstance(h, int) and n == 1:
                turn_taps(slice(2, CH))
                act.wait_ge(turned_taps, 2)
                if context_pairs:
                    act.wait_ge(diag_done, 2)

        act.wait_ge(turned_taps, 1)
        if context_pairs:
            act.wait_ge(diag_done, 1)
        each_unit(act, place_taps)

    def gpsimd(pool):
        pool.wait_ge(*gate)
        if context_pairs:
            core.clear(pool, "f_")
        if not context_pairs:
            def add_skip(b, k):
                pool.wait_ge(skip_done, b + 1)
                pool.tensor_tensor(core.tile(b), core.tile(b), sk[:, k, :], ALU.add).then_inc(x_skipped, 1)

            pipeline(pool, ((3, add_skip),))

        def product(half, h, k):
            n = CH * half + h
            wait_from(pool, conv_done, n - 1)
            for c in range(DC):
                last = pool.tensor_tensor(cube(p[:, k, c, :]), channels(a_of, c, h, half, "j"),
                                          channels(b_of, c, h, half, "i"), ALU.mult)
            last.then_inc(prod_done, 1)

        if not context_pairs:
            pool.wait_ge(nT_done, B)
        else:
            pool.wait_ge(aux_loaded, 16)
            pool.tensor_tensor(diagonal[:, :, :], ident[:, :].unsqueeze(1).to_broadcast([P, CH, P]),
                               dcol[:, :].unsqueeze(2).to_broadcast([P, CH, P]), ALU.mult).then_inc(diagonal_made, 1)
        pool.wait_ge(core.ctx_loaded, 16)
        each_unit(pool, product)

    def vector(dve):
        dve.wait_ge(*gate)
        stats_vector(dve)
        dve.wait_ge(rstd_done, 1)

        def norm_tile(b, k):
            wait_from(dve, nt_done, b - 1)
            normalise(dve, xn[:, k, :], b).then_inc(xn_done, 1)

        def context(b):
            return ctok[:, bass.ds(b, 1), :].rearrange("p a d -> p (a d)")

        def weigh_skip(b, k):
            if not isinstance(b, int) or b >= FIRST:
                dve.wait_ge(rest_loaded, 16)
            dve.wait_ge(xn_done, b + 1)
            wait_from(dve, g_done, b - 1)
            dve.scalar_tensor_tensor(out=w[:, k, :], in0=xn[:, k, :], scalar=skip[:, 0:1], in1=context(b),
                                     op0=ALU.mult, op1=ALU.mult).then_inc(w_done, 1)

        def skip_tile(b, k):
            dve.wait_ge(g_done, b + 1)
            wait_from(dve, x_skipped, b - 1)
            dve.tensor_tensor(sk[:, k, :], ps_g[k][:, 0:D], context(b), ALU.mult).then_inc(skip_done, 1)

        if context_pairs:
            pipeline(dve, ((0, norm_tile),))
            dve.wait_ge(diagonal_made, 1)
            for i, heads in enumerate((slice(0, 2), slice(2, CH))):
                dve.wait_ge(turned_taps, i + 1)
                near = all_taps[:, heads, 0:P]
                dve.tensor_tensor(near, near, diagonal[:, heads, :], ALU.add).then_inc(diag_done, 1)
            dve.wait_ge(nT_done, B)
        else:
            dve.wait_ge(aux_loaded, 48)
            pipeline(dve, ((1, weigh_skip), (3, skip_tile), (0, norm_tile)))

        def read_out(half, h, k):
            n = CH * half + h
            dve.wait_ge(conv_done, n + 1)
            for c in range(DC):
                wait_from(dve, o_done, 2 * n - 1 + c)
                dve.tensor_tensor(cube(z[:, c, :]), cube(ps_c[k][c][:, :]),
                                  channels(c_of, c, h, half, "j"), ALU.mult).then_inc(z_done, 1)
            for c in range(DC):
                dve.wait_ge(z_done, 2 * n + 1 + c)
                dst = oT[:, c, :].rearrange("p (b h j) -> p b h j", h=CH, j=CW)[:, half * HB:(half + 1) * HB, bass.ds(h, 1), :]
                dve.tensor_reduce(dst.rearrange("p b a j -> p b (a j)"), z[:, c, :].rearrange("p (b i j) -> p b j i", i=CW, j=CW),
                                  AX.X, ALU.add).then_inc(o_done, 1)

        def pair_stats(pair):
            for b in (2 * pair, 2 * pair + 1):
                core.tile_stats(dve, b, added, pair + 1)

        def add_half(half):
            if not context_pairs and half == 0:
                dve.wait_ge(x_skipped, B)
            for pair in range(HB // 2 * half, HB // 2 * (half + 1)):
                dve.wait_ge(back_done, pair + 1)
                two = x[:, 2 * pair:2 * pair + 2, :]
                dve.tensor_tensor(two, two, ps_n[pair % 2][:, :].rearrange("p (b d) -> p b d", b=2),
                                  ALU.add).then_inc(added, 1)
                if pair > 0:
                    pair_stats(pair - 1)

        each_unit(dve, read_out, lambda: add_half(0))
        add_half(1)
        pair_stats(B // 2 - 1)

    return (sync, tensor, scalar, gpsimd, vector), (added, B // 2)


def convolution0(core, ctx, gate):
    return convolution(core, ctx, gate, "c0_", "taps0", False)


def convolution1(core, ctx, gate):
    return convolution(core, ctx, gate, "c1_", "taps1", True)


H1, HF = 16, 16
RC = slice(2 * H1, 9 * H1)
IC = slice(9 * H1, 16 * H1)


def transforms():
    forward, inverse = np.zeros((2, D, D))
    n = np.arange(HF)
    rows = [(k, 0) for k in (0, 8, *range(1, 8))] + [(k, 1) for k in range(1, 8)]
    for r, (k, imaginary) in enumerate(rows):
        turn = 2 * np.pi * k * n / HF
        wave = -np.sin(turn) if imaginary else np.cos(turn)
        for h in range(H1):
            forward[h * HF + n, r * H1 + h] = wave * (1 if k in (0, 8) else np.sqrt(2))
            inverse[h * HF + n, r * H1 + h] = wave / HF
    return forward.astype(np.float32), inverse.astype(np.float32)


def attention1(core, ctx, gate):
    dram, ident = core.dram, core.ident
    tag = "a1_"
    raw = core.sbuf(ctx, tag + "raw", [P, 5, DC, D])
    w = core.sbuf(ctx, tag + "w", [P, DC, 3 * D])
    before = core.sbuf(ctx, tag + "before", [P, P])
    xn = core.sbuf(ctx, tag + "xn", [P, 2, D])
    xT = core.sbuf(ctx, tag + "xT", [P, 2, D])
    sq = core.sbuf(ctx, tag + "sq", [P, 2, 2 * D])
    norm2 = core.sbuf(ctx, tag + "norm2", [P, 2, 2 * H1])
    root = core.sbuf(ctx, tag + "root", [P, 2, 2 * H1])
    scratch = core.sbuf(ctx, tag + "scratch", [P, 2 * H1])
    rn = core.sbuf(ctx, tag + "rn", [P, 2, 2 * H1])
    qk = core.sbuf(ctx, tag + "qk", [P, 2, 2 * D])
    pp = core.sbuf(ctx, tag + "pp", [P, 2, D])
    ii = core.sbuf(ctx, tag + "ii", [P, 2, 7 * H1])
    ir = core.sbuf(ctx, tag + "ir", [P, 2, 7 * H1])
    pT = core.sbuf(ctx, tag + "pT", [P, 2, D])
    ps_n = core.psum(ctx, tag + "ps_n", [P, 512])
    ps_p = core.psum(ctx, tag + "ps_p", [P, 512])
    ps_qk = [core.psum(ctx, f"{tag}ps_qk{k}", [P, 512]) for k in range(2)]
    ps_c = [core.psum(ctx, f"{tag}ps_c{k}", [P, 512]) for k in range(2)]
    ps_o = [core.psum(ctx, f"{tag}ps_o{k}", [P, 512]) for k in range(2)]
    (raw_loaded, before_loaded, fold_done, folded, xn_done, xt_done, xT_done, qk_done, sq_done, norm2_done,
     newton, root_done, inverted, rn_done, scaled, sum_done, prod_done, pp_done, pt_done, pT_done, out_done, added) = core.sems(
        tag, "raw_loaded before_loaded fold_done folded xn_done xt_done xT_done qk_done sq_done norm2_done "
        "newton root_done inverted rn_done scaled sum_done prod_done pp_done pt_done pT_done out_done added")
    stats_vector, stats_scalar, normalise, rstd_done = row_stats(core, ctx, tag)
    folds = ((0, 2), (1, 2), (3, 4))

    def sync(sp):
        sp.wait_ge(*gate)
        for i, name in enumerate(("L1_attn_W_q", "L1_attn_W_kv", "forward", "inverse", "L1_WoT")):
            sp.dma_start(raw[:, i, :, :], dram[name].rearrange("(c p) n -> p c n", p=P)).then_inc(raw_loaded, 16)
        sp.dma_start(before[:, :], dram["before"]).then_inc(before_loaded, 16)

    def tensor(pe):
        pe.wait_ge(*gate)
        pe.wait_ge(raw_loaded, 80)
        for i, (left, right) in enumerate(folds):
            for m in range(DC):
                f = i * DC + m
                if f >= 2:
                    pe.wait_ge(folded, f - 1)
                for c in range(DC):
                    last = pe.matmul(ps_qk[f % 2][:, 0:D], raw[:, left, c, m * P:(m + 1) * P], raw[:, right, c, :],
                                     start=c == 0, stop=c == DC - 1)
                last.then_inc(fold_done, 1)
        pe.wait_ge(folded, 6)
        pe.wait_ge(before_loaded, 16)

        def turn(b, k):
            pe.wait_ge(xn_done, b + 1)
            wait_from(pe, xT_done, b)
            for c in range(DC):
                last = pe.transpose(ps_n[:, c * P:(c + 1) * P], xn[:, k, c * P:(c + 1) * P], ident[:, :])
            last.then_inc(xt_done, 1)

        def project(b, k):
            pe.wait_ge(xT_done, b + 1)
            wait_from(pe, scaled, b - 1)
            for c in range(DC):
                last = pe.matmul(ps_qk[k][:, :], xT[:, k, c * P:(c + 1) * P], w[:, c, 0:2 * D],
                                 start=c == 0, stop=c == DC - 1)
            last.then_inc(qk_done, 1)

        def running_sum(b, k):
            pe.wait_ge(scaled, b + 1)
            wait_from(pe, prod_done, b - 1)
            pe.matmul(ps_c[k][:, 0:D], before[:, :], qk[:, k, D:2 * D], start=True, stop=True).then_inc(sum_done, 1)

        def turn_products(b, k):
            pe.wait_ge(pp_done, b + 1)
            wait_from(pe, pT_done, b)
            for c in range(DC):
                last = pe.transpose(ps_p[:, c * P:(c + 1) * P], pp[:, k, c * P:(c + 1) * P], ident[:, :])
            last.then_inc(pt_done, 1)

        def output(b, k):
            pe.wait_ge(pT_done, b + 1)
            wait_from(pe, added, b - 1)
            for c in range(DC):
                last = pe.matmul(ps_o[k][:, 0:D], pT[:, k, c * P:(c + 1) * P], w[:, c, 2 * D:3 * D],
                                 start=c == 0, stop=c == DC - 1)
            last.then_inc(out_done, 1)

        pipeline(pe, ((6, turn_products), (7, output), (1, turn), (2, project), (4, running_sum)))

    def scalar(act):
        act.wait_ge(*gate)
        stats_scalar(act)
        for f in range(6):
            act.wait_ge(fold_done, f + 1)
            i, m = divmod(f, DC)
            act.activation(w[:, m, i * D:(i + 1) * D], ps_qk[f % 2][:, 0:D], ACT.Copy).then_inc(folded, 1)

        def copy_turned(b, k):
            act.wait_ge(xt_done, b + 1)
            wait_from(act, qk_done, b - 1)
            act.activation(xT[:, k, :], ps_n[:, 0:D], ACT.Copy).then_inc(xT_done, 1)

        def square(b, k):
            act.wait_ge(qk_done, b + 1)
            wait_from(act, norm2_done, b - 1)
            act.activation(sq[:, k, :], ps_qk[k][:, :], ACT.Square).then_inc(sq_done, 1)

        def copy_products(b, k):
            act.wait_ge(pt_done, b + 1)
            wait_from(act, out_done, b - 1)
            act.activation(pT[:, k, :], ps_p[:, 0:D], ACT.Copy).then_inc(pT_done, 1)

        def roots(b, k):
            act.wait_ge(norm2_done, b + 1)
            wait_from(act, inverted, b - 1)
            act.activation(root[:, k, :], norm2[:, k, :], ACT.Sqrt).then_inc(root_done, 1)

        pipeline(act, ((3, roots), (6, copy_products), (1, copy_turned), (2, square)))

    def gpsimd(pool):
        pool.wait_ge(*gate)
        core.clear(pool, "c_")

        def join_products(b, k):
            pool.wait_ge(prod_done, b + 1)
            pool.tensor_tensor(pp[:, k, RC], pp[:, k, RC], ii[:, k, :], ALU.subtract)
            pool.tensor_tensor(pp[:, k, IC], pp[:, k, IC], ir[:, k, :], ALU.add).then_inc(pp_done, 1)

        def refine(b, k):
            r, a = rn[:, k, :], norm2[:, k, :]
            pool.wait_ge(inverted, b + 1)
            pool.tensor_tensor(scratch[:, :], r, r, ALU.mult).then_inc(newton, 1)
            pool.wait_ge(newton, 4 * b + 1)
            pool.tensor_tensor(scratch[:, :], scratch[:, :], a, ALU.mult).then_inc(newton, 1)
            for i, (factor, op) in enumerate(((core.minus_half, ALU.mult), (core.three_halves, ALU.add))):
                pool.wait_ge(newton, 4 * b + 2 + i)
                pool.tensor_tensor(scratch[:, :], scratch[:, :], factor[:, :].to_broadcast([P, 2 * H1]),
                                   op).then_inc(newton, 1)
            pool.wait_ge(newton, 4 * b + 4)
            pool.tensor_tensor(r, r, scratch[:, :], ALU.mult).then_inc(rn_done, 1)

        pipeline(pool, ((3, refine), (5, join_products)))

    def vector(dve):
        dve.wait_ge(*gate)
        stats_vector(dve)
        dve.wait_ge(rstd_done, 1)

        def norm_tile(b, k):
            wait_from(dve, xt_done, b - 1)
            normalise(dve, xn[:, k, :], b).then_inc(xn_done, 1)

        def sum_squares(b, k):
            dve.wait_ge(sq_done, b + 1)
            wait_from(dve, rn_done, b - 1)
            dve.tensor_reduce(norm2[:, k, :].rearrange("p (a h) -> p a h", a=2),
                              sq[:, k, :].rearrange("p (a f h) -> p a h f", a=2, h=H1), AX.X,
                              ALU.add).then_inc(norm2_done, 1)

        def invert(b, k):
            dve.wait_ge(root_done, b + 1)
            dve.reciprocal(rn[:, k, :], root[:, k, :]).then_inc(inverted, 1)

        def scale_unit(b, k):
            dve.wait_ge(rn_done, b + 1)
            wait_from(dve, prod_done, b - 1)
            scale = rn[:, k, :].rearrange("p (a h) -> p a h", a=2).unsqueeze(2).to_broadcast([P, 2, HF, H1])
            dve.tensor_tensor(qk[:, k, :].rearrange("p (a f h) -> p a f h", a=2, h=H1),
                              ps_qk[k][:, :].rearrange("p (a f h) -> p a f h", a=2, h=H1), scale,
                              ALU.mult).then_inc(scaled, 1)

        def products(b, k):
            dve.wait_ge(sum_done, b + 1)
            wait_from(dve, pt_done, b - 1)
            c, q, both = ps_c[k], qk[:, k, :], slice(0, 9 * H1)
            dve.tensor_tensor(pp[:, k, both], q[:, both], c[:, both], ALU.mult)
            dve.tensor_tensor(ii[:, k, :], q[:, IC], c[:, IC], ALU.mult)
            dve.tensor_tensor(pp[:, k, IC], q[:, RC], c[:, IC], ALU.mult)
            dve.tensor_tensor(ir[:, k, :], q[:, IC], c[:, RC], ALU.mult).then_inc(prod_done, 1)

        def add_tile(b, k):
            dve.wait_ge(out_done, b + 1)
            dve.tensor_tensor(core.tile(b), core.tile(b), ps_o[k][:, 0:D], ALU.add).then_inc(added, 1)

        def stats_tile(b, k):
            core.tile_stats(dve, b, added, b + 1)

        pipeline(dve, ((4, scale_unit), (3, sum_squares), (3, invert), (5, products), (9, stats_tile), (8, add_tile),
                       (0, norm_tile)))

    return (sync, tensor, scalar, gpsimd, vector), (added, B)


GT = 512
NG = B * S // GT


class Layer0:
    tag, experts, top, slots, chunks, tail = "f0_", 16, 6, 13, (128, 128), (96,)
    width, shared, final = 176, 352, False
    biased, limit, cells = True, None, 2 * 16 + 1
    names = dict(router="L0_routerT", in_="L0_in", out="L0_out", pick="pick0")


class Layer1:
    tag, experts, top, slots, chunks, tail = "f1_", 8, 2, 8, (128, 128), None
    width, shared, final = 256, 0, True
    biased, limit, cells = False, 7.0, 2 * 8
    names = dict(router="L1_ffn_Wr", in_="L1_in", out="L1_out", pick="pick1")


def pick(cfg):
    hidden = sum(cfg.chunks)
    table = np.zeros((cfg.cells, cfg.slots, hidden), np.float32)
    for s in range(cfg.slots):
        for r in range(hidden):
            e = (s * hidden + r) // cfg.width
            if e < cfg.experts:
                table[e, s, r] = table[cfg.experts + e, s, r] = 1.0
            elif cfg.shared:
                table[2 * cfg.experts, s, r] = 1.0
    return table


def expert_layer(core, ctx, gate, cfg):
    dram, x, ident, tag = core.dram, core.x, core.ident, cfg.tag
    E, NS, NC, hidden, cells = cfg.experts, cfg.slots, len(cfg.chunks), sum(cfg.chunks), cfg.cells
    UNITS = NG * NC
    one_expert = cfg.width == hidden
    xT_h = core.sbuf(ctx, tag + "xT_h", [P, DC, B * S], F32R)
    xT_l = core.sbuf(ctx, tag + "xT_l", [P, DC, B * S], F32R)
    xn = core.sbuf(ctx, tag + "xn", [P, 2, D])
    in_raw = core.sbuf(ctx, tag + "in_raw", [P, DC, 2 * hidden])
    out_raw = core.sbuf(ctx, tag + "out_raw", [P, NC, D])
    pick_raw = core.sbuf(ctx, tag + "pick_raw", [cells, hidden])
    in_h = core.sbuf(ctx, tag + "in_h", [P, 2, DC, 2 * hidden], F32R)
    in_l = core.sbuf(ctx, tag + "in_l", [P, 2, DC, 2 * hidden], F32R)
    out_h = core.sbuf(ctx, tag + "out_h", [P, 2, NC, D], F32R)
    out_l = core.sbuf(ctx, tag + "out_l", [P, 2, NC, D], F32R)
    picked = core.sbuf(ctx, tag + "picked", [cells, 2, hidden], F32R)
    r_raw = core.sbuf(ctx, tag + "r_raw", [P, DC, E])
    r_both = core.sbuf(ctx, tag + "r_both", [P, DC, 2 * E], F32R)
    r_h, r_l = r_both[:, :, 0:E], r_both[:, :, E:2 * E]
    table = [P, B, E]
    logits, ex, prob, key, above, equal, run0, run1 = (core.sbuf(ctx, tag + n, table) for n in (
        "logits", "ex", "prob", "key", "above", "equal", "run0", "run1"))
    eight = core.sbuf(ctx, tag + "eight", [P, B, 8])
    row = core.sbuf(ctx, tag + "row", [P, B])
    row2 = core.sbuf(ctx, tag + "row2", [P, B])
    c_h = core.sbuf(ctx, tag + "c_h", table, F32R)
    cell = core.sbuf(ctx, tag + "cell", [P, B, cells])
    cellT = core.sbuf(ctx, tag + "cellT", [cells, B * S], F32R)
    s = core.sbuf(ctx, tag + "s", [P, 2, GT])
    m = core.sbuf(ctx, tag + "m", [P, 2, GT])
    h = core.sbuf(ctx, tag + "h", [P, 2, GT])
    h_h = core.sbuf(ctx, tag + "h_h", [P, 2, GT], F32R)
    h_l = core.sbuf(ctx, tag + "h_l", [P, 2, GT], F32R)
    if cfg.biased:
        bias_raw = core.sbuf(ctx, tag + "bias_raw", [P, 2, NC])
        bias = core.sbuf(ctx, tag + "bias", [P, 2, 2, NC])
        b2_raw = core.sbuf(ctx, tag + "b2_raw", [cells, D])
        b2_h = core.sbuf(ctx, tag + "b2_h", [cells, D], F32R)
        b2_l = core.sbuf(ctx, tag + "b2_l", [cells, D], F32R)
        router_b = core.sbuf(ctx, tag + "router_b", [P, E])
    ps_a, ps_u, ps_c, ps_y = ([core.psum(ctx, f"{tag}ps_{n}{k}", [P, 512]) for k in range(2)] for n in "aucy")
    (w0_loaded, w1_loaded, aux_loaded, router_hi, router_lo, b2_hi, b2_lo, xn_done, xt_done, xt_hi, xt_lo,
     logits_done, turned, exp_in, exp_done, step, cell_done, cellT_done, w_hi, w_lo, in_done, spread_done,
     silu_done, clipped, gated, h_done, h_hi, h_lo, out_done, added) = core.layer_sems(
        "f_", "w0_loaded w1_loaded aux_loaded router_hi router_lo b2_hi b2_lo xn_done xt_done xt_hi xt_lo "
        "logits_done turned exp_in exp_done step cell_done cellT_done w_hi w_lo in_done spread_done "
        "silu_done clipped gated h_done h_hi h_lo out_done added")
    w_loaded = (w0_loaded, w1_loaded)
    aux = 16 * (3 if cfg.biased else 1)
    slot_loads = 16 * (4 if cfg.biased else 3)
    stats_vector, stats_scalar, normalise, rstd_done = row_stats(core, ctx, tag)

    def each_slot(eng, slot):
        slot(0, 0, True)
        slot(1, 1, True)
        rest = NS - 3 if NS % 2 else NS - 2
        with eng.Fori(2, rest - 1, 2) as t:
            slot(t, 0, True)
            slot(t + 1, 1, True)
        for t in range(rest, NS):
            slot(t, t % 2, t < NS - 1)

    def chunks_of(t):
        return cfg.tail if cfg.tail and isinstance(t, int) and t == NS - 1 else cfg.chunks

    def units(t):
        rows = chunks_of(t)
        return [(g, c, R, c == len(rows) - 1, (g * len(rows) + c) % 2) for g in range(NG) for c, R in enumerate(rows)]

    def weight_bank(g, q):
        return g % 2 if one_expert else q

    def sync(sp):
        sp.wait_ge(*gate)
        sp.dma_start(r_raw[:, :, :], dram[cfg.names["router"]].rearrange("(c p) e -> p c e", p=P)).then_inc(aux_loaded, 16)
        if cfg.biased:
            gb = dram["L0_ffn_gate_b"]
            sp.dma_start(router_b[:, :], bass.AP(gb.tensor, 0, [[0, P], [1, E]])).then_inc(aux_loaded, 16)
            sp.dma_start(b2_raw[:, :], dram["L0_b2"]).then_inc(aux_loaded, 16)

        def slot(t, k, more):
            wait_from(sp, w_lo, t)
            one = bass.ds(t, 1)
            sp.dma_start(in_raw[:, :, :], dram[cfg.names["in_"]][one].rearrange("a p c n -> p (a c) n")).then_inc(w_loaded[k], 16)
            sp.dma_start(out_raw[:, :, :], dram[cfg.names["out"]][one].rearrange("a p c n -> p (a c) n")).then_inc(w_loaded[k], 16)
            sp.dma_start(pick_raw[:, :], dram[cfg.names["pick"]][:, one, :].rearrange("e a r -> e (a r)")).then_inc(w_loaded[k], 16)
            if cfg.biased:
                sp.dma_start(bias_raw[:, :, :], dram["L0_b13"][one].rearrange("a p w c -> p (a w) c")).then_inc(w_loaded[k], 16)

        each_slot(sp, slot)

    def tensor(pe):
        pe.wait_ge(*gate)

        def turn(b, k):
            pe.wait_ge(xn_done, b + 1)
            wait_from(pe, xt_lo, b - 1)
            for c in range(DC):
                last = pe.transpose(ps_a[k][:, c * P:(c + 1) * P], xn[:, k, c * P:(c + 1) * P], ident[:, :])
            last.then_inc(xt_done, 1)

        def route(b, k):
            pe.wait_ge(xt_hi, b + 1)
            pe.wait_ge(xt_lo, b + 1)
            for c in range(DC):
                tile = slice(b * S, (b + 1) * S)
                at = 2 * E * b
                pe.matmul(ps_y[0][:, at:at + 2 * E], xT_h[:, c, tile], r_both[:, c, :], start=c == 0, stop=False,
                          skip_group_check=True)
                last = pe.matmul(ps_y[0][:, at:at + E], xT_l[:, c, tile], r_h[:, c, :], start=False,
                                 stop=c == DC - 1, skip_group_check=True)
            last.then_inc(logits_done, 1)

        pe.wait_ge(router_hi, 1)
        pe.wait_ge(router_lo, 1)
        pipeline(pe, ((1, turn), (3, route)), looped=False)

        def hidden_sums(t, k, n, g, c, R, final, q):
            if (g, c) == (0, 0):
                pe.wait_ge(w_hi, t + 1)
                pe.wait_ge(w_lo, t + 1)
            wait_from(pe, silu_done, n - 1)
            wait_from(pe, gated, n - 1)
            cols = slice(g * GT, (g + 1) * GT)
            for dst, first in ((ps_a, 0), (ps_u, hidden)):
                rows = slice(first + c * P, first + c * P + R)
                for d in range(DC):
                    last = three_pass(pe, dst[q][0:R, :], (in_h[:, k, d, rows], in_l[:, k, d, rows]),
                                      (xT_h[:, d, cols], xT_l[:, d, cols]), d == 0, d == DC - 1)
            last.then_inc(in_done, 1)

        def unit_weights(k, n, g, c, R, final, q):
            if one_expert and c > 0:
                return
            if isinstance(n, int) and n < UNITS:
                pe.wait_ge(cellT_done, g + 1)
            wait_from(pe, h_done, n - 1)
            pe.matmul(ps_c[weight_bank(g, q)][0:R, :], picked[:, k, c * P:c * P + R], cellT[:, g * GT:(g + 1) * GT],
                      start=True, stop=True).then_inc(spread_done, 1)

        def output_sums(t, k, n, g, c, R, final, q):
            opening = c == 0
            if isinstance(n, int) and n == 0:
                pe.wait_ge(cellT_done, NG)
                if cfg.biased:
                    pe.wait_ge(b2_hi, 1)
                    pe.wait_ge(b2_lo, 1)
            pe.wait_ge(h_hi, n + 1)
            pe.wait_ge(h_lo, n + 1)
            if c == 0:
                wait_from(pe, added, NG * t + g)
            for b in range(4):
                s4, out = slice(b * S, (b + 1) * S), ps_y[b // 2][:, b % 2 * D:(b % 2 + 1) * D]
                begins = opening and b % 2 == 0
                if cfg.biased and opening and isinstance(t, int) and t == 0:
                    tokens = slice((4 * g + b) * S, (4 * g + b + 1) * S)
                    for w in (b2_h, b2_l):
                        pe.matmul(out, cellT[:, tokens], w[:, :], start=begins, stop=False, skip_group_check=True)
                        begins = False
                for i, (a, w) in enumerate(((h_h, out_h), (h_h, out_l), (h_l, out_h))):
                    last = pe.matmul(out, a[0:R, q, s4], w[0:R, k, c, :], start=begins and i == 0,
                                     stop=final and b % 2 == 1 and i == 2, skip_group_check=True)
            last.then_inc(out_done, 1)

        for n in range(2):
            hidden_sums(0, 0, n, *units(0)[n])
        pe.wait_ge(cell_done, 1)
        for g in range(NG):
            if g >= 2:
                pe.wait_ge(cellT_done, g - 1)
            for b in range(4):
                last = pe.transpose(ps_y[g % 2][0:cells, b * S:(b + 1) * S], cell[:, 4 * g + b, :], ident[:, :])
            last.then_inc(turned, 1)
            if g == 1:
                for n in range(2):
                    unit_weights(0, n, *units(0)[n])

        def slot(t, k, more):
            todo, following = units(t), units(t + 1)
            for i, unit in enumerate(todo):
                n, ahead = UNITS * t + i, i + 2
                if ahead < len(todo):
                    hidden_sums(t, k, n + 2, *todo[ahead])
                    unit_weights(k, n + 2, *todo[ahead])
                elif more:
                    hidden_sums(t + 1, 1 - k, n + 2, *following[ahead - len(todo)])
                    unit_weights(1 - k, n + 2, *following[ahead - len(todo)])
                output_sums(t, k, n, *unit)

        each_slot(pe, slot)

    def split_hi(act, t, k):
        act.wait_ge(w_loaded[k], slot_loads // 2 * (t - k) + slot_loads)
        wait_from(act, out_done, UNITS * (t - 1))
        copy_hi(act, in_h[:, k, :, :], in_raw[:, :, :])
        copy_hi(act, out_h[:, k, :, :], out_raw[:, :, :])
        if cfg.biased:
            act.activation(bias[:, k, :, :], bias_raw[:, :, :], ACT.Copy)
        copy_hi(act, picked[:, k, :], pick_raw[:, :]).then_inc(w_hi, 1)

    def scalar(act):
        act.wait_ge(*gate)
        act.wait_ge(aux_loaded, aux)
        copy_hi(act, r_h, r_raw[:, :, :]).then_inc(router_hi, 1)
        if cfg.biased:
            copy_hi(act, b2_h[:, :], b2_raw[:, :]).then_inc(b2_hi, 1)
        stats_scalar(act)
        split_hi(act, 0, 0)

        def turn(b, k):
            act.wait_ge(xt_done, b + 1)
            copy_hi(act, xT_h[:, :, bass.ds(b * S, S)], ps_a[k][:, 0:D].rearrange("p (c s) -> p c s", c=DC)).then_inc(xt_hi, 1)

        pipeline(act, ((1, turn),))
        act.wait_ge(exp_in, 1)
        act.activation(ex[:, :, :], ex[:, :, :], ACT.Exp).then_inc(exp_done, 1)

        def silu(k, n, g, c, R, final, q):
            act.wait_ge(in_done, n + 1)
            wait_from(act, gated, n - 1)
            offset = dict(bias=bias[0:R, k, 0, c:c + 1]) if cfg.biased else {}
            act.activation(s[0:R, q, :], ps_a[q][0:R, :], ACT.Silu, **offset).then_inc(silu_done, 1)

        silu(0, 0, *units(0)[0])
        for g in range(NG):
            act.wait_ge(turned, g + 1)
            copy_hi(act, cellT[:, g * GT:(g + 1) * GT], ps_y[g % 2][0:cells, :]).then_inc(cellT_done, 1)

        def slot(t, k, more):
            todo = units(t)
            for i, (g, c, R, final, q) in enumerate(todo):
                n = UNITS * t + i
                if i + 1 < len(todo):
                    silu(k, n + 1, *todo[i + 1])
                elif more:
                    silu(1 - k, n + 1, *units(t + 1)[0])
                act.wait_ge(h_done, n + 1)
                wait_from(act, out_done, n - 1)
                copy_hi(act, h_h[0:R, q, :], h[0:R, q, :]).then_inc(h_hi, 1)
                if i == 2 and more:
                    split_hi(act, t + 1, 1 - k)

        each_slot(act, slot)

    def gpsimd(pool):
        pool.wait_ge(*gate)
        pool.wait_ge(router_hi, 1)
        sub_lo(pool, r_l, r_raw[:, :, :], r_h).then_inc(router_lo, 1)
        if cfg.biased:
            pool.wait_ge(b2_hi, 1)
            sub_lo(pool, b2_l[:, :], b2_raw[:, :], b2_h[:, :]).then_inc(b2_lo, 1)

        def split_lo(t, k):
            pool.wait_ge(w_hi, t + 1)
            sub_lo(pool, in_l[:, k, :, :], in_raw[:, :, :], in_h[:, k, :, :])
            sub_lo(pool, out_l[:, k, :, :], out_raw[:, :, :], out_h[:, k, :, :]).then_inc(w_lo, 1)

        split_lo(0, 0)

        def slot(t, k, more):
            for i, (g, c, R, final, q) in enumerate(units(t)):
                n = UNITS * t + i
                pool.wait_ge(h_hi, n + 1)
                wait_from(pool, out_done, n - 1)
                sub_lo(pool, h_l[0:R, q, :], h[0:R, q, :], h_h[0:R, q, :]).then_inc(h_lo, 1)
                if i == 2 and more:
                    split_lo(t + 1, 1 - k)

        each_slot(pool, slot)

    def vector(dve):
        dve.wait_ge(*gate)
        stats_vector(dve)
        dve.wait_ge(rstd_done, 1)

        def norm_tile(b, k):
            wait_from(dve, xt_done, b - 1)
            normalise(dve, xn[:, k, :], b).then_inc(xn_done, 1)

        def split_tile(b, k):
            dve.wait_ge(xt_hi, b + 1)
            to = xT_l[:, :, bass.ds(b * S, S)]
            sub_lo(dve, to, ps_a[k][:, 0:D].rearrange("p (c s) -> p c s", c=DC), xT_h[:, :, bass.ds(b * S, S)]).then_inc(xt_lo, 1)

        pipeline(dve, ((0, norm_tile), (2, split_tile)))

        done = [0]

        def chain(ins):
            done[0] += 1
            ins.then_inc(step, 1)
            dve.wait_ge(step, done[0])

        def wide(v, n=E):
            return v.unsqueeze(2).to_broadcast([P, B, n])

        def choose(values):
            for b in range(B):
                last = dve.max(eight[:, b, :], values[:, b, :])
            chain(last)
            least = wide(eight[:, :, cfg.top - 1])
            dve.tensor_tensor(equal[:, :, :], values[:, :, :], least, ALU.is_equal)
            chain(dve.tensor_tensor(above[:, :, :], values[:, :, :], least, ALU.is_gt))
            chain(dve.tensor_reduce(row[:, :], above[:, :, :], AX.X, ALU.add))
            chain(dve.tensor_scalar(row[:, :], row[:, :], -1.0, float(cfg.top), ALU.mult, ALU.add))
            src, shift, spare = equal, 1, [run0, run1]
            while shift < E:
                dst = spare[0]
                dve.tensor_copy(dst[:, :, 0:shift], src[:, :, 0:shift])
                chain(dve.tensor_tensor(dst[:, :, shift:E], src[:, :, shift:E], src[:, :, 0:E - shift], ALU.add))
                src, spare, shift = dst, spare[::-1], 2 * shift
            dst = spare[0]
            chain(dve.tensor_tensor(dst[:, :, :], src[:, :, :], wide(row[:, :]), ALU.is_le))
            chain(dve.tensor_tensor(dst[:, :, :], dst[:, :, :], equal[:, :, :], ALU.mult))
            chain(dve.tensor_tensor(above[:, :, :], above[:, :, :], dst[:, :, :], ALU.add))

        dve.wait_ge(logits_done, B)
        both = ps_y[0][:, 0:2 * B * E].rearrange("p (b a e) -> p b a e", a=2, e=E)
        chain(dve.tensor_copy(logits[:, :, :], both[:, :, 0, :]))
        chain(dve.tensor_tensor(logits[:, :, :], logits[:, :, :], both[:, :, 1, :], ALU.add))
        chain(dve.tensor_reduce(row2[:, :], logits[:, :, :], AX.X, ALU.max))
        dve.tensor_tensor(ex[:, :, :], logits[:, :, :], wide(row2[:, :]), ALU.subtract).then_inc(exp_in, 1)
        if not cfg.biased:
            choose(logits)
        dve.wait_ge(exp_done, 1)
        if not cfg.biased:
            chain(dve.tensor_tensor(ex[:, :, :], ex[:, :, :], above[:, :, :], ALU.mult))
        chain(dve.tensor_reduce(row2[:, :], ex[:, :, :], AX.X, ALU.add))
        chain(dve.reciprocal(row2[:, :], row2[:, :]))
        chain(dve.tensor_tensor(prob[:, :, :], ex[:, :, :], wide(row2[:, :]), ALU.mult))
        if cfg.biased:
            dve.wait_ge(aux_loaded, aux)
            chain(dve.tensor_tensor(key[:, :, :], prob[:, :, :], router_b[:, :].unsqueeze(1).to_broadcast(table), ALU.add))
            choose(key)
            chain(dve.tensor_tensor(prob[:, :, :], prob[:, :, :], above[:, :, :], ALU.mult))
        chain(dve.tensor_copy(c_h[:, :, :], prob[:, :, :]))
        dve.tensor_copy(cell[:, :, 0:E], c_h[:, :, :].bitcast(F32))
        if cfg.biased:
            dve.memset(cell[:, :, 2 * E:cells], 1.0)
        dve.tensor_tensor(cell[:, :, E:2 * E], prob[:, :, :], c_h[:, :, :].bitcast(F32), ALU.subtract).then_inc(cell_done, 1)
        def gate_unit(t, k, n, g, c, R, final, q):
            dve.wait_ge(silu_done, n + 1)
            if cfg.limit is not None:
                dve.tensor_scalar(s[0:R, q, :], s[0:R, q, :], -cfg.limit, cfg.limit, ALU.max, ALU.min).then_inc(clipped, 1)
                dve.wait_ge(clipped, n + 1)
                dve.tensor_tensor(m[0:R, q, :], ps_u[q][0:R, :], s[0:R, q, :], ALU.mult).then_inc(gated, 1)
            else:
                dve.scalar_tensor_tensor(out=m[0:R, q, :], in0=ps_u[q][0:R, :], scalar=bias[0:R, k, 1, c:c + 1],
                                         in1=s[0:R, q, :], op0=ALU.add, op1=ALU.mult).then_inc(gated, 1)
            dve.wait_ge(gated, n + 1)
            dve.wait_ge(spread_done, NG * t + g + 1 if one_expert else n + 1)
            wait_from(dve, h_lo, n - 1)
            dve.tensor_tensor(h[0:R, q, :], m[0:R, q, :], ps_c[weight_bank(g, q)][0:R, :],
                              ALU.mult).then_inc(h_done, 1)

        def group_stats(g):
            if not cfg.final:
                for b in range(4 * g, 4 * g + 4):
                    core.tile_stats(dve, b, added, NG * (NS - 1) + g + 1)

        def add_group(t, g):
            dve.wait_ge(out_done, UNITS * t + len(chunks_of(t)) * (g + 1))
            for j in range(2):
                two = x[:, 4 * g + 2 * j:4 * g + 2 * j + 2, :]
                last = dve.tensor_tensor(two, two, ps_y[j][:, :].rearrange("p (b d) -> p b d", b=2), ALU.add)
            last.then_inc(added, 1)
            if isinstance(t, int) and t == NS - 1 and g > 0:
                group_stats(g - 1)

        def slot(t, k, more):
            for i, unit in enumerate(units(t)):
                gate_unit(t, k, UNITS * t + i, *unit)
                g, c = unit[0:2]
                if c == 0:
                    if g > 0:
                        add_group(t, g - 1)
                    elif not (isinstance(t, int) and t == 0):
                        add_group(t - 1, NG - 1)

        each_slot(dve, slot)
        add_group(NS - 1, NG - 1)
        group_stats(NG - 1)

    return (sync, tensor, scalar, gpsimd, vector), (added, NG * NS)


def experts0(core, ctx, gate):
    return expert_layer(core, ctx, gate, Layer0)


def experts1(core, ctx, gate):
    return expert_layer(core, ctx, gate, Layer1)


PHASES = (attention0, convolution0, experts0, attention1, convolution1, experts1,)


def build(nc, dram, out):
    with ExitStack() as stack:
        core = Core(nc, stack, dram)
        programs, gate = [], None
        for phase in PHASES:
            with ExitStack() as ctx:
                engines, done = phase(core, ctx) if gate is None else phase(core, ctx, gate)
            programs.append(engines)
            gate = done

        with nc.Block() as block:
            @block.sync
            def _(sp):
                for sync, _, _, _, _ in programs:
                    sync(sp)
                added, all_added = gate
                for g in range(NG):
                    sp.wait_ge(added, all_added - NG + g + 1)
                    of_group = slice(g * B // NG, (g + 1) * B // NG)
                    sp.dma_start(out[of_group].rearrange("b s d -> s b d"), core.x[:, of_group, :]).then_inc(core.stored, 16)
                sp.wait_ge(core.stored, 16 * NG)

            @block.tensor
            def _(pe):
                for _, tensor, _, _, _ in programs:
                    tensor(pe)

            @block.scalar
            def _(act):
                for _, _, scalar, _, _ in programs:
                    scalar(act)

            @block.gpsimd
            def _(pool):
                for _, _, _, gpsimd, _ in programs:
                    gpsimd(pool)

            @block.vector
            def _(dve):
                for _, _, _, _, vector in programs:
                    vector(dve)


def lay_out(inputs):
    a = {k: np.asarray(v) for k, v in inputs.items()}
    out = {k: a[k] for k in ("x", "ctx_2048", "fside_S2_0", "L0_attn_Wq", "L0_attn_Wk", "L0_attn_Wv", "L0_attn_Wo",
                             "L1_xattn_D", "L1_attn_W_q", "L1_attn_W_kv", "L0_ffn_gate_b", "L1_ffn_Wr")}
    out["ctxT"] = a["ctx_2048"].reshape(B * S, D).T
    out["L1_WoT"] = a["L1_attn_W_o"].T
    for name, taps in (("taps0", a["L0_xattn_k"]), ("taps1", a["L1_xattn_ssm_kernel"])):
        padded = np.zeros((CH, 2 * D), np.float32)
        padded[:, D:] = taps
        out[name] = padded[:, ::-1]

    def by_slot(v, cfg):
        n = sum(cfg.chunks)
        full = np.zeros((cfg.slots * n,) + v.shape[1:], np.float32)
        full[:len(v)] = v
        return full.reshape((cfg.slots, n) + v.shape[1:])

    def hidden_first(w, cfg):
        return by_slot(w, cfg).reshape(cfg.slots, -1, DC, P).transpose(0, 3, 2, 1)

    def by_chunk(v, cfg):
        full = by_slot(v, cfg).reshape((cfg.slots, len(cfg.chunks), P) + v.shape[1:])
        return np.moveaxis(full, 2, 1)

    w1, w3 = (np.concatenate([a["L0_ffn_" + n].reshape(-1, D), a["L0_ffn_ws" + n[1]]]) for n in ("w1", "w3"))
    w2 = np.concatenate([a["L0_ffn_w2"].transpose(0, 2, 1).reshape(-1, D), a["L0_ffn_ws2"].T])
    out["L0_in"] = np.concatenate([hidden_first(w1, Layer0), hidden_first(w3, Layer0)], -1)
    out["L0_out"] = by_chunk(w2, Layer0)
    out["L0_b13"] = np.stack([by_chunk(np.concatenate([a["L0_ffn_b" + n].reshape(-1), a["L0_ffn_bs" + n]]), Layer0)
                              for n in "13"], 2)
    out["L0_b2"] = np.concatenate([a["L0_ffn_b2"], a["L0_ffn_b2"], a["L0_ffn_bs2"][None]])
    out["L0_routerT"] = a["L0_ffn_gate_w"].T
    inputs1 = [a["L1_ffn_" + n].reshape(Layer1.slots, DC, P, -1).transpose(0, 2, 1, 3) for n in ("Wg", "Wu")]
    out["L1_in"] = np.concatenate(inputs1, -1)
    out["L1_out"] = by_chunk(a["L1_ffn_Wd"].reshape(-1, D), Layer1)
    return out


def kernel(**inputs):
    import concourse.bacc as bacc
    from concourse.bass_utils import run_bass_kernel_spmd

    nc = bacc.Bacc("TRN2", target_bir_lowering=False, num_devices=1)
    arrays, dram = {}, {}
    for name, a in {**lay_out(inputs), **constants()}.items():
        a = np.ascontiguousarray(a)
        arrays["in_" + name] = a
        dram[name] = nc.dram_tensor("in_" + name, a.shape, mybir.dt.from_np(a.dtype), kind="ExternalInput").ap()
    out = nc.dram_tensor("out_x", (B, S, D), F32, kind="ExternalOutput").ap()
    build(nc, dram, out)
    r = run_bass_kernel_spmd(nc, [arrays], core_ids=[0])
    return r.results[0]["out_x"]
```
